# Optimizing a Trainium2 kernel written in Bass

```python
import numpy as np
import jax
import jax.numpy as jnp

def _softmax(x, axis=-1):
    return jax.nn.softmax(x, axis=axis)

def _gelu(x):
    return jax.nn.gelu(x, approximate=True)

def _silu(x):
    return jax.nn.silu(x)

def _sigmoid(x):
    return jax.nn.sigmoid(x)

def _layernorm(x, axis=-1, eps=1e-05):
    m = jnp.mean(x, axis=axis, keepdims=True)
    v = jnp.var(x, axis=axis, keepdims=True)
    return (x - m) / jnp.sqrt(v + eps)

def _scatter_add(tgt, idx, src, axis=0):
    return tgt.at[idx].add(src)

def _segment_sum(src, seg, n):
    return jax.ops.segment_sum(src, seg, n)
kernel_name = 'mk_audio_tower_d2_tok_aud1d768_r4_7265b9'

def setup_inputs(seed: int=0):
    np.random.seed(seed)
    _w = jnp.asarray

    def _rec_inputs():
        import jax
        import jax.numpy as jnp
        _rk = jax.random.key(seed)
        x = -6.41493e-05 + 1.00002 * jax.random.normal(jax.random.fold_in(_rk, 1), (64, 4000), jnp.float32)
        return x
    x = _rec_inputs()

    def _L0_tok_setup():
        import jax, jax.numpy as jnp
        import numpy as np
        import math
        SR = 4000
        FRAME_LEN = 100
        FRAME_STEP = 160
        N_FILTERS = 40
        N_MFCC = 13
        EMBED = 192
        BATCH = 64
        AUDIO_LEN = 40000
        N_FFT_BINS = FRAME_LEN // 2 + 1

        def _mel_filterbank():
            low_mel = 2595.0 * math.log10(1.0 + 0.0 / 700.0)
            high_mel = 2595.0 * math.log10(1.0 + SR // 2 / 700.0)
            mel_points = np.linspace(low_mel, high_mel, N_FILTERS + 2)
            hz_points = 700.0 * (10.0 ** (mel_points / 2595.0) - 1.0)
            bin_points = np.floor((FRAME_LEN + 1) * hz_points / SR)
            filt = np.zeros((N_FILTERS, N_FFT_BINS), dtype=np.float32)
            for i in range(1, N_FILTERS + 1):
                l, c, r = (bin_points[i - 1], bin_points[i], bin_points[i + 1])
                for j in range(int(l), int(c)):
                    filt[i - 1, j] = (j - l) / (c - l)
                for j in range(int(c), int(r)):
                    filt[i - 1, j] = (r - j) / (r - c)
            return jnp.asarray(filt)

        def _dct_matrix():
            k = np.arange(N_MFCC)[:, None]
            j = np.arange(N_FILTERS)[None, :]
            m = np.cos(np.pi * k * (2 * j + 1) / (2 * N_FILTERS)) * math.sqrt(2.0 / N_FILTERS)
            return jnp.asarray(m.astype(np.float32))
        key = jax.random.key(seed)
        kx, kw = jax.random.split(key)
        x = jax.random.normal(kx, (BATCH, AUDIO_LEN), dtype=jnp.float32)
        bound = 1.0 / math.sqrt(N_MFCC)
        w_proj = jax.random.uniform(kw, (N_MFCC, EMBED), minval=-bound, maxval=bound, dtype=jnp.float32)
        b_proj = jnp.zeros((EMBED,), dtype=jnp.float32)
        return {'x': x, 'mel_filters': _mel_filterbank(), 'dct': _dct_matrix(), 'w_proj': w_proj, 'b_proj': b_proj}
    _L0_tok_all = _L0_tok_setup()
    _L0_tok_in = {k: v for k, v in _L0_tok_all.items() if k in ('mel_filters', 'dct', 'w_proj', 'b_proj')}
    del _L0_tok_all

    def _L0_attn_setup():
        import jax, jax.numpy as jnp
        import numpy as np
        EPS = 1e-05

        def _ste(y, x):
            return x + jax.lax.stop_gradient(y - x)

        def _absmean_quant(x):
            s = jnp.mean(jnp.abs(x)) + EPS
            u = x / s
            q = _ste(jnp.round(jnp.clip(u, -1.0, 1.0)), u)
            return (q, s)

        def _ternary_weight(w):
            s = jnp.mean(jnp.abs(w)) + EPS
            u = w / s
            return _ste(jnp.round(jnp.clip(u, -1.0, 1.0)), u) * s

        def _l1norm(x):
            return x / (jnp.sum(jnp.abs(x), axis=-1, keepdims=True) + EPS)
        key = jax.random.key(seed)
        k1, k2 = jax.random.split(key)
        B, N, C = (16, 1025, 192)
        x = jax.random.normal(k1, (B, N, C), dtype=jnp.float32)
        w_qkv = jax.random.normal(k2, (3 * C, C), dtype=jnp.float32) * 0.02
        return {'x': x, 'w_qkv': w_qkv}
    _L0_attn_all = _L0_attn_setup()
    _L0_attn_in = {k: v for k, v in _L0_attn_all.items() if k in ('w_qkv',)}
    del _L0_attn_all

    def _L0_ffn_setup():
        import jax, jax.numpy as jnp
        import numpy as np
        EPS_NORM = 1e-06
        EPS_Q = 1e-05

        def rmsnorm(x, g):
            return x * jax.lax.rsqrt(jnp.mean(x * x, axis=-1, keepdims=True) + EPS_NORM) * g

        def activation_quant(x):
            scale = 127.0 / jnp.maximum(jnp.max(jnp.abs(x), axis=-1, keepdims=True), EPS_Q)
            return jnp.clip(jnp.round(x * scale), -128, 127) / scale

        def weight_quant(w):
            scale = 1.0 / jnp.maximum(jnp.mean(jnp.abs(w)), EPS_Q)
            return jnp.clip(jnp.round(w * scale), -1, 1) / scale

        def bitlinear(x, w, g):
            x_norm = rmsnorm(x, g)
            x_q = x_norm + jax.lax.stop_gradient(activation_quant(x_norm) - x_norm)
            w_q = w + jax.lax.stop_gradient(weight_quant(w) - w)
            return jnp.einsum('bsd,od->bso', x_q, w_q)
        key = jax.random.key(seed)
        k1, k2, k3 = jax.random.split(key, 3)
        B, S, D, H = (8, 1024, 192, 512)
        x = jax.random.normal(k1, (B, S, D), dtype=jnp.float32)
        w_in = jax.random.normal(k2, (2 * H, D), dtype=jnp.float32) * 0.002
        w_out = jax.random.normal(k3, (D, H), dtype=jnp.float32) * 0.002
        g_in = jnp.ones((D,), dtype=jnp.float32)
        g_out = jnp.ones((H,), dtype=jnp.float32)
        return {'x': x, 'w_in': w_in, 'g_in': g_in, 'w_out': w_out, 'g_out': g_out}
    _L0_ffn_all = _L0_ffn_setup()
    _L0_ffn_in = {k: v for k, v in _L0_ffn_all.items() if k in ('w_in', 'g_in', 'w_out', 'g_out')}
    del _L0_ffn_all

    def _L1_attn_setup():
        import jax, jax.numpy as jnp
        import numpy as np
        NUM_HEADS = 12
        DIM_HEAD = 64
        SCALE = DIM_HEAD ** (-0.5)
        LOG2PI = float(np.log(2.0 * np.pi))
        key = jax.random.key(seed)
        k1, k2, k3, k4 = jax.random.split(key, 4)
        b, n, e = (2, 512, 192)
        inner = NUM_HEADS * DIM_HEAD
        return {'x': jax.random.normal(k1, (b, n, e), dtype=jnp.float32), 'w_qkv': jax.random.normal(k2, (e, 3 * inner), dtype=jnp.float32) * e ** (-0.5), 'w_out': jax.random.normal(k3, (inner, e), dtype=jnp.float32) * inner ** (-0.5), 'b_out': jax.random.normal(k4, (e,), dtype=jnp.float32) * 0.02}
    _L1_attn_all = _L1_attn_setup()
    _L1_attn_in = {k: v for k, v in _L1_attn_all.items() if k in ('w_qkv', 'w_out', 'b_out')}
    del _L1_attn_all

    def _L1_ffn_setup():
        import jax, jax.numpy as jnp
        import numpy as np
        B, S, D, F, E = (8, 512, 192, 768, 16)
        CAP = 64
        EPS = 1e-06

        def _switch_moe_block(x, ln_w, w_router, wi, wo):
            var = jnp.mean(jnp.square(x.astype(jnp.float32)), axis=-1, keepdims=True)
            normed = (x * jax.lax.rsqrt(var + EPS)).astype(x.dtype) * ln_w
            logits = jnp.einsum('bsd,de->bse', normed.astype(jnp.float32), w_router.astype(jnp.float32))
            probs = jax.nn.softmax(logits, axis=-1)
            expert_idx = jnp.argmax(probs, axis=-1)
            onehot = jax.nn.one_hot(expert_idx, E, dtype=jnp.float32)
            priority = jnp.cumsum(onehot, axis=1)
            keep = onehot * (priority <= CAP)
            pos = (priority - 1.0).astype(jnp.int32)
            dispatch = keep[..., None] * jax.nn.one_hot(pos, CAP, dtype=jnp.float32)
            expert_in = jnp.einsum('bsec,bsd->becd', dispatch, normed)
            h = jax.nn.relu(jnp.einsum('becd,edf->becf', expert_in, wi))
            expert_out = jnp.einsum('becf,efd->becd', h, wo)
            combined = jnp.einsum('bsec,becd->bsd', dispatch, expert_out)
            routed = jnp.sum(dispatch, axis=(2, 3)) > 0
            next_states = jnp.where(routed[..., None], combined.astype(x.dtype), normed)
            router_prob = jnp.max(probs, axis=-1, keepdims=True).astype(x.dtype)
            return x + router_prob * next_states
        key = jax.random.key(seed)
        k_x, k_r, k_wi, k_wo = jax.random.split(key, 4)
        x = jax.random.normal(k_x, (B, S, D), dtype=jnp.float32)
        ln_w = jnp.ones((D,), dtype=jnp.float32)
        w_router = jax.random.normal(k_r, (D, E), dtype=jnp.float32) * 0.02
        wi = jax.random.normal(k_wi, (E, D, F), dtype=jnp.float32) * D ** (-0.5)
        wo = jax.random.normal(k_wo, (E, F, D), dtype=jnp.float32) * F ** (-0.5)
        return {'x': x, 'ln_w': ln_w, 'w_router': w_router, 'wi': wi, 'wo': wo}
    _L1_ffn_all = _L1_ffn_setup()
    _L1_ffn_in = {k: v for k, v in _L1_ffn_all.items() if k in ('ln_w', 'w_router', 'wi', 'wo')}
    del _L1_ffn_all
    return {'x': x, 'L0_tok_mel_filters': _L0_tok_in['mel_filters'], 'L0_tok_dct': _L0_tok_in['dct'], 'L0_tok_w_proj': _L0_tok_in['w_proj'], 'L0_tok_b_proj': _L0_tok_in['b_proj'], 'L0_attn_w_qkv': _L0_attn_in['w_qkv'], 'L0_ffn_w_in': _L0_ffn_in['w_in'], 'L0_ffn_g_in': _L0_ffn_in['g_in'], 'L0_ffn_w_out': _L0_ffn_in['w_out'], 'L0_ffn_g_out': _L0_ffn_in['g_out'], 'L1_attn_w_qkv': _L1_attn_in['w_qkv'], 'L1_attn_w_out': _L1_attn_in['w_out'], 'L1_attn_b_out': _L1_attn_in['b_out'], 'L1_ffn_ln_w': _L1_ffn_in['ln_w'], 'L1_ffn_w_router': _L1_ffn_in['w_router'], 'L1_ffn_wi': _L1_ffn_in['wi'], 'L1_ffn_wo': _L1_ffn_in['wo']}

def reference(x, L0_tok_mel_filters, L0_tok_dct, L0_tok_w_proj, L0_tok_b_proj, L0_attn_w_qkv, L0_ffn_w_in, L0_ffn_g_in, L0_ffn_w_out, L0_ffn_g_out, L1_attn_w_qkv, L1_attn_w_out, L1_attn_b_out, L1_ffn_ln_w, L1_ffn_w_router, L1_ffn_wi, L1_ffn_wo):
    import jax
    import jax.numpy as jnp

    def _L0_tok_ref(x, mel_filters, dct, w_proj, b_proj):
        import jax, jax.numpy as jnp
        import numpy as np
        import math
        SR = 4000
        FRAME_LEN = 100
        FRAME_STEP = 160
        N_FILTERS = 40
        N_MFCC = 13
        EMBED = 192
        BATCH = 64
        AUDIO_LEN = 40000
        N_FFT_BINS = FRAME_LEN // 2 + 1

        def _mel_filterbank():
            low_mel = 2595.0 * math.log10(1.0 + 0.0 / 700.0)
            high_mel = 2595.0 * math.log10(1.0 + SR // 2 / 700.0)
            mel_points = np.linspace(low_mel, high_mel, N_FILTERS + 2)
            hz_points = 700.0 * (10.0 ** (mel_points / 2595.0) - 1.0)
            bin_points = np.floor((FRAME_LEN + 1) * hz_points / SR)
            filt = np.zeros((N_FILTERS, N_FFT_BINS), dtype=np.float32)
            for i in range(1, N_FILTERS + 1):
                l, c, r = (bin_points[i - 1], bin_points[i], bin_points[i + 1])
                for j in range(int(l), int(c)):
                    filt[i - 1, j] = (j - l) / (c - l)
                for j in range(int(c), int(r)):
                    filt[i - 1, j] = (r - j) / (r - c)
            return jnp.asarray(filt)

        def _dct_matrix():
            k = np.arange(N_MFCC)[:, None]
            j = np.arange(N_FILTERS)[None, :]
            m = np.cos(np.pi * k * (2 * j + 1) / (2 * N_FILTERS)) * math.sqrt(2.0 / N_FILTERS)
            return jnp.asarray(m.astype(np.float32))
        B, T = x.shape
        n_frames = 1 + (T - FRAME_LEN) // FRAME_STEP
        idx = jnp.arange(n_frames)[:, None] * FRAME_STEP + jnp.arange(FRAME_LEN)[None, :]
        frames = x[:, idx]
        window = 0.54 - 0.46 * jnp.cos(2.0 * jnp.pi * jnp.arange(FRAME_LEN, dtype=jnp.float32) / (FRAME_LEN - 1))
        windowed = frames * window
        fft = jnp.fft.rfft(windowed, axis=-1)
        power = fft.real ** 2 + fft.imag ** 2
        mel_energies = jnp.einsum('bnf,mf->bnm', power, mel_filters)
        log_energies = jnp.log(mel_energies + 1e-06)
        mfcc = jnp.einsum('bnm,km->bnk', log_energies, dct)
        out = mfcc @ w_proj + b_proj
        return out

    def _L0_attn_ref(x, w_qkv):
        import jax, jax.numpy as jnp
        import numpy as np
        EPS = 1e-05

        def _ste(y, x):
            return x + jax.lax.stop_gradient(y - x)

        def _absmean_quant(x):
            s = jnp.mean(jnp.abs(x)) + EPS
            u = x / s
            q = _ste(jnp.round(jnp.clip(u, -1.0, 1.0)), u)
            return (q, s)

        def _ternary_weight(w):
            s = jnp.mean(jnp.abs(w)) + EPS
            u = w / s
            return _ste(jnp.round(jnp.clip(u, -1.0, 1.0)), u) * s

        def _l1norm(x):
            return x / (jnp.sum(jnp.abs(x), axis=-1, keepdims=True) + EPS)
        B, N, C = x.shape
        H = 12
        D = C // H
        scale = D ** (-0.5)
        wq = _ternary_weight(w_qkv)
        qkv = jnp.einsum('bnc,oc->bno', x, wq)
        qkv = qkv.reshape(B, N, 3, H, D).transpose(2, 0, 3, 1, 4)
        q, k, v = (qkv[0], qkv[1], qkv[2])
        q_q, q_s = _absmean_quant(_l1norm(q))
        k_q, k_s = _absmean_quant(_l1norm(k))
        v_q, v_s = _absmean_quant(_l1norm(v))
        attn = jnp.einsum('bhnd,bhmd->bhnm', q_q, k_q) * scale
        attn = attn * q_s * k_s
        attn_q, qk_s = _absmean_quant(attn)
        out = jnp.einsum('bhnm,bhmd->bhnd', attn_q, v_q)
        out = out.transpose(0, 2, 1, 3).reshape(B, N, C)
        return out * qk_s * v_s

    def _L0_ffn_ref(x, w_in, g_in, w_out, g_out):
        import jax, jax.numpy as jnp
        import numpy as np
        EPS_NORM = 1e-06
        EPS_Q = 1e-05

        def rmsnorm(x, g):
            return x * jax.lax.rsqrt(jnp.mean(x * x, axis=-1, keepdims=True) + EPS_NORM) * g

        def activation_quant(x):
            scale = 127.0 / jnp.maximum(jnp.max(jnp.abs(x), axis=-1, keepdims=True), EPS_Q)
            return jnp.clip(jnp.round(x * scale), -128, 127) / scale

        def weight_quant(w):
            scale = 1.0 / jnp.maximum(jnp.mean(jnp.abs(w)), EPS_Q)
            return jnp.clip(jnp.round(w * scale), -1, 1) / scale

        def bitlinear(x, w, g):
            x_norm = rmsnorm(x, g)
            x_q = x_norm + jax.lax.stop_gradient(activation_quant(x_norm) - x_norm)
            w_q = w + jax.lax.stop_gradient(weight_quant(w) - w)
            return jnp.einsum('bsd,od->bso', x_q, w_q)
        h = bitlinear(x, w_in, g_in)
        up, gate = jnp.split(h, 2, axis=-1)
        y = jax.nn.silu(gate) * up
        return bitlinear(y, w_out, g_out)

    def _L1_attn_ref(x, w_qkv, w_out, b_out):
        import jax, jax.numpy as jnp
        import numpy as np
        NUM_HEADS = 12
        DIM_HEAD = 64
        SCALE = DIM_HEAD ** (-0.5)
        LOG2PI = float(np.log(2.0 * np.pi))
        b, n, _ = x.shape
        h, d = (NUM_HEADS, DIM_HEAD)
        qkv = x @ w_qkv
        q, k, v = jnp.split(qkv, 3, axis=-1)
        to_heads = lambda t: t.reshape(b, n, h, d).transpose(0, 2, 1, 3)
        q, k, v = (to_heads(q), to_heads(k), to_heads(v))
        dots = jnp.einsum('bhid,bhjd->bhij', q, k) * SCALE
        attn = jax.nn.softmax(dots, axis=-1)
        product = jnp.einsum('bhij,bhjd->bhid', attn, v)
        mean = jnp.mean(product, axis=1, keepdims=True)
        variance = jnp.var(product, axis=1, ddof=1, keepdims=True)
        log_probs = -0.5 * (LOG2PI + jnp.log(variance) - 0.5 * (product - mean) ** 2 / variance)
        log_probs = jnp.sum(log_probs, axis=-1) - jnp.sum(jnp.log(jnp.sqrt(variance)), axis=-1)
        out = jnp.einsum('bhij,bhjd->bhid', log_probs[..., None] * attn, v)
        out = out.transpose(0, 2, 1, 3).reshape(b, n, h * d)
        return out @ w_out + b_out

    def _L1_ffn_ref(x, ln_w, w_router, wi, wo):
        import jax, jax.numpy as jnp
        import numpy as np
        B, S, D, F, E = (8, 512, 192, 768, 16)
        CAP = 64
        EPS = 1e-06

        def _switch_moe_block(x, ln_w, w_router, wi, wo):
            var = jnp.mean(jnp.square(x.astype(jnp.float32)), axis=-1, keepdims=True)
            normed = (x * jax.lax.rsqrt(var + EPS)).astype(x.dtype) * ln_w
            logits = jnp.einsum('bsd,de->bse', normed.astype(jnp.float32), w_router.astype(jnp.float32))
            probs = jax.nn.softmax(logits, axis=-1)
            expert_idx = jnp.argmax(probs, axis=-1)
            onehot = jax.nn.one_hot(expert_idx, E, dtype=jnp.float32)
            priority = jnp.cumsum(onehot, axis=1)
            keep = onehot * (priority <= CAP)
            pos = (priority - 1.0).astype(jnp.int32)
            dispatch = keep[..., None] * jax.nn.one_hot(pos, CAP, dtype=jnp.float32)
            expert_in = jnp.einsum('bsec,bsd->becd', dispatch, normed)
            h = jax.nn.relu(jnp.einsum('becd,edf->becf', expert_in, wi))
            expert_out = jnp.einsum('becf,efd->becd', h, wo)
            combined = jnp.einsum('bsec,becd->bsd', dispatch, expert_out)
            routed = jnp.sum(dispatch, axis=(2, 3)) > 0
            next_states = jnp.where(routed[..., None], combined.astype(x.dtype), normed)
            router_prob = jnp.max(probs, axis=-1, keepdims=True).astype(x.dtype)
            return x + router_prob * next_states
        return _switch_moe_block(x, ln_w, w_router, wi, wo)
    h = _L0_tok_ref(x, L0_tok_mel_filters, L0_tok_dct, L0_tok_w_proj, L0_tok_b_proj)
    h = h + _L0_attn_ref(_layernorm(h, axis=-1), L0_attn_w_qkv)
    h = h + _L0_ffn_ref(_layernorm(h, axis=-1), L0_ffn_w_in, L0_ffn_g_in, L0_ffn_w_out, L0_ffn_g_out)
    h = h + _L1_attn_ref(_layernorm(h, axis=-1), L1_attn_w_qkv, L1_attn_w_out, L1_attn_b_out)
    h = h + _L1_ffn_ref(_layernorm(h, axis=-1), L1_ffn_ln_w, L1_ffn_w_router, L1_ffn_wi, L1_ffn_wo)
    return h

_drawn_inputs = setup_inputs


def setup_inputs(seed=0):
    import zlib

    import numpy as np

    out = dict(_drawn_inputs(seed))
    spreads = {'L0_tok_b_proj': (0.0, 0.321),
     'L0_ffn_g_in': (1.0, 0.6),
     'L0_ffn_g_out': (1.0, 0.6),
     'L1_ffn_ln_w': (1.0, 0.6)}
    factors = {'L0_attn_w_qkv': 64.0,
     'L0_ffn_w_in': 8.0,
     'L0_ffn_w_out': 8.0,
     'L1_attn_b_out': 64.0,
     'L1_ffn_w_router': 8.0,
     'L1_ffn_wi': 8.0,
     'L1_ffn_wo': 8.0}
    for name, (base, spread) in spreads.items():
        noise = np.random.default_rng([zlib.crc32(name.encode()), seed]).standard_normal(out[name].shape)
        drawn = base * np.exp(spread * noise) if base else spread * noise
        out[name] = jnp.asarray(drawn.astype(out[name].dtype))
    for name, factor in factors.items():
        out[name] = (out[name] * factor).astype(out[name].dtype)
    return out
```

```python
import concourse.bass as bass
from concourse import mybir
from contextlib import ExitStack

F32, BF16, I32 = mybir.dt.float32, mybir.dt.bfloat16, mybir.dt.int32
U32 = mybir.dt.uint32
ALU = mybir.AluOpType
ACT = mybir.ActivationFunctionType
AX = mybir.AxisListType

CLIPS, SAMPLES, FRAME, HOP = 64, 4000, 100, 160
SEQ, DIM = 25, 192
TOKENS = CLIPS * SEQ
ROWS = 5 * SEQ
NT = -(-TOKENS // ROWS)
LAST = TOKENS - (NT - 1) * ROWS
BINS, MELS, MFCC = FRAME // 2 + 1, 40, 13
KC = DIM // 2
HEADS = 12
D0 = DIM // HEADS
D1 = 64
INNER = HEADS * D1
HID0 = 512
FF, EXPERTS, SLOTS = 768, 16, 128
NS = (TOKENS - EXPERTS) // SLOTS + EXPERTS
RK = NT - 1
ROWLEN = 450
RES, GATE = 256, 448
BLOCK = FF + 6 * DIM
PAIR = 2 * BLOCK + FF
PITCH16 = ROWS + 1
WIDE = HEADS * ROWS
ORDER1 = (0, 2, 4, 6, 1, 3, 5, 7, 8, 10, 9, 11)
ROUND = 12582912.0
LOG2PI = 1.8378770664093453
NEG = -1.0e30

CONST = {}
_at = 0
for _name, _n in (("ident", 128), ("tri", 128), ("ones", 128), ("same", ROWS), ("other", ROWS),
                  ("rev", EXPERTS), ("count", NT), ("below", EXPERTS * EXPERTS), ("slot", NS),
                  ("token", NT), ("lane", 128), ("side", 1), ("eps6", 1), ("minus_half", 2), ("dft", 2 * BINS)):
    CONST[_name] = (_at, _at + _n)
    _at += _n
CONSTS = _at


def constants():
    import numpy as np
    c = np.zeros((128, CONSTS), np.float64)

    def put(name, value, rows=128):
        a, b = CONST[name]
        c[:rows, a:b] = value

    p = np.arange(128)[:, None]
    j = np.arange(128)[None, :]
    put("ident", p == j)
    put("tri", p < j)
    put("ones", 1.0)
    q = np.arange(ROWS)[None, :]
    put("same", (p // SEQ) == (q // SEQ))
    put("other", np.where((p // SEQ) == (q // SEQ), 0.0, NEG))
    put("rev", EXPERTS - np.arange(EXPERTS)[None, :])
    put("count", SLOTS * np.arange(NT)[None, :])
    e = np.arange(EXPERTS)
    put("below", (e[None, :] < e[:, None]).reshape(1, -1))
    put("slot", np.arange(NS)[None, :])
    put("token", p + ROWS * np.arange(NT)[None, :] + 1)
    put("lane", j)
    put("side", p >= 64)
    put("eps6", 1e-6)
    put("minus_half", -0.5)
    n = np.arange(FRAME)[:, None]
    k = np.arange(BINS)[None, :]
    window = 0.54 - 0.46 * np.cos(2 * np.pi * n / (FRAME - 1))
    put("dft", np.concatenate([window * np.cos(2 * np.pi * n * k / FRAME),
                               -window * np.sin(2 * np.pi * n * k / FRAME)], 1), FRAME)
    return c.astype(np.float32)


def at_least(eng, sem, n):
    if not (isinstance(n, int) and n <= 0):
        eng.wait_ge(sem, n)


def capped(n, top=NT):
    return min(n, top) if isinstance(n, int) else n


def pipeline(eng, stages, tiles):
    top = max(lag for _, lag in stages)

    def step(s):
        for stage, lag in stages:
            if not isinstance(s, int) or 0 <= s - lag < tiles:
                stage(s - lag)

    for s in range(top + 1):
        step(s)
    with eng.Fori(top + 1, tiles) as s:
        step(s)
    for s in range(tiles, tiles + top):
        step(s)


def tile_of(t3, t):
    if isinstance(t, int):
        return t3[:, t, :]
    return t3[:, bass.ds(t, 1), :].rearrange("p a n -> p (a n)")


def build(nc, x, consts, melT, dct, w_proj, b_proj, w_qkv0, w_in, g_in, w_out0, g_out,
          w_qkv1, w_out1, b_out, ln_w, w_router, experts, out, rows_dram):
    ctx = ExitStack()
    with ctx:
        def sb(name, shape, dt=F32):
            return ctx.enter_context(nc.sbuf_tensor(name, shape, dt))

        sems = {}

        def sem(name):
            if name not in sems:
                sems[name] = ctx.enter_context(nc.semaphore(name))
            return sems[name]

        bank = [ctx.enter_context(nc.psum_tensor(f"bank{i}", [128, 512], F32)) for i in range(8)]
        bank16 = [b[:, :].bitcast(BF16) for b in bank]

        cst = sb("cst", [128, CONSTS])

        def C(name, rows=128):
            a, b = CONST[name]
            return cst[0:rows, a:b]

        h = sb("h", [ROWS, NT, DIM])
        ident16 = sb("ident16", [128, 128], BF16)
        tri16 = sb("tri16", [128, 128], BF16)
        ones16 = sb("ones16", [128, 128], BF16)
        same16 = sb("same16", [ROWS, ROWS], BF16)
        bprojb = sb("bprojb", [ROWS, DIM])
        ginb = sb("ginb", [ROWS, DIM])
        goutb = sb("goutb", [ROWS, HID0])
        boutb = sb("boutb", [ROWS, DIM])
        lnwb = sb("lnwb", [ROWS, DIM])
        router = sb("router", [KC, 2, EXPERTS])
        win16 = sb("win16", [KC, 2, 2 * HID0], BF16)
        wout16 = sb("wout16", [128, 4, DIM], BF16)
        w1_mem = sb("w1_mem", [128, 2 * 3 * INNER])
        w1 = w1_mem[0:KC, :].rearrange("p (c n) -> p c n", c=2)
        wo1 = sb("wo1", [128, 6, DIM])
        scal = sb("scal", [128, 32])
        small = sb("small", [128, 64])
        logits = sb("logits", [ROWS, NT, EXPERTS])
        big = sb("big", [128, 8 * PAIR])

        def carve(start):
            at = [start]

            def take(n, dt=F32, rows=128):
                words = n if dt is not BF16 else -(-n // 2)
                a = big[0:rows, at[0]:at[0] + words]
                at[0] += words
                assert at[0] <= 8 * PAIR
                return a if dt is F32 else a.bitcast(dt)[:, 0:n]
            return take, at

        EARLY = 6 * PAIR
        take, early_end = carve(0)
        qkv = take(NT * 3 * DIM, rows=ROWS).rearrange("p (t n) -> p t n", t=NT)
        scores0 = take(NT * WIDE, BF16, ROWS).rearrange("p (t n) -> p t n", t=NT)
        v16 = take(NT * DIM, BF16, ROWS).rearrange("p (t n) -> p t n", t=NT)
        nv16 = take(NT * DIM, BF16, ROWS).rearrange("p (t n) -> p t n", t=NT)
        above_below = take(2 * WIDE, BF16, ROWS)
        melT_sb = take(MELS, rows=2 * BINS)
        dct_sb = take(MELS, rows=MFCC)
        wproj_sb = take(DIM, rows=MFCC)
        w_emb = take(DIM, rows=MELS)
        wq0 = take(2 * 3 * DIM, rows=KC).rearrange("p (c n) -> p c n", c=2)
        frame = take(FRAME, rows=ROWS)
        frameT = take(ROWS, rows=FRAME)
        power = take(ROWS, rows=2 * BINS)
        logmel = take(ROWS, rows=MELS)
        hn = take(DIM, rows=ROWS)
        hnT = take(2 * ROWS, rows=KC).rearrange("p (c n) -> p c n", c=2)
        assert early_end[0] <= EARLY, early_end[0]
        take, _ = carve(EARLY)
        win_raw = take(2 * 2 * HID0, rows=KC).rearrange("p (c n) -> p c n", c=2)
        wout_raw = take(4 * DIM).rearrange("p (c n) -> p c n", c=4)
        l1sum = take(NT * 3 * HEADS, rows=ROWS).rearrange("p (t n) -> p t n", t=NT)
        l1inv = take(NT * 3 * HEADS, rows=ROWS)
        l1ratio = take(NT * 3 * HEADS, rows=ROWS)
        l1unit = take(NT * 3 * HEADS, rows=ROWS)
        unit = take(3 * DIM, rows=ROWS)
        whole = take(3 * DIM, rows=ROWS)
        qk_pad = take(2 * HEADS * 32, BF16, ROWS)
        qkT0 = take(6 * ROWS, BF16)
        raw16 = take(WIDE, BF16, ROWS)
        junk16 = take(WIDE, BF16, ROWS)
        abs0 = take(NT, rows=ROWS)

        take, _ = carve(EARLY)
        xq = take(DIM, BF16, ROWS)
        xz = take(DIM, rows=ROWS)
        xqT = take(2 * ROWS, BF16, KC)
        egate = take(HID0, rows=ROWS)
        ug = take(HID0, rows=ROWS)
        yz = take(HID0, rows=ROWS)
        yq = take(HID0, BF16, ROWS)
        yqT = take(4 * ROWS, BF16)
        x2 = xz
        x2T = take(2 * ROWS, rows=KC).rearrange("p (c n) -> p c n", c=2)
        qkT1 = take(12 * ROWS)
        vx = take(HEADS * (D1 + 1), rows=ROWS).rearrange("p (h d) -> p h d", h=HEADS)
        probs = take(WIDE, rows=ROWS)
        probsT = take(WIDE, rows=ROWS)
        outT = take(6 * ROWS)
        nT = take(2 * ROWS, rows=KC)
        row = sb("row", [ROWS, ROWLEN])
        h3 = row[:, RES:RES + DIM]
        heads_mem = sb("heads_mem", [128, NT * 128])
        prod = heads_mem[0:ROWS, 0:INNER]
        dev = heads_mem[0:ROWS, INNER:2 * INNER]
        mean64 = sb("mean64", [ROWS, D1])
        var64 = sb("var64", [ROWS, D1])
        ivar64 = sb("ivar64", [ROWS, D1])
        logv = sb("logv", [ROWS, D1])
        stats6 = sb("stats6", [ROWS, 6])
        rowmax, nmax, rsum, factor = (sb(n, [ROWS, HEADS]) for n in ("rowmax", "nmax", "rsum", "factor"))

        spot = [0]

        def reuse(n, dt=F32, rows=128):
            words = n if dt is not BF16 else -(-n // 2)
            a = w1_mem[0:rows, spot[0]:spot[0] + words]
            spot[0] += words
            assert spot[0] <= 6 * INNER
            return a if dt is F32 else a.bitcast(dt)[:, 0:n]

        slot_rows = [reuse(ROWLEN) for _ in range(2)]
        rowsT = reuse(2 * SLOTS)
        hid = reuse(FF)
        hidT = reuse(FF)
        y_out = [reuse(DIM) for _ in range(2)]
        onehot16 = reuse(NT * EXPERTS, BF16, ROWS)
        hot = reuse(NT * EXPERTS, rows=ROWS).rearrange("p (t e) -> p t e", t=NT)
        where = reuse(NT * EXPERTS, rows=ROWS).rearrange("p (t e) -> p t e", t=NT)
        cmp13 = reuse(EXPERTS * NT).rearrange("p (e k) -> p e k", e=EXPERTS)
        cmp16 = reuse(EXPERTS * EXPERTS).rearrange("p (a b) -> p a b", a=EXPERTS)
        token_at = reuse(NT * NS, rows=ROWS).rearrange("p (t s) -> p t s", t=NT)
        lane_hot = heads_mem[0:ROWS, :].rearrange("p (t l) -> p t l", t=NT)
        cmp28 = sb("cmp28", [128, NS, EXPERTS])[:, :, :]
        best, pos, lane_f, tile_f = (sb(n, [ROWS, NT])[:, :] for n in ("best", "pos", "lane_f", "tile_f"))
        pos_i, lane_i, tile_i = (sb(n, [ROWS, NT], I32)[:, :] for n in ("pos_i", "lane_i", "tile_i"))
        cnt, ntile, base, base128, ends = (sb(n, [128, EXPERTS])[:, :]
                                           for n in ("cnt", "ntile", "base", "base128", "ends"))
        expert, odd, pair2, own_f, both_f = (
            sb(n, [128, NS])[:, :] for n in ("expert", "odd", "pair2", "own_f", "both_f"))
        mine = sb("mine", [128, NS + 1])
        expert_i, odd_i = (sb(n, [128, NS], I32)[:, :] for n in ("expert_i", "odd_i"))
        slot_f, empty = expert, pair2
        slot_i = sb("slot_i", [128, NS], I32)[:, :]
        picks = sb("picks", [128, 2 * NS + 2], I32)[:, :]
        out_rows = out.rearrange("b n c -> (b n) c")

        def slot_pipeline(eng, stages):
            def step(s, odd_step):
                for stage, lag in stages:
                    if not isinstance(s, int) or 0 <= s - lag < NS:
                        stage(s - lag, (odd_step + lag) % 2)

            step(0, 0)
            step(1, 1)
            with eng.Fori(2, NS, 2) as s:
                step(s, 0)
                step(s + 1, 1)
            step(NS, 0)

        block = ctx.enter_context(nc.Block())

        chains = []

        def chain(eng, name, t=0, steps=0):
            n = [0]
            chains.append((name, n, steps))

            def link(ins):
                n[0] += 1
                ins.then_inc(sem(name), 1)
                eng.wait_ge(sem(name), t * steps + n[0] if steps else n[0])
            return link

        def hold(eng):
            eng.sem_inc(sem("held"), 1)

        S_W, S_IN, S_OUT = (scal[:, i:i + 1] for i in (0, 1, 2))
        COLSUM = scal[:, 3:6]
        S_QKV, R_QKV = scal[:, 6:9], scal[:, 9:12]
        PART1, PART2 = scal[:, 12:15], scal[:, 15:18]
        GAIN, INT_SUM, S_A, T_HI, T_LO, FAC0 = (scal[:, i:i + 1] for i in range(18, 24))
        R_W = scal[:, 24:27]
        IGAIN = scal[:, 27:28]

        @block.sync
        def _(sp):
            sp.dma_start(cst[:, :], consts).then_inc(sem("in_const"), 16)
            sp.dma_start(melT_sb, melT).then_inc(sem("in_tok"), 16)
            sp.dma_start(dct_sb, dct).then_inc(sem("in_tok"), 16)
            sp.dma_start(wproj_sb, w_proj).then_inc(sem("in_tok"), 16)
            sp.dma_start(wq0, w_qkv0).then_inc(sem("in_wq0"), 16)
            frames = x.rearrange("b (n s) -> (b n) s", s=HOP)

            def load_frames(t):
                at_least(sp, sem("frame_turned"), t)
                if isinstance(t, int) and t == NT - 1:
                    sp.dma_start(frame[0:LAST, :], frames[t * ROWS:TOKENS, 0:FRAME])\
                        .then_inc(sem("frame_in"), 16)
                else:
                    sp.dma_start(frame, frames[bass.ds(t * ROWS, ROWS), 0:FRAME])\
                        .then_inc(sem("frame_in"), 16)

            load_frames(0)
            for dst, src in ((bprojb, b_proj), (ginb, g_in), (goutb, g_out), (boutb, b_out),
                             (lnwb, ln_w)):
                sp.dma_start(dst[:, :], src.partition_broadcast(ROWS)).then_inc(sem("in_vec"), 16)
            sp.dma_start(win_raw, w_in).then_inc(sem("in_ffn"), 16)
            sp.dma_start(wout_raw, w_out0).then_inc(sem("in_ffn"), 16)
            with sp.Fori(1, NT - 1) as t:
                load_frames(t)
            load_frames(NT - 1)
            sp.dma_start(w1, w_qkv1).then_inc(sem("in_attn1"), 16)
            sp.dma_start(wo1[:, :, :], w_out1).then_inc(sem("in_attn1"), 16)
            sp.dma_start(router[:, :, :], w_router).then_inc(sem("in_attn1"), 16)
            sp.wait_ge(sem("pv0_mm"), NT)
            for pair in range(6):
                sp.dma_start(big[:, pair * PAIR:(pair + 1) * PAIR], experts[pair, :, :])\
                    .then_inc(sem("in_experts"), 16)

            def store_row(t):
                sp.wait_ge(sem("row_ready"), t + 1)
                sp.dma_start(rows_dram[bass.ds(t * ROWS, ROWS), :], row[:, :])\
                    .then_inc(sem("row_stored"), 16)

            pipeline(sp, [(store_row, 0)], NT)
            sp.wait_ge(sem("row_ready"), NT)
            for pair in range(6, 8):
                sp.dma_start(big[:, pair * PAIR:(pair + 1) * PAIR], experts[pair, :, :])\
                    .then_inc(sem("in_experts"), 16)

        @block.tensor
        def _(pe):
            ident = C("ident")

            pe.wait_ge(sem("in_const"), 16)
            pe.wait_ge(sem("in_tok"), 48)
            pe.matmul(bank[7][0:MELS, 0:DIM], dct_sb, wproj_sb, start=True, stop=True)\
                .then_inc(sem("emb_mm"), 1)
            pe.wait_ge(sem("colsum"), 1)
            pe.matmul(bank[6][:, 0:1], C("ones", KC), COLSUM[0:KC, 0:1], start=True, stop=True)\
                .then_inc(sem("wsum_mm"), 1)

            def frame_turn(t):
                pe.wait_ge(sem("frame_in"), 16 * (t + 1))
                at_least(pe, sem("frameT"), t)
                pe.transpose(bank[0][0:FRAME, 0:ROWS], frame, ident[0:ROWS, 0:ROWS])\
                    .then_inc(sem("frame_turned"), 1)

            def spectrum(t):
                pe.wait_ge(sem("frameT"), t + 1)
                at_least(pe, sem("power"), t)
                pe.matmul(bank[1][0:2 * BINS, 0:ROWS], C("dft", FRAME), frameT,
                          start=True, stop=True).then_inc(sem("spectrum_mm"), 1)

            def mel(t):
                pe.wait_ge(sem("power"), t + 1)
                at_least(pe, sem("logmel"), t)
                pe.matmul(bank[2][0:MELS, 0:ROWS], melT_sb, power, start=True, stop=True)\
                    .then_inc(sem("mel_mm"), 1)

            def embed(t):
                if isinstance(t, int) and t == 0:
                    pe.wait_ge(sem("w_emb"), 1)
                pe.wait_ge(sem("logmel"), t + 1)
                at_least(pe, sem("h0"), t)
                pe.matmul(bank[3][0:ROWS, 0:DIM], logmel, w_emb, start=True, stop=True)\
                    .then_inc(sem("embed_mm"), 1)

            def hn_turn(t):
                pe.wait_ge(sem("hn"), t + 1)
                at_least(pe, sem("hnT"), t)
                for c in range(2):
                    mm = pe.transpose(bank[4][0:KC, c * ROWS:(c + 1) * ROWS],
                                      hn[:, c * KC:(c + 1) * KC], ident[0:ROWS, 0:ROWS])
                mm.then_inc(sem("hn_turned"), 1)

            def project0(t):
                if isinstance(t, int) and t == 0:
                    pe.wait_ge(sem("wq0_ternary"), 1)
                pe.wait_ge(sem("hnT"), t + 1)
                at_least(pe, sem("qkv"), 2 * t)
                for half in range(2):
                    for c in range(2):
                        mm = pe.matmul(bank[5 + half][0:ROWS, 0:288], hnT[:, c, :],
                                       wq0[:, c, half * 288:(half + 1) * 288],
                                       start=(c == 0), stop=(c == 1))
                mm.then_inc(sem("qkv_mm"), 1)

            pipeline(pe, [(frame_turn, 0), (mel, 1), (hn_turn, 2),
                          (spectrum, 0), (embed, 1), (project0, 2)], NT)

            pe.wait_ge(sem("colsum"), 3)
            pe.matmul(bank[7][:, 0:1], C("ones", KC), COLSUM[0:KC, 1:2], start=True, stop=True)
            pe.matmul(bank[7][:, 1:2], C("ones"), COLSUM[:, 2:3], start=True, stop=True)\
                .then_inc(sem("wsum_mm"), 1)
            pe.wait_ge(sem("l1_parts"), 2)
            pe.matmul(bank[7][:, 8:11], C("ones", ROWS), PART1[0:ROWS, :], start=True, stop=False)
            pe.matmul(bank[7][:, 8:11], C("ones", LAST), PART2[0:LAST, :], start=False, stop=True)\
                .then_inc(sem("l1_mm"), 1)

            def qk_turn(t):
                pe.wait_ge(sem("qk_ternary"), t + 1)
                at_least(pe, sem("qkT0"), t)
                if isinstance(t, int) and t == 0:
                    pe.wait_ge(sem("ident16"), 4)
                for c in range(6):
                    mm = pe.transpose(bank16[0][:, c * PITCH16:c * PITCH16 + ROWS],
                                      qk_pad[:, c * 128:(c + 1) * 128], ident16[0:ROWS, 0:ROWS])
                mm.then_inc(sem("qk_turned"), 1)

            def scores0_mm(t):
                pe.wait_ge(sem("qkT0"), t + 1)
                for r in range(4):
                    at_least(pe, sem("raw16"), 4 * t - 3 + r)
                for b in range(3):
                    for r in range(4):
                        mm = pe.matmul(bank[1 + r][0:ROWS, b * ROWS:(b + 1) * ROWS],
                                       qkT0[32 * r:32 * r + D0, (3 + b) * ROWS:(4 + b) * ROWS],
                                       qkT0[32 * r:32 * r + D0, b * ROWS:(b + 1) * ROWS],
                                       start=True, stop=True)
                        if b == 2:
                            mm.then_inc(sem("scores0_mm"), 1)

            pipeline(pe, [(qk_turn, 0), (scores0_mm, 1)], NT)

            pe.wait_ge(sem("abs0"), NT)
            pe.matmul(bank[5][:, 0:NT - 1], C("ones", ROWS), abs0[:, 0:NT - 1],
                      start=True, stop=True)
            pe.matmul(bank[5][:, NT - 1:NT], C("ones", LAST), abs0[0:LAST, NT - 1:NT],
                      start=True, stop=True).then_inc(sem("abs0_mm"), 1)

            def pv0(t):
                pe.wait_ge(sem("above_below"), t + 1)
                at_least(pe, sem("h1"), t)
                v, nv = tile_of(v16, t), tile_of(nv16, t)
                for n in range(HEADS):
                    head = 4 * (n % 3) + n // 3
                    o = bank[0][0:ROWS, head * D0:(head + 1) * D0]
                    pe.matmul(o, above_below[:, n * ROWS:(n + 1) * ROWS],
                              v[:, head * D0:(head + 1) * D0], start=True, stop=False)
                    mm = pe.matmul(o, above_below[:, WIDE + n * ROWS:WIDE + (n + 1) * ROWS],
                                   nv[:, head * D0:(head + 1) * D0], start=False, stop=True)
                mm.then_inc(sem("pv0_mm"), 1)

            pipeline(pe, [(pv0, 0)], NT)

            pe.wait_ge(sem("h1"), NT)
            pe.wait_ge(sem("in_attn1"), 48)

            def x2_turn(t):
                pe.wait_ge(sem("x2"), t + 1)
                at_least(pe, sem("logits"), t - 2)
                for c in range(2):
                    mm = pe.transpose(bank[1][0:KC, c * ROWS:(c + 1) * ROWS],
                                      x2[:, c * KC:(c + 1) * KC], ident[0:ROWS, 0:ROWS])
                mm.then_inc(sem("x2_turned"), 1)

            def qk1(t):
                pe.wait_ge(sem("x2T"), t + 1)
                at_least(pe, sem("masked"), t)
                for j in range(12):
                    for c in range(2):
                        mm = pe.matmul(bank[5 + j // 4][:, (j % 4) * ROWS:(j % 4 + 1) * ROWS],
                                       w1[:, c, j * 128:(j + 1) * 128], x2T[:, c, :],
                                       start=(c == 0), stop=(c == 1))
                    if j % 4 == 3:
                        mm.then_inc(sem("qk1_mm"), 1)

            def xq_turn(t):
                pe.wait_ge(sem("xq"), t + 1)
                at_least(pe, sem("yqT"), t)
                for c in range(2):
                    mm = pe.transpose(bank16[0][0:KC, c * PITCH16:c * PITCH16 + ROWS],
                                      xq[:, c * KC:(c + 1) * KC], ident16[0:ROWS, 0:ROWS])
                mm.then_inc(sem("xq_turned"), 1)

            def gated_turn(t):
                pe.wait_ge(sem("gated"), t + 1)
                at_least(pe, sem("vx"), capped(t + 2))
                for c in range(6):
                    mm = pe.transpose(bank[3 + c // 3][:, (c % 3) * ROWS:(c % 3 + 1) * ROWS],
                                      prod[:, c * 128:(c + 1) * 128], ident[0:ROWS, 0:ROWS])
                mm.then_inc(sem("gated_turned"), 1)

            def ffn_in(t):
                if isinstance(t, int) and t == 0:
                    pe.wait_ge(sem("win_ternary"), 1)
                pe.wait_ge(sem("xqT"), t + 1)
                at_least(pe, sem("outT"), t - 2)
                at_least(pe, sem("vx"), t - 1)
                for half in (1, 0):
                    for c in range(2):
                        mm = pe.matmul(bank[3 + half][0:ROWS, :], xqT[:, c * ROWS:(c + 1) * ROWS],
                                       win16[:, c, half * HID0:(half + 1) * HID0],
                                       start=(c == 0), stop=(c == 1))
                mm.then_inc(sem("ffn_in_mm"), 1)

            def probs_turn(t):
                pe.wait_ge(sem("probs"), t + 1)
                at_least(pe, sem("qkT1"), capped(3 * (t + 2), 3 * NT))
                for n in range(HEADS):
                    mm = pe.transpose(bank[5 + n // 4][0:ROWS, (n % 4) * ROWS:(n % 4 + 1) * ROWS],
                                      probs[:, n * ROWS:(n + 1) * ROWS], ident[0:ROWS, 0:ROWS])
                    if n % 4 == 3:
                        mm.then_inc(sem("probs_turned"), 1)

            def project1(t):
                pe.wait_ge(sem("outT"), t + 1)
                at_least(pe, sem("h2"), capped(t + 3))
                at_least(pe, sem("h3"), t)
                for c in range(6):
                    mm = pe.matmul(bank[2][0:ROWS, 0:DIM], outT[:, c * ROWS:(c + 1) * ROWS],
                                   wo1[:, c, :], start=(c == 0), stop=(c == 5))
                mm.then_inc(sem("project1_mm"), 1)

            def pv1(t):
                pe.wait_ge(sem("probsT"), 3 * (t + 1))
                pe.wait_ge(sem("vx"), t + 1)
                at_least(pe, sem("hidden_read"), capped(t + 3))
                at_least(pe, sem("outT"), t)
                for n, head in enumerate(ORDER1):
                    mm = pe.matmul(bank[3 + head // 6][0:ROWS, (head % 6) * 65:(head % 6 + 1) * 65],
                                   probsT[:, n * ROWS:(n + 1) * ROWS], vx[:, head, :],
                                   start=True, stop=True)
                mm.then_inc(sem("pv1_mm"), 1)

            def normed_turn(t):
                pe.wait_ge(sem("normed"), t + 1)
                at_least(pe, sem("x2T"), capped(t + 3))
                at_least(pe, sem("logits"), t)
                for c in range(2):
                    mm = pe.transpose(bank[1][0:KC, c * ROWS:(c + 1) * ROWS],
                                      row[:, c * KC:(c + 1) * KC], ident[0:ROWS, 0:ROWS])
                mm.then_inc(sem("normed_turned"), 1)

            def v1(t):
                at_least(pe, sem("prod"), t)
                at_least(pe, sem("hidden_read"), capped(t + 2))
                for half in range(2):
                    for c in range(2):
                        mm = pe.matmul(bank[3 + half][0:ROWS, 0:384], x2T[:, c, :],
                                       w1[:, c, 2 * INNER + half * 384:2 * INNER + (half + 1) * 384],
                                       start=(c == 0), stop=(c == 1))
                mm.then_inc(sem("v1_mm"), 1)

            def router_mm(t):
                pe.wait_ge(sem("nT"), t + 1)
                for c in range(2):
                    mm = pe.matmul(bank[1][0:ROWS, 0:EXPERTS], nT[:, c * ROWS:(c + 1) * ROWS],
                                   router[:, c, :], start=(c == 0), stop=(c == 1))
                mm.then_inc(sem("router_mm"), 1)

            def yq_turn(t):
                pe.wait_ge(sem("yq"), t + 1)
                pe.wait_ge(sem("xqT"), t + 1)
                for c in range(4):
                    mm = pe.transpose(bank16[0][:, c * PITCH16:c * PITCH16 + ROWS],
                                      yq[:, c * 128:(c + 1) * 128], ident16[0:ROWS, 0:ROWS])
                mm.then_inc(sem("yq_turned"), 1)

            def scores1(t):
                pe.wait_ge(sem("qkT1"), 3 * (t + 1))
                at_least(pe, sem("probsT"), 3 * t)
                def one(n):
                    head = ORDER1[n]
                    p, j = 64 * (head % 2), head // 2
                    return pe.matmul(bank[5 + n // 4][0:ROWS, (n % 4) * ROWS:(n % 4 + 1) * ROWS],
                                     qkT1[p:p + 64, j * ROWS:(j + 1) * ROWS],
                                     qkT1[p:p + 64, (6 + j) * ROWS:(7 + j) * ROWS],
                                     start=True, stop=True)

                one(8)
                one(9).then_inc(sem("even_heads"), 1)
                for n in range(8):
                    mm = one(n)
                    if n % 4 == 3:
                        mm.then_inc(sem("scores1_mm"), 1)
                pe.wait_ge(sem("even_heads"), t + 1)
                one(10)
                one(11).then_inc(sem("scores1_mm"), 1)

            def ffn_out(t):
                pe.wait_ge(sem("yqT"), t + 1)
                at_least(pe, sem("h3"), t - 2)
                at_least(pe, sem("h2"), t)
                for c in range(4):
                    mm = pe.matmul(bank[2][0:ROWS, 0:DIM], yqT[:, c * ROWS:(c + 1) * ROWS],
                                   wout16[:, c, :], start=(c == 0), stop=(c == 3))
                mm.then_inc(sem("ffn_out_mm"), 1)

            pipeline(pe, [(x2_turn, 1), (qk1, 1), (xq_turn, 0), (gated_turn, 3), (ffn_in, 0),
                          (probs_turn, 2), (project1, 3), (pv1, 2), (normed_turn, 3), (v1, 1),
                          (router_mm, 3), (yq_turn, 0), (scores1, 1), (ffn_out, 0)], NT)

            pe.wait_ge(sem("onehot"), 1)
            rank = bank[2][0:ROWS, 0:NT * EXPERTS]
            real = [ROWS] * (NT - 1) + [LAST]
            hot16 = lambda i, n=ROWS: onehot16[0:n, i * EXPERTS:(i + 1) * EXPERTS]
            for i in range(NT):
                o = rank[:, i * EXPERTS:(i + 1) * EXPERTS]
                pe.matmul(o, tri16[0:real[i], 0:ROWS], hot16(i, real[i]), start=True, stop=(i == 0))
                for before in range(i):
                    pe.matmul(o, ones16[0:ROWS, 0:ROWS], hot16(before), start=False,
                              stop=(before == i - 1))
            for i in range(NT):
                mm = pe.matmul(bank[3][:, 0:EXPERTS], ones16[0:real[i], :],
                               onehot16[0:real[i], i * EXPERTS:(i + 1) * EXPERTS],
                               start=(i == 0), stop=(i == NT - 1))
            mm.then_inc(sem("rank_mm"), 1)
            pe.wait_ge(sem("lanes"), 1)
            for i in range(NT):
                mm = pe.matmul(bank[4][:, 0:NS], lane_hot[0:real[i], i, :], token_at[0:real[i], i, :],
                               start=(i == 0), stop=(i == NT - 1))
            mm.then_inc(sem("slots_mm"), 1)

            pe.wait_ge(sem("picks"), 1)
            pe.wait_ge(sem("in_experts"), 8 * 16)

            def rows_turn(s, p):
                pe.wait_ge(sem(f"rows_in{p}"), 8 * (s - p) + 16)
                at_least(pe, sem("rowsT"), 2 * s)
                for c in range(2):
                    mm = pe.transpose(bank[0][:, c * SLOTS:(c + 1) * SLOTS],
                                      slot_rows[p][:, c * 128:(c + 1) * 128], ident)
                mm.then_inc(sem("rows_turned"), 1)

            def expert_in(s, p):
                own = pe.value_load(picks[0:1, bass.ds(s, 1)], min_val=0, max_val=7 * PAIR + BLOCK)
                both = pe.value_load(picks[0:1, bass.ds(s + NS + 1, 1)], min_val=0,
                                     max_val=7 * PAIR + 2 * BLOCK)
                pe.wait_ge(sem("rowsT"), 2 * (s + 1))
                at_least(pe, sem("hid"), 2 * s)
                for half in range(2):
                    pe.matmul(bank[1 + half][:, 0:384], rowsT[:, 0:SLOTS],
                              big[:, bass.ds(own + half * 384, 384)], start=True, stop=False)
                    mm = pe.matmul(bank[1 + half][:, 0:384], rowsT[:, SLOTS:2 * SLOTS],
                                   big[:, bass.ds(both + half * 384, 384)], start=False, stop=True)
                    mm.then_inc(sem("expert_in_mm"), 1)

            def hid_turn(s, p):
                pe.wait_ge(sem("hid"), 2 * (s + 1))
                at_least(pe, sem("hidT"), 2 * s)
                for c in range(6):
                    mm = pe.transpose(bank[3 + c // 3][:, (c % 3) * SLOTS:(c % 3 + 1) * SLOTS],
                                      hid[:, c * 128:(c + 1) * 128], ident)
                    if c % 3 == 2:
                        mm.then_inc(sem("hid_turned"), 1)

            def expert_out(s, p):
                own = pe.value_load(picks[0:1, bass.ds(s, 1)], min_val=0, max_val=7 * PAIR + BLOCK)
                pe.wait_ge(sem("hidT"), 2 * (s + 1))
                at_least(pe, sem("y_slots"), s)
                for c in range(6):
                    mm = pe.matmul(bank[5][:, 0:DIM], hidT[:, c * SLOTS:(c + 1) * SLOTS],
                                   big[:, bass.ds(own + (FF + c * DIM), DIM)],
                                   start=(c == 0), stop=(c == 5))
                mm.then_inc(sem("expert_out_mm"), 1)

            slot_pipeline(pe, [(rows_turn, 0), (hid_turn, 1), (expert_in, 0), (expert_out, 1)])

        @block.scalar
        def _(act):
            def by_chunk(a):
                return a.rearrange("p (c n) -> p c n", n=ROWS)

            def turned16(n):
                return bank16[0][:, 0:n * PITCH16].rearrange("p (c n) -> p c n", n=PITCH16)[:, :, 0:ROWS]

            def copy(out_, in_):
                return act.activation(out_, in_, ACT.Copy)

            act.wait_ge(sem("emb_mm"), 1)
            copy(w_emb, bank[7][0:MELS, 0:DIM]).then_inc(sem("w_emb"), 1)

            def frame_copy(t):
                act.wait_ge(sem("frame_turned"), t + 1)
                at_least(act, sem("spectrum_mm"), t)
                copy(frameT, bank[0][0:FRAME, 0:ROWS]).then_inc(sem("frameT"), 1)

            def square(t):
                act.wait_ge(sem("spectrum_mm"), t + 1)
                at_least(act, sem("mel_mm"), t)
                act.activation(power, bank[1][0:2 * BINS, 0:ROWS], ACT.Square)\
                    .then_inc(sem("power"), 1)

            def log(t):
                act.wait_ge(sem("mel_mm"), t + 1)
                at_least(act, sem("embed_mm"), t)
                act.activation(logmel, bank[2][0:MELS, 0:ROWS], ACT.Ln, bias=C("eps6", MELS))\
                    .then_inc(sem("logmel"), 1)

            def hnT_copy(t):
                act.wait_ge(sem("hn_turned"), t + 1)
                at_least(act, sem("qkv_mm"), t)
                copy(hnT, bank[4][0:KC, 0:2 * ROWS].rearrange("p (c n) -> p c n", c=2))\
                    .then_inc(sem("hnT"), 1)

            def qkv_copy(t):
                act.wait_ge(sem("qkv_mm"), t + 1)
                for half in range(2):
                    copy(tile_of(qkv, t)[:, half * 288:(half + 1) * 288],
                         bank[5 + half][0:ROWS, 0:288]).then_inc(sem("qkv"), 1)

            pipeline(act, [(frame_copy, 0), (log, 1), (hnT_copy, 2), (square, 0), (qkv_copy, 2)], NT)

            def qkT0_copy(t):
                act.wait_ge(sem("qk_turned"), t + 1)
                at_least(act, sem("scores0_mm"), 4 * t)
                copy(by_chunk(qkT0), turned16(6)).then_inc(sem("qkT0"), 1)

            def raw_copy(t):
                at_least(act, sem("scores0"), t)
                for r in range(4):
                    act.wait_ge(sem("scores0_mm"), 4 * t + r + 1)
                    copy(raw16[:, r * 375:(r + 1) * 375], bank[1 + r][0:ROWS, 0:375])\
                        .then_inc(sem("raw16"), 1)

            def abs_sum(t):
                act.wait_ge(sem("scores0"), t + 1)
                at_least(act, sem("abs0"), t)
                col = abs0[:, t:t + 1] if isinstance(t, int) else abs0[:, bass.ds(t, 1)]
                act.activation(junk16, tile_of(scores0, t), ACT.Abs, accum_out=col)\
                    .then_inc(sem("abs0"), 1)

            pipeline(act, [(qkT0_copy, 0), (raw_copy, 1), (abs_sum, 2)], NT)

            def x2T_copy(t):
                act.wait_ge(sem("x2_turned"), t + 1)
                at_least(act, sem("v1_mm"), t)
                copy(x2T, bank[1][0:KC, 0:2 * ROWS].rearrange("p (c n) -> p c n", c=2))\
                    .then_inc(sem("x2T"), 1)

            def log_var(t):
                act.wait_ge(sem("var64"), t + 1)
                act.activation(logv[:, :], var64[:, :], ACT.Ln,
                               scale=1.0 / (HEADS - 1), accum_out=small[0:ROWS, 40:41])\
                    .then_inc(sem("logvar"), 1)

            def qkT1_copy(t):
                at_least(act, sem("scores1_mm"), 3 * t)
                for b in range(3):
                    act.wait_ge(sem("qk1_mm"), 3 * t + b + 1)
                    copy(qkT1[:, b * 500:(b + 1) * 500], bank[5 + b][:, 0:500])\
                        .then_inc(sem("qkT1"), 1)

            def xqT_copy(t):
                act.wait_ge(sem("xq_turned"), t + 1)
                at_least(act, sem("ffn_in_mm"), t)
                copy(by_chunk(xqT), turned16(2)[0:KC]).then_inc(sem("xqT"), 1)

            def outT_copy(t):
                act.wait_ge(sem("gated_turned"), t + 1)
                at_least(act, sem("project1_mm"), t)
                copy(outT[:, 0:375], bank[3][:, 0:375])
                copy(outT[:, 375:750], bank[4][:, 0:375]).then_inc(sem("outT"), 1)

            def gate_exp(t):
                act.wait_ge(sem("ffn_in_mm"), t + 1)
                act.wait_ge(sem("xq"), t + 1)
                at_least(act, sem("y"), t)
                act.activation(egate, bank[4][0:ROWS, :], ACT.Exp, scale=small[0:ROWS, 12:13])\
                    .then_inc(sem("egate"), 1)

            def y_square(t):
                act.wait_ge(sem("y"), t + 1)
                act.activation(egate, ug, ACT.Square, accum_out=small[0:ROWS, 41:42])\
                    .then_inc(sem("ysum"), 1)

            def probsT_copy(t):
                at_least(act, sem("pv1_mm"), t)
                for b in range(3):
                    act.wait_ge(sem("probs_turned"), 3 * t + b + 1)
                    copy(probsT[:, b * 500:(b + 1) * 500], bank[5 + b][0:ROWS, 0:500])\
                        .then_inc(sem("probsT"), 1)

            def nT_copy(t):
                act.wait_ge(sem("normed_turned"), t + 1)
                at_least(act, sem("router_mm"), t)
                copy(nT, bank[1][0:KC, 0:2 * ROWS]).then_inc(sem("nT"), 1)

            def vx_copy(t):
                act.wait_ge(sem("v1_mm"), t + 1)
                at_least(act, sem("pv1_mm"), t)
                for half in range(2):
                    ins = copy(vx[:, half * 6:half * 6 + 6, 0:D1],
                               bank[3 + half][0:ROWS, 0:384].rearrange("p (h d) -> p h d", d=D1))
                ins.then_inc(sem("vx"), 1)

            def dev_square(t):
                act.wait_ge(sem("dev"), t + 1)
                act.activation(dev, dev, ACT.Square).then_inc(sem("sq"), 1)

            def router_exp(t):
                act.wait_ge(sem("logits"), t + 1)
                act.activation(small[0:ROWS, 44:60], tile_of(logits, t), ACT.Exp,
                               bias=small[0:ROWS, 43:44], accum_out=small[0:ROWS, 42:43])\
                    .then_inc(sem("router_exp"), 1)

            def yqT_copy(t):
                act.wait_ge(sem("yq_turned"), t + 1)
                at_least(act, sem("ffn_out_mm"), t)
                copy(by_chunk(yqT), turned16(4)).then_inc(sem("yqT"), 1)

            def softmax_exp(t):
                act.wait_ge(sem("rowmax"), t + 1)
                for n in range(HEADS):
                    o = probs[:, n * ROWS:(n + 1) * ROWS]
                    ins = act.activation(o, o, ACT.Exp, bias=nmax[:, n:n + 1], scale=D1 ** -0.5)
                ins.then_inc(sem("probs"), 1)

            pipeline(act, [(x2T_copy, 1), (log_var, 3), (qkT1_copy, 1), (xqT_copy, 0),
                           (outT_copy, 3), (gate_exp, 0), (probsT_copy, 2), (y_square, 0),
                           (nT_copy, 3), (vx_copy, 1), (dev_square, 2), (router_exp, 3),
                           (yqT_copy, 0), (softmax_exp, 1)], NT)

            def hid_relu(s, p):
                at_least(act, sem("hid_turned"), 2 * s)
                for half in range(2):
                    act.wait_ge(sem("expert_in_mm"), 2 * s + half + 1)
                    act.activation(hid[:, half * 384:(half + 1) * 384], bank[1 + half][:, 0:384],
                                   ACT.Relu).then_inc(sem("hid"), 1)

            slot_pipeline(act, [(hid_relu, 0)])

        @block.vector
        def _(v):
            v.wait_ge(sem("in_const"), 16)
            for dst, src in ((ident16, "ident"), (tri16, "tri"), (ones16, "ones")):
                v.tensor_copy(dst[:, :], C(src)).then_inc(sem("ident16"), 1)
            v.tensor_copy(same16[:, :], C("same", ROWS)).then_inc(sem("ident16"), 1)
            v.memset(qk_pad, 0.0).then_inc(sem("pads"), 1)
            v.wait_ge(sem("in_wq0"), 16)
            v.tensor_reduce(COLSUM[0:KC, 0:1], wq0, AX.XY, ALU.add, apply_absolute_value=True)\
                .then_inc(sem("colsum"), 1)
            v.wait_ge(sem("in_ffn"), 32)
            v.tensor_reduce(COLSUM[0:KC, 1:2], win_raw, AX.XY, ALU.add, apply_absolute_value=True)\
                .then_inc(sem("colsum"), 1)
            v.tensor_reduce(COLSUM[:, 2:3], wout_raw, AX.XY, ALU.add, apply_absolute_value=True)\
                .then_inc(sem("colsum"), 1)
            link = chain(v, "w_step")
            v.wait_ge(sem("wsum_mm"), 1)
            link(v.tensor_scalar(S_W, bank[6][:, 0:1], 1.0 / (3 * DIM * DIM), 1e-5, ALU.mult, ALU.add))
            link(v.reciprocal(R_W[:, 2:3], S_W))
            link(v.tensor_scalar(wq0, wq0, R_W[0:KC, 2:3], ROUND, ALU.mult, ALU.add))
            link(v.tensor_scalar(wq0, wq0, ROUND, 1.0, ALU.subtract, ALU.min))
            v.tensor_scalar(wq0, wq0, -1.0, None, ALU.max).then_inc(sem("wq0_ternary"), 1)

            v.wait_ge(sem("in_vec"), 80)
            mv = small[0:ROWS, 0:2]

            def statistics(link, src):
                hold(v)
                link(v.bn_stats(stats6[:, :], src))
                hold(v)
                link(v.bn_aggr(mv, stats6[:, :]))

            def rsqrt(name, t):
                v.wait_ge(sem(name + "_rsqrt"), t + 1)

            def embed_norm(t):
                link = chain(v, "embed_step", t, 2)
                v.wait_ge(sem("embed_mm"), t + 1)
                v.tensor_tensor(tile_of(h, t), bank[3][0:ROWS, 0:DIM], bprojb[:, :], ALU.add)\
                    .then_inc(sem("h0"), 1)
                v.wait_ge(sem("h0"), t + 1)
                at_least(v, sem("hn_turned"), t)
                statistics(link, tile_of(h, t))
                v.tensor_scalar(small[0:ROWS, 24:25], mv[:, 1:2], 1e-5, None, ALU.add)\
                    .then_inc(sem("embed_var"), 1)
                rsqrt("embed", t)
                v.tensor_scalar(hn, tile_of(h, t), mv[:, 0:1], small[0:ROWS, 25:26],
                                ALU.subtract, ALU.mult).then_inc(sem("hn"), 1)

            def l1_sums(t):
                v.wait_ge(sem("qkv"), 2 * (t + 1))
                hold(v)
                v.tensor_reduce(tile_of(l1sum, t), tile_of(qkv, t).rearrange("p (g d) -> p g d", d=D0),
                                AX.X, ALU.add, apply_absolute_value=True).then_inc(sem("l1sum"), 1)

            pipeline(v, [(embed_norm, 1), (l1_sums, 2)], NT)

            v.wait_ge(sem("l1sum"), NT)
            sums = l1sum.rearrange("p t n -> p (t n)")
            link(v.tensor_scalar(sums, sums, S_W[0:ROWS, :], None, ALU.mult))
            link(v.tensor_scalar(l1unit, sums, 1e-5, None, ALU.add))
            link(v.reciprocal(l1inv, l1unit))
            link(v.tensor_tensor(l1ratio, sums, l1inv, ALU.mult))
            by_kind = l1ratio.rearrange("p (t g n) -> p g t n", t=NT, g=3)
            v.tensor_reduce(PART1[0:ROWS, :], by_kind[:, :, 0:NT - 1, :], AX.XY, ALU.add)\
                .then_inc(sem("l1_parts"), 1)
            v.tensor_reduce(PART2[0:ROWS, :], by_kind[:, :, NT - 1, :], AX.X, ALU.add)\
                .then_inc(sem("l1_parts"), 1)
            v.wait_ge(sem("l1_mm"), 1)
            link(v.tensor_scalar(S_QKV, bank[7][:, 8:11], 1.0 / (TOKENS * DIM), 1e-5, ALU.mult, ALU.add))
            link(v.reciprocal(R_QKV, S_QKV))
            link(v.tensor_scalar(l1inv, l1inv, S_W[0:ROWS, :], None, ALU.mult))
            link(v.tensor_tensor(
                l1unit.rearrange("p (t g n) -> p t g n", t=NT, g=3),
                l1inv.rearrange("p (t g n) -> p t g n", t=NT, g=3),
                R_QKV[0:ROWS, :].unsqueeze(1).unsqueeze(3).to_broadcast([ROWS, NT, 3, HEADS]),
                ALU.mult))
            unit3 = l1unit.rearrange("p (t n) -> p t n", t=NT)

            def ternary(t):
                link = chain(v, "ternary_step", t, 3)
                link(v.tensor_tensor(
                    unit.rearrange("p (g d) -> p g d", d=D0),
                    tile_of(qkv, t).rearrange("p (g d) -> p g d", d=D0),
                    tile_of(unit3, t).unsqueeze(2).to_broadcast([ROWS, 3 * HEADS, D0]), ALU.mult))
                link(v.tensor_scalar(whole, unit, ROUND, ROUND, ALU.add, ALU.subtract))
                at_least(v, sem("qk_turned"), t)
                v.tensor_scalar(qk_pad.rearrange("p (g w) -> p g w", w=32)[:, :, 0:D0],
                                whole[:, 0:2 * DIM].rearrange("p (g d) -> p g d", d=D0),
                                1.0, -1.0, ALU.min, ALU.max).then_inc(sem("qk_ternary"), 1)
                link(v.tensor_scalar(tile_of(v16, t), whole[:, 2 * DIM:3 * DIM], 1.0, -1.0,
                                     ALU.min, ALU.max))
                v.tensor_scalar(tile_of(nv16, t), tile_of(v16, t), -1.0, None, ALU.mult)\
                    .then_inc(sem("values16"), 1)

            def mask0(t):
                v.wait_ge(sem("raw16"), 4 * (t + 1))
                v.tensor_tensor(tile_of(scores0, t).rearrange("p (h n) -> p h n", h=HEADS),
                                raw16.rearrange("p (h n) -> p h n", h=HEADS),
                                same16[:, :].unsqueeze(1).to_broadcast([ROWS, HEADS, ROWS]),
                                ALU.mult).then_inc(sem("scores0"), 1)

            v.wait_ge(sem("pads"), 1)
            pipeline(v, [(ternary, 0), (mask0, 1)], NT)

            v.wait_ge(sem("wsum_mm"), 2)
            link(v.tensor_scalar(S_IN, bank[7][:, 0:1], 1.0 / (2 * HID0 * DIM), 1e-5, ALU.mult, ALU.max))
            link(v.tensor_scalar(S_OUT, bank[7][:, 1:2], 1.0 / (HID0 * DIM), 1e-5, ALU.mult, ALU.max))
            link(v.reciprocal(R_W[:, 0:2], scal[:, 1:3]))
            link2 = chain(v, "w2_step")
            link2(v.tensor_scalar(win_raw, win_raw, R_W[0:KC, 0:1], ROUND, ALU.mult, ALU.add))
            link2(v.tensor_scalar(win_raw, win_raw, ROUND, 1.0, ALU.subtract, ALU.min))
            v.tensor_scalar(win16[:, :, :], win_raw, -1.0, None, ALU.max).then_inc(sem("win_ternary"), 1)
            link2(v.tensor_scalar(wout_raw, wout_raw, R_W[:, 1:2], ROUND, ALU.mult, ALU.add))
            link2(v.tensor_scalar(wout_raw, wout_raw, ROUND, 1.0, ALU.subtract, ALU.min))
            v.tensor_scalar(wout16[:, :, :], wout_raw, -1.0, None, ALU.max).then_inc(sem("win_ternary"), 1)

            v.wait_ge(sem("abs0_mm"), 1)
            link2(v.tensor_reduce(INT_SUM, bank[5][:, 0:NT], AX.X, ALU.add))
            link2(v.scalar_tensor_tensor(GAIN, S_QKV[:, 0:1], D0 ** -0.5, S_QKV[:, 1:2], ALU.mult, ALU.mult))
            link2(v.tensor_tensor(S_A, INT_SUM, GAIN, ALU.mult))
            link2(v.tensor_scalar(S_A, S_A, 1.0 / (CLIPS * HEADS * SEQ * SEQ), 1e-5, ALU.mult, ALU.add))
            link2(v.reciprocal(IGAIN, GAIN))
            link2(v.scalar_tensor_tensor(T_HI, S_A, 0.5, IGAIN, ALU.mult, ALU.mult))
            link2(v.tensor_scalar(T_LO, T_HI, -1.0, None, ALU.mult))
            link2(v.tensor_tensor(FAC0, S_A, S_QKV[:, 2:3], ALU.mult))

            def thresholds(t):
                at_least(v, sem("pv0_mm"), t)
                s = tile_of(scores0, t)
                v.tensor_scalar(above_below[:, 0:WIDE], s, T_HI[0:ROWS, :], None, ALU.is_gt)
                v.tensor_scalar(above_below[:, WIDE:2 * WIDE], s, T_LO[0:ROWS, :], None, ALU.is_lt)\
                    .then_inc(sem("above_below"), 1)

            def add_attn0(t):
                v.wait_ge(sem("pv0_mm"), t + 1)
                v.scalar_tensor_tensor(tile_of(h, t), bank[0][0:ROWS, 0:DIM], FAC0[0:ROWS, :],
                                       tile_of(h, t), ALU.mult, ALU.add).then_inc(sem("h1"), 1)

            pipeline(v, [(thresholds, 0), (add_attn0, 1)], NT)

            v.memset(vx[:, :, D1:D1 + 1], 1.0).then_inc(sem("vx_ones"), 1)

            def quantise(t):
                link = chain(v, "quant_step", t, 7)
                s = lambda a: small[0:ROWS, a:a + 1]
                v.wait_ge(sem("h1"), t + 1)
                x = tile_of(h, t)
                at_least(v, sem("x2_turned"), t)
                statistics(link, x)
                v.tensor_scalar(s(26), s(1), 1 + 1e-6, 1e-11, ALU.mult, ALU.add)\
                    .then_inc(sem("quant_var"), 1)
                link(v.scalar_tensor_tensor(xz, x, s(0), ginb[:, :], ALU.subtract, ALU.mult))
                link(v.tensor_reduce(s(5), xz, AX.X, ALU.max, apply_absolute_value=True))
                rsqrt("quant", t)
                link(v.tensor_tensor(s(7), s(5), s(27), ALU.mult))
                link(v.tensor_scalar(s(8), s(7), 1e-5, 1.0 / 127, ALU.max, ALU.mult))
                link(v.reciprocal(s(9), s(8)))
                link2 = chain(v, "quant_step2", t, 5)
                link2(v.tensor_tensor(s(10), s(27), s(9), ALU.mult))
                link2(v.tensor_tensor(s(11), s(8), S_IN[0:ROWS, :], ALU.mult))
                link2(v.tensor_tensor(s(13), s(11), s(11), ALU.mult))
                link2(v.tensor_scalar(s(12), s(11), -1.0, None, ALU.mult))
                link2(v.tensor_scalar(xz, xz, s(10), ROUND, ALU.mult, ALU.add))
                at_least(v, sem("xq_turned"), t)
                v.tensor_scalar(xq, xz, ROUND, None, ALU.subtract).then_inc(sem("xq"), 1)

            def silu_quantise(t):
                s = lambda a: small[0:ROWS, a:a + 1]
                link = chain(v, "y_step", t, 7)
                v.wait_ge(sem("egate"), t + 1)
                at_least(v, sem("ysum"), t)
                link(v.tensor_copy(yz, bank[3][0:ROWS, :]))
                v.scalar_tensor_tensor(ug, bank[4][0:ROWS, :], s(13), yz, ALU.mult, ALU.mult)\
                    .then_inc(sem("hidden_read"), 1)
                link(v.tensor_scalar(egate, egate, 1.0, None, ALU.add))
                link(v.reciprocal(egate, egate))
                v.wait_ge(sem("hidden_read"), t + 1)
                v.tensor_tensor(ug, ug, egate, ALU.mult).then_inc(sem("y"), 1)
                v.wait_ge(sem("y"), t + 1)
                link(v.tensor_tensor(yz, ug, goutb[:, :], ALU.mult))
                link(v.tensor_reduce(s(14), yz, AX.X, ALU.max, apply_absolute_value=True))
                v.wait_ge(sem("ysum"), t + 1)
                v.tensor_scalar(s(28), s(41), 1.0 / HID0, 1e-6, ALU.mult, ALU.add)\
                    .then_inc(sem("y_var"), 1)
                rsqrt("y", t)
                link(v.tensor_tensor(s(17), s(14), s(29), ALU.mult))
                link(v.tensor_scalar(s(18), s(17), 1e-5, 1.0 / 127, ALU.max, ALU.mult))
                link2 = chain(v, "y_step2", t, 4)
                link2(v.reciprocal(s(19), s(18)))
                link2(v.tensor_tensor(s(20), s(19), s(29), ALU.mult))
                link2(v.tensor_tensor(s(21), s(18), S_OUT[0:ROWS, :], ALU.mult))
                link2(v.tensor_scalar(yz, yz, s(20), ROUND, ALU.mult, ALU.add))
                at_least(v, sem("yq_turned"), t)
                v.tensor_scalar(yq, yz, ROUND, None, ALU.subtract).then_inc(sem("yq"), 1)

            def add_ffn_norm(t):
                link = chain(v, "x2_step", t, 2)
                v.wait_ge(sem("ffn_out_mm"), t + 1)
                v.scalar_tensor_tensor(tile_of(h, t), bank[2][0:ROWS, 0:DIM], small[0:ROWS, 21:22],
                                       tile_of(h, t), ALU.mult, ALU.add).then_inc(sem("h2"), 1)
                v.wait_ge(sem("h2"), t + 1)
                at_least(v, sem("x2_turned"), t)
                statistics(link, tile_of(h, t))
                v.tensor_scalar(small[0:ROWS, 30:31], mv[:, 1:2], 1e-5, None, ALU.add)\
                    .then_inc(sem("x2_var"), 1)
                rsqrt("x2", t)
                v.tensor_scalar(x2, tile_of(h, t), mv[:, 0:1], small[0:ROWS, 31:32],
                                ALU.subtract, ALU.mult).then_inc(sem("x2"), 1)

            def mask_max(t):
                link = chain(v, "max_step", t, 1)
                at_least(v, sem("probs_turned"), 3 * t)
                for b in range(3):
                    v.wait_ge(sem("scores1_mm"), 3 * t + b + 1)
                    ins = v.tensor_tensor(
                        probs[:, b * 500:(b + 1) * 500].rearrange("p (h n) -> p h n", h=4),
                        bank[5 + b][0:ROWS, 0:500].rearrange("p (h n) -> p h n", h=4),
                        C("other", ROWS).unsqueeze(1).to_broadcast([ROWS, 4, ROWS]), ALU.add)
                ins.then_inc(sem("masked"), 1)
                v.wait_ge(sem("masked"), t + 1)
                link(v.tensor_reduce(rowmax[:, :], probs.rearrange("p (h n) -> p h n", h=HEADS),
                                     AX.X, ALU.max))
                v.tensor_scalar(nmax[:, :], rowmax[:, :], -(D1 ** -0.5), None, ALU.mult)\
                    .then_inc(sem("rowmax"), 1)

            def product(t):
                link = chain(v, "prod_step", t, 3)
                v.wait_ge(sem("pv1_mm"), t + 1)
                prod3 = prod.rearrange("p (h d) -> p h d", h=HEADS)
                pv = [bank[3 + i][0:ROWS, 0:390].rearrange("p (h d) -> p h d", d=D1 + 1) for i in range(2)]
                v.reciprocal(rsum[:, 0:6], pv[0][:, :, D1:D1 + 1].rearrange("p h a -> p (h a)"))
                link(v.reciprocal(rsum[:, 6:12], pv[1][:, :, D1:D1 + 1].rearrange("p h a -> p (h a)")))
                at_least(v, sem("gated_turned"), t)
                for i in range(2):
                    ins = v.tensor_tensor(
                        prod3[:, 6 * i:6 * i + 6, :], pv[i][:, :, 0:D1],
                        rsum[:, 6 * i:6 * i + 6].unsqueeze(2).to_broadcast([ROWS, 6, D1]), ALU.mult)
                ins.then_inc(sem("prod"), 1)
                v.wait_ge(sem("prod"), t + 1)
                link(v.tensor_reduce(mean64[:, :], prod.rearrange("p (h d) -> p d h", h=HEADS),
                                     AX.X, ALU.add))
                link(v.tensor_scalar(mean64[:, :], mean64[:, :], 1.0 / HEADS, None, ALU.mult))
                v.tensor_tensor(dev.rearrange("p (h d) -> p h d", h=HEADS), prod3,
                                mean64[:, :].unsqueeze(1).to_broadcast([ROWS, HEADS, D1]),
                                ALU.subtract).then_inc(sem("dev"), 1)

            def variance(t):
                v.wait_ge(sem("sq"), t + 1)
                v.tensor_reduce(var64[:, :], dev.rearrange("p (h d) -> p d h", h=HEADS),
                                AX.X, ALU.add).then_inc(sem("var64"), 1)

            def gate_heads(t):
                link = chain(v, "gate_step", t, 5)
                dev3 = dev.rearrange("p (h d) -> p h d", h=HEADS)
                v.wait_ge(sem("var64"), t + 1)
                link(v.reciprocal(ivar64[:, :], var64[:, :]))
                link(v.tensor_tensor(dev3, dev3, ivar64[:, :].unsqueeze(1)
                                     .to_broadcast([ROWS, HEADS, D1]), ALU.mult))
                link(v.tensor_reduce(factor[:, :], dev3, AX.X, ALU.add))
                v.wait_ge(sem("logvar"), t + 1)
                link(v.tensor_scalar(small[0:ROWS, 22:23], small[0:ROWS, 40:41], -1.0,
                                     -0.5 * D1 * LOG2PI, ALU.mult, ALU.add))
                link(v.tensor_scalar(factor[:, :], factor[:, :], 0.25 * (HEADS - 1),
                                     small[0:ROWS, 22:23], ALU.mult, ALU.add))
                v.tensor_tensor(prod.rearrange("p (h d) -> p h d", h=HEADS),
                                prod.rearrange("p (h d) -> p h d", h=HEADS),
                                factor[:, :].unsqueeze(2).to_broadcast([ROWS, HEADS, D1]),
                                ALU.mult).then_inc(sem("gated"), 1)

            def add_attn1_norm(t):
                link = chain(v, "h3_step", t, 5)
                v.wait_ge(sem("project1_mm"), t + 1)
                at_least(v, sem("row_stored"), 16 * t)
                v.tensor_tensor(h3, bank[2][0:ROWS, 0:DIM], tile_of(h, t), ALU.add)\
                    .then_inc(sem("h3"), 1)
                v.wait_ge(sem("h3"), t + 1)
                link(v.tensor_tensor(h3, h3, boutb[:, :], ALU.add))
                s = lambda a: small[0:ROWS, a:a + 1]
                x3 = tile_of(h, t)
                statistics(link, h3)
                link(v.tensor_scalar(s(33), s(1), 1 + 1e-6, 1e-11, ALU.mult, ALU.add))
                v.tensor_scalar(s(32), s(1), 1e-5, None, ALU.add).then_inc(sem("h3_var"), 1)
                rsqrt("h3", t)
                v.scalar_tensor_tensor(row[:, 0:DIM], h3, s(0), lnwb[:, :], ALU.subtract, ALU.mult)\
                    .then_inc(sem("h3_centred"), 1)
                link(v.tensor_scalar(x3, h3, s(0), s(34), ALU.subtract, ALU.mult))
                v.wait_ge(sem("h3_centred"), t + 1)
                v.tensor_scalar(row[:, 0:DIM], row[:, 0:DIM], s(35), None, ALU.mult)\
                    .then_inc(sem("normed"), 1)
                v.wait_ge(sem("normed"), t + 1)
                v.tensor_copy(row[:, DIM:DIM + 64], row[:, 128:DIM])
                v.tensor_tensor(h3, x3, h3, ALU.add).then_inc(sem("row_dup"), 1)

            def router_gate(t):
                v.wait_ge(sem("router_mm"), t + 1)
                link = chain(v, "router_step", t, 2)
                lg = tile_of(logits, t)
                link(v.tensor_copy(lg, bank[1][0:ROWS, 0:EXPERTS]))
                hold(v)
                link(v.tensor_reduce(small[0:ROWS, 23:24], lg, AX.X, ALU.max))
                v.tensor_scalar(small[0:ROWS, 43:44], small[0:ROWS, 23:24], -1.0, None, ALU.mult)\
                    .then_inc(sem("logits"), 1)
                v.wait_ge(sem("router_exp"), t + 1)
                v.wait_ge(sem("row_dup"), t + 1)
                v.reciprocal(row[:, GATE:GATE + 1], small[0:ROWS, 42:43]).then_inc(sem("row_ready"), 1)

            v.memset(row[:, :], 0.0).then_inc(sem("vx_ones"), 1)
            v.wait_ge(sem("vx_ones"), 2)
            pipeline(v, [(variance, 3), (quantise, 0), (gate_heads, 3), (silu_quantise, 0),
                         (add_attn1_norm, 3), (product, 2), (router_gate, 3), (mask_max, 1),
                         (add_ffn_norm, 0)], NT)

            link = chain(v, "route_step")
            v.wait_ge(sem("logits"), NT)
            grid = [ROWS, NT, EXPERTS]
            lg = logits[:, :, :]
            link(v.tensor_reduce(best, lg, AX.X, ALU.max))
            link(v.tensor_tensor(hot, lg, best.unsqueeze(2).to_broadcast(grid), ALU.is_equal))
            link(v.tensor_tensor(hot, hot, C("rev", ROWS).unsqueeze(1).to_broadcast(grid), ALU.mult))
            link(v.tensor_reduce(best, hot, AX.X, ALU.max))
            link(v.tensor_tensor(hot, hot, best.unsqueeze(2).to_broadcast(grid), ALU.is_equal))
            v.tensor_copy(onehot16, hot.rearrange("p t e -> p (t e)")).then_inc(sem("onehot"), 1)
            v.wait_ge(sem("rank_mm"), 1)
            link(v.tensor_copy(cnt, bank[3][:, 0:EXPERTS]))
            link(v.tensor_tensor(cmp13, cnt.unsqueeze(2).to_broadcast([128, EXPERTS, NT]),
                                 C("count").unsqueeze(1).to_broadcast([128, EXPERTS, NT]), ALU.is_gt))
            link(v.tensor_reduce(ntile, cmp13, AX.X, ALU.add))
            link(v.tensor_tensor(cmp16, ntile.unsqueeze(1).to_broadcast([128, EXPERTS, EXPERTS]),
                                 C("below").rearrange("p (a b) -> p a b", a=EXPERTS), ALU.mult))
            link(v.tensor_reduce(base, cmp16, AX.X, ALU.add))
            link(v.tensor_scalar(base128, base, float(SLOTS), None, ALU.mult))
            link(v.tensor_tensor(where, bank[2][0:ROWS, 0:NT * EXPERTS]
                                 .rearrange("p (t e) -> p t e", e=EXPERTS),
                                 base128[0:ROWS, :].unsqueeze(1).to_broadcast(grid), ALU.add))
            link(v.tensor_tensor(where, where, hot, ALU.mult))
            link(v.tensor_reduce(pos, where, AX.X, ALU.add))
            link(v.tensor_copy(pos_i, pos))
            link(v.tensor_scalar(lane_i, pos_i, SLOTS - 1, None, ALU.bitwise_and))
            link(v.tensor_scalar(tile_i, pos_i, 7, None, ALU.logical_shift_right))
            link(v.tensor_copy(lane_f, lane_i))
            link(v.tensor_copy(tile_f, tile_i))
            link(v.tensor_tensor(lane_hot, C("lane", ROWS).unsqueeze(1).to_broadcast([ROWS, NT, 128]),
                                 lane_f.unsqueeze(2).to_broadcast([ROWS, NT, 128]), ALU.is_equal))
            link(v.tensor_tensor(token_at, C("slot", ROWS).unsqueeze(1).to_broadcast([ROWS, NT, NS]),
                                 tile_f.unsqueeze(2).to_broadcast([ROWS, NT, NS]), ALU.is_equal))
            v.tensor_tensor(token_at, token_at, C("token", ROWS).unsqueeze(2)
                            .to_broadcast([ROWS, NT, NS]), ALU.mult).then_inc(sem("lanes"), 1)
            link(v.tensor_tensor(ends, base, ntile, ALU.add))
            link(v.tensor_tensor(cmp28, ends.unsqueeze(1).to_broadcast([128, NS, EXPERTS]),
                                 C("slot").unsqueeze(2).to_broadcast([128, NS, EXPERTS]), ALU.is_le))
            link(v.tensor_reduce(expert, cmp28, AX.X, ALU.add))
            link(v.tensor_scalar(expert, expert, float(EXPERTS - 1), None, ALU.min))
            link(v.tensor_copy(expert_i, expert))
            link(v.tensor_scalar(odd_i, expert_i, 1, None, ALU.bitwise_and))
            link(v.tensor_copy(odd, odd_i))
            link(v.tensor_tensor(pair2, expert, odd, ALU.subtract))
            link(v.tensor_scalar(own_f, pair2, PAIR / 2.0, None, ALU.mult))
            link(v.tensor_scalar(both_f, own_f, float(2 * BLOCK), None, ALU.add))
            link(v.scalar_tensor_tensor(own_f, odd, float(BLOCK), own_f, ALU.mult, ALU.add))
            link(v.tensor_scalar(mine[:, 0:NS], odd, C("side"), None, ALU.is_equal))
            v.tensor_copy(picks[:, 0:NS], own_f)
            v.tensor_copy(picks[:, NS + 1:2 * NS + 1], both_f).then_inc(sem("picks"), 1)
            v.wait_ge(sem("slots_mm"), 1)
            link(v.tensor_copy(slot_f, bank[4][:, 0:NS]))
            link(v.tensor_scalar(empty, slot_f, 0.0, float(4 * TOKENS), ALU.is_equal, ALU.mult))
            link(v.scalar_tensor_tensor(slot_f, slot_f, -1.0, empty, ALU.add, ALU.add))
            for p in range(2):
                v.memset(slot_rows[p], 0.0).then_inc(sem("slots"), 1)
            v.tensor_copy(slot_i, slot_f).then_inc(sem("slots"), 1)

            def rowsT_copy(s, p):
                v.wait_ge(sem("rows_turned"), s + 1)
                at_least(v, sem("expert_in_mm"), 2 * s)
                v.tensor_copy(rowsT[:, 0:SLOTS], bank[0][:, 0:SLOTS]).then_inc(sem("rowsT"), 1)
                m = mine[:, s:s + 1] if isinstance(s, int) else mine[:, bass.ds(s, 1)]
                v.tensor_scalar(rowsT[:, SLOTS:2 * SLOTS], bank[0][:, SLOTS:2 * SLOTS], m, None,
                                ALU.mult).then_inc(sem("rowsT"), 1)

            def hidT_copy(s, p):
                at_least(v, sem("expert_out_mm"), s)
                for half in range(2):
                    v.wait_ge(sem("hid_turned"), 2 * s + half + 1)
                    v.tensor_copy(hidT[:, half * 384:(half + 1) * 384], bank[3 + half][:, 0:384])\
                        .then_inc(sem("hidT"), 1)

            def combine(s, p):
                v.wait_ge(sem("expert_out_mm"), s + 1)
                at_least(v, sem(f"y_stored{p}"), 8 * (s - p))
                r = slot_rows[p]
                v.scalar_tensor_tensor(y_out[p], bank[5][:, 0:DIM], r[:, GATE:GATE + 1],
                                       r[:, RES:RES + DIM], ALU.mult, ALU.add)\
                    .then_inc(sem("y_slots"), 1)

            slot_pipeline(v, [(rowsT_copy, 0), (hidT_copy, 1), (combine, 1)])

        @block.gpsimd
        def _(g):
            def powers(name, a, n=1):
                def stage(t):
                    g.wait_ge(sem(name + "_var"), t + 1)
                    g.tensor_tensor(small[0:ROWS, a + n:a + 2 * n], small[0:ROWS, a:a + n],
                                    C("minus_half", ROWS)[:, 0:n], ALU.pow)\
                        .then_inc(sem(name + "_rsqrt"), 1)
                return stage

            g.wait_ge(sem("in_const"), 16)
            pipeline(g, [(powers("embed", 24), 0)], NT)
            pipeline(g, [(powers("quant", 26), 0), (powers("y", 28), 0), (powers("h3", 32, 2), 3),
                         (powers("x2", 30), 0)], NT)

            g.wait_ge(sem("slots"), 3)
            g.wait_ge(sem("row_stored"), 16 * NT)

            def gather(s):
                if s >= 2:
                    g.wait_ge(sem("y_slots"), s - 1)
                g.indirect_dma_start(slot_rows[s % 2], None, rows_dram,
                                     bass.IndirectOffsetOnAxis(ap=slot_i[:, s:s + 1], axis=0),
                                     bounds_check=TOKENS - 1, oob_is_err=False)\
                    .then_inc(sem(f"rows_in{s % 2}"), 16)

            gather(0)
            gather(1)
            for s in range(NS):
                g.wait_ge(sem("y_slots"), s + 1)
                g.indirect_dma_start(out_rows, bass.IndirectOffsetOnAxis(ap=slot_i[:, s:s + 1], axis=0),
                                     y_out[s % 2], None,
                                     bounds_check=TOKENS - 1, oob_is_err=False)\
                    .then_inc(sem(f"y_stored{s % 2}"), 16)
                if s + 2 < NS:
                    gather(s + 2)
            for p in range(2):
                g.wait_ge(sem(f"y_stored{p}"), 8 * NS)

        for name, n, steps in chains:
            assert not steps or n[0] == steps, (name, n[0], steps)


def kernel(**inputs):
    import numpy as np
    import concourse.bacc as bacc
    from concourse.bass_utils import run_bass_kernel_spmd

    nc = bacc.Bacc("TRN2", target_bir_lowering=False, num_devices=1)
    arrays, args = {}, []

    def give(name, a):
        a = np.ascontiguousarray(a)
        arrays[name] = a
        args.append(nc.dram_tensor(name, a.shape, mybir.dt.from_np(a.dtype), kind="ExternalInput").ap())

    def chunks(w, rows):
        return w.reshape(-1, rows, w.shape[1]).transpose(1, 0, 2)

    i = {k: np.asarray(v) for k, v in inputs.items()}
    give("in_x", i["x"])
    give("in_consts", constants())
    mel = i["L0_tok_mel_filters"].T
    give("in_melT", np.concatenate([mel, mel], 0))
    give("in_dct", i["L0_tok_dct"])
    give("in_w_proj", i["L0_tok_w_proj"])
    give("in_b_proj", i["L0_tok_b_proj"])
    give("in_w_qkv0", chunks(i["L0_attn_w_qkv"].T, KC))
    give("in_w_in", chunks(i["L0_ffn_w_in"].T, KC))
    give("in_g_in", i["L0_ffn_g_in"])
    give("in_w_out0", chunks(i["L0_ffn_w_out"].T, 128))
    give("in_g_out", i["L0_ffn_g_out"])
    give("in_w_qkv1", chunks(i["L1_attn_w_qkv"], KC))
    give("in_w_out1", chunks(i["L1_attn_w_out"], 128))
    give("in_b_out", i["L1_attn_b_out"])
    give("in_ln_w", i["L1_ffn_ln_w"])
    give("in_w_router", chunks(i["L1_ffn_w_router"], KC))
    wi, wo = i["L1_ffn_wi"], i["L1_ffn_wo"]
    first = wi[:, 0:128, :]
    last = wi[:, 128:DIM, :].reshape(EXPERTS // 2, 128, FF)
    down = wo.reshape(EXPERTS, 6, 128, DIM).transpose(0, 2, 1, 3).reshape(EXPERTS, 128, 6 * DIM)
    give("in_experts", np.concatenate([first[0::2], down[0::2], first[1::2], down[1::2], last], 2))
    out = nc.dram_tensor("out", (CLIPS, SEQ, DIM), F32, kind="ExternalOutput").ap()
    rows_dram = nc.dram_tensor("rows_dram", (NT * ROWS, ROWLEN), F32, kind="Internal").ap()
    build(nc, *args, out, rows_dram)
    r = run_bass_kernel_spmd(nc, [arrays], core_ids=[0])
    return r.results[0]["out"]
```

```python
import concourse.bass as bass
from concourse import mybir
from contextlib import ExitStack

F32, BF16, I32 = mybir.dt.float32, mybir.dt.bfloat16, mybir.dt.int32
U32 = mybir.dt.uint32
ALU = mybir.AluOpType
ACT = mybir.ActivationFunctionType
AX = mybir.AxisListType

CLIPS, SAMPLES, FRAME, HOP = 64, 4000, 100, 160
SEQ, DIM = 25, 192
TOKENS = CLIPS * SEQ
ROWS = 5 * SEQ
NT = -(-TOKENS // ROWS)
LAST = TOKENS - (NT - 1) * ROWS
BINS, MELS, MFCC = FRAME // 2 + 1, 40, 13
KC = DIM // 2
HEADS = 12
D0 = DIM // HEADS
D1 = 64
INNER = HEADS * D1
HID0 = 512
FF, EXPERTS, SLOTS = 768, 16, 128
NS = (TOKENS - EXPERTS) // SLOTS + EXPERTS
RK = NT - 1
ROWLEN = 450
RES, GATE = 256, 448
BLOCK = FF + 6 * DIM
PAIR = 2 * BLOCK + FF
PITCH16 = ROWS + 1
WIDE = HEADS * ROWS
ORDER1 = (0, 2, 4, 6, 1, 3, 5, 7, 8, 10, 9, 11)
ROUND = 12582912.0
FFN_OUT = 256
LOG2PI = 1.8378770664093453
NEG = -1.0e30

CONST = {}
_at = 0
for _name, _n in (("ident", 128), ("tri", 128), ("ones", 128), ("same", ROWS), ("other", ROWS),
                  ("rev", EXPERTS), ("count", NT), ("below", EXPERTS * EXPERTS), ("slot", NS),
                  ("token", NT), ("lane", 128), ("side", 1), ("eps6", 1), ("minus_half", 2), ("dft", 2 * BINS)):
    CONST[_name] = (_at, _at + _n)
    _at += _n
CONSTS = _at


def constants():
    import numpy as np
    c = np.zeros((128, CONSTS), np.float64)

    def put(name, value, rows=128):
        a, b = CONST[name]
        c[:rows, a:b] = value

    p = np.arange(128)[:, None]
    j = np.arange(128)[None, :]
    put("ident", p == j)
    put("tri", p < j)
    put("ones", 1.0)
    q = np.arange(ROWS)[None, :]
    put("same", (p // SEQ) == (q // SEQ))
    put("other", np.where((p // SEQ) == (q // SEQ), 0.0, NEG))
    put("rev", EXPERTS - np.arange(EXPERTS)[None, :])
    put("count", SLOTS * np.arange(NT)[None, :])
    e = np.arange(EXPERTS)
    put("below", (e[None, :] < e[:, None]).reshape(1, -1))
    put("slot", np.arange(NS)[None, :])
    put("token", p + ROWS * np.arange(NT)[None, :] + 1)
    put("lane", j)
    put("side", p >= 64)
    put("eps6", 1e-6)
    put("minus_half", -0.5)
    n = np.arange(FRAME)[:, None]
    k = np.arange(BINS)[None, :]
    window = 0.54 - 0.46 * np.cos(2 * np.pi * n / (FRAME - 1))
    put("dft", np.concatenate([window * np.cos(2 * np.pi * n * k / FRAME),
                               -window * np.sin(2 * np.pi * n * k / FRAME)], 1), FRAME)
    return c.astype(np.float32)


def at_least(eng, sem, n):
    if not (isinstance(n, int) and n <= 0):
        eng.wait_ge(sem, n)


def capped(n, top=NT):
    return min(n, top) if isinstance(n, int) else n


def pipeline(eng, stages, tiles):
    top = max(lag for _, lag in stages)

    def step(s):
        for stage, lag in stages:
            if not isinstance(s, int) or 0 <= s - lag < tiles:
                stage(s - lag)

    for s in range(top + 1):
        step(s)
    with eng.Fori(top + 1, tiles) as s:
        step(s)
    for s in range(tiles, tiles + top):
        step(s)


def tile_of(t3, t):
    if isinstance(t, int):
        return t3[:, t, :]
    return t3[:, bass.ds(t, 1), :].rearrange("p a n -> p (a n)")


def build(nc, x, consts, melT, dct, w_proj, b_proj, w_qkv0, w_in, g_in, w_out0, g_out,
          w_qkv1, w_out1, b_out, ln_w, w_router, experts, out, rows_dram):
    ctx = ExitStack()
    with ctx:
        def sb(name, shape, dt=F32):
            return ctx.enter_context(nc.sbuf_tensor(name, shape, dt))

        sems = {}

        def sem(name):
            if name not in sems:
                sems[name] = ctx.enter_context(nc.semaphore(name))
            return sems[name]

        bank = [ctx.enter_context(nc.psum_tensor(f"bank{i}", [128, 512], F32)) for i in range(8)]
        bank16 = [b[:, :].bitcast(BF16) for b in bank]

        cst = sb("cst", [128, CONSTS])

        def C(name, rows=128):
            a, b = CONST[name]
            return cst[0:rows, a:b]

        h = sb("h", [ROWS, NT, DIM])
        ident16 = sb("ident16", [128, 128], BF16)
        tri16 = sb("tri16", [128, 128], BF16)
        ones16 = sb("ones16", [128, 128], BF16)
        same16 = sb("same16", [ROWS, ROWS], BF16)
        other16 = sb("other16", [ROWS, ROWS], BF16)
        bprojb = sb("bprojb", [ROWS, DIM])
        ginb = sb("ginb", [ROWS, DIM])
        goutb = sb("goutb", [ROWS, HID0])
        boutb = sb("boutb", [ROWS, DIM])
        lnwb = sb("lnwb", [ROWS, DIM])
        router = sb("router", [KC, 2, EXPERTS])
        win16 = sb("win16", [KC, 2, 2 * HID0], BF16)
        wout16 = sb("wout16", [128, 4, DIM], BF16)
        w1_mem = sb("w1_mem", [128, 2 * 3 * INNER])
        w1 = w1_mem[0:KC, :].rearrange("p (c n) -> p c n", c=2)
        wo1 = sb("wo1", [128, 6, DIM])
        scal = sb("scal", [128, 32])
        small = sb("small", [128, 64])
        logits = sb("logits", [ROWS, NT, EXPERTS])
        big = sb("big", [128, 8 * PAIR])

        def carve(start):
            at = [start]

            def take(n, dt=F32, rows=128):
                words = n if dt is not BF16 else -(-n // 2)
                a = big[0:rows, at[0]:at[0] + words]
                at[0] += words
                assert at[0] <= 8 * PAIR
                return a if dt is F32 else a.bitcast(dt)[:, 0:n]
            return take, at

        EARLY = 6 * PAIR
        take, early_end = carve(0)
        qkv = take(NT * 3 * DIM, rows=ROWS).rearrange("p (t n) -> p t n", t=NT)
        scores0 = take(NT * WIDE, BF16, ROWS).rearrange("p (t n) -> p t n", t=NT)
        v16 = take(NT * DIM, BF16, ROWS).rearrange("p (t n) -> p t n", t=NT)
        nv16 = take(NT * DIM, BF16, ROWS).rearrange("p (t n) -> p t n", t=NT)
        above = [take(WIDE // 2, BF16, ROWS) for _ in range(2)]
        below = [take(WIDE // 2, BF16, ROWS) for _ in range(2)]
        melT_sb = take(MELS, rows=2 * BINS)
        dct_sb = take(MELS, rows=MFCC)
        wproj_sb = take(DIM, rows=MFCC)
        w_emb = take(DIM, rows=MELS)
        wq0 = take(2 * 3 * DIM, rows=KC).rearrange("p (c n) -> p c n", c=2)
        frame = take(FRAME, rows=ROWS)
        frameT = take(ROWS, rows=FRAME)
        power = take(ROWS, rows=2 * BINS)
        logmel = take(ROWS, rows=MELS)
        hn = take(DIM, rows=ROWS)
        hnT = take(2 * ROWS, rows=KC).rearrange("p (c n) -> p c n", c=2)
        assert early_end[0] <= EARLY, early_end[0]
        take, _ = carve(EARLY)
        win_raw = take(2 * 2 * HID0, rows=KC).rearrange("p (c n) -> p c n", c=2)
        wout_raw = take(4 * DIM).rearrange("p (c n) -> p c n", c=4)
        l1sum = take(NT * 3 * HEADS, rows=ROWS).rearrange("p (t n) -> p t n", t=NT)
        l1inv = take(NT * 3 * HEADS, rows=ROWS)
        l1ratio = take(NT * 3 * HEADS, rows=ROWS)
        l1unit = take(NT * 3 * HEADS, rows=ROWS)
        unit = take(3 * DIM, rows=ROWS)
        whole = take(3 * DIM, rows=ROWS)
        qk_pad = take(2 * HEADS * 32, BF16, ROWS)
        qkT0 = take(6 * ROWS, BF16)
        junk16 = take(WIDE, BF16, ROWS)
        abs0 = take(NT, rows=ROWS)

        take, _ = carve(EARLY)
        xq = take(DIM, BF16, ROWS)
        xz = take(DIM, rows=ROWS)
        xqT = take(2 * ROWS, BF16, KC)
        egate = take(HID0, rows=ROWS)
        ug = take(HID0, rows=ROWS)
        yz = take(HID0, rows=ROWS)
        yq = take(HID0, BF16, ROWS)
        yqT = take(4 * ROWS, BF16)
        x2 = take(DIM, rows=ROWS)
        x2T = take(2 * ROWS, rows=KC).rearrange("p (c n) -> p c n", c=2)
        qkT1 = take(12 * ROWS)
        vx = take(HEADS * (D1 + 1), rows=ROWS).rearrange("p (h d) -> p h d", h=HEADS)
        probs = take(WIDE, rows=ROWS)
        probsT = take(WIDE, rows=ROWS)
        outT = take(6 * ROWS)
        nT = take(2 * ROWS, rows=KC)
        row = sb("row", [ROWS, ROWLEN])
        h3 = row[:, RES:RES + DIM]
        heads_mem = sb("heads_mem", [128, NT * 128])
        prod = heads_mem[0:ROWS, 0:INNER]
        dev = heads_mem[0:ROWS, INNER:2 * INNER]
        mean64 = sb("mean64", [ROWS, D1])
        var64 = sb("var64", [ROWS, D1])
        ivar64 = sb("ivar64", [ROWS, D1])
        logv = sb("logv", [ROWS, D1])
        stats6 = sb("stats6", [ROWS, 6])
        rowmax, nmax, rsum, factor = (sb(n, [ROWS, HEADS]) for n in ("rowmax", "nmax", "rsum", "factor"))

        def reuse_of(mem, size):
            spot = [0]

            def take(n, dt=F32, rows=128):
                words = n if dt is not BF16 else -(-n // 2)
                a = mem[0:rows, spot[0]:spot[0] + words]
                spot[0] += words
                assert spot[0] <= size
                return a if dt is F32 else a.bitcast(dt)[:, 0:n]
            return take

        reuse = reuse_of(w1_mem, 6 * INNER)

        slot_rows = [reuse(ROWLEN) for _ in range(4)]
        rowsT = [reuse(2 * SLOTS) for _ in range(2)]
        hid = reuse(FF)
        hidT = reuse(FF)
        y_out = [reuse(DIM) for _ in range(2)]
        token_at = reuse(NT * NS, rows=ROWS).rearrange("p (t s) -> p t s", t=NT)
        reuse = reuse_of(wo1[:, :, :].rearrange("p c n -> p (c n)"), 6 * DIM)
        onehot16 = reuse(NT * EXPERTS, BF16, ROWS)
        hot = reuse(NT * EXPERTS, rows=ROWS).rearrange("p (t e) -> p t e", t=NT)
        where = reuse(NT * EXPERTS, rows=ROWS).rearrange("p (t e) -> p t e", t=NT)
        cmp13 = reuse(EXPERTS * NT).rearrange("p (e k) -> p e k", e=EXPERTS)
        cmp16 = reuse(EXPERTS * EXPERTS).rearrange("p (a b) -> p a b", a=EXPERTS)
        lane_hot = heads_mem[0:ROWS, :].rearrange("p (t l) -> p t l", t=NT)
        cmp28 = sb("cmp28", [128, NS, EXPERTS])[:, :, :]
        best, pos, lane_f, tile_f = (sb(n, [ROWS, NT])[:, :] for n in ("best", "pos", "lane_f", "tile_f"))
        pos_i, lane_i, tile_i = (sb(n, [ROWS, NT], I32)[:, :] for n in ("pos_i", "lane_i", "tile_i"))
        cnt, ntile, base, base128, ends = (sb(n, [128, EXPERTS])[:, :]
                                           for n in ("cnt", "ntile", "base", "base128", "ends"))
        expert, odd, pair2, own_f, both_f = (
            sb(n, [128, NS])[:, :] for n in ("expert", "odd", "pair2", "own_f", "both_f"))
        mine = sb("mine", [128, NS + 4])
        expert_i, odd_i = (sb(n, [128, NS], I32)[:, :] for n in ("expert_i", "odd_i"))
        slot_f, empty = expert, pair2
        slot_i = sb("slot_i", [128, NS], I32)[:, :]
        picks = sb("picks", [128, 2 * NS + 6], I32)[:, :]
        out_rows = out.rearrange("b n c -> (b n) c")

        def slot_pipeline(eng, stages):
            assert NS % 4 == 0

            def step(s, k):
                for stage, lag in stages:
                    if not isinstance(s, int) or 0 <= s - lag < NS:
                        stage(s - lag, (k - lag) % 4)

            for k in range(4):
                step(k, k)
            with eng.Fori(4, NS, 4) as s:
                for k in range(4):
                    step(s + k, k)
            for k in range(max(lag for _, lag in stages)):
                step(NS + k, k)

        block = ctx.enter_context(nc.Block())

        chains = []

        def chain(eng, name, t=0, steps=0):
            n = [0]
            chains.append((name, n, steps))

            def link(ins):
                n[0] += 1
                ins.then_inc(sem(name), 1)
                eng.wait_ge(sem(name), t * steps + n[0] if steps else n[0])
            return link

        def hold(eng):
            eng.sem_inc(sem("held"), 1)

        S_W, S_IN, S_OUT = (scal[:, i:i + 1] for i in (0, 1, 2))
        COLSUM = scal[:, 3:6]
        S_QKV, R_QKV = scal[:, 6:9], scal[:, 9:12]
        PART1, PART2 = scal[:, 12:15], scal[:, 15:18]
        GAIN, INT_SUM, S_A, T_HI, T_LO, FAC0 = (scal[:, i:i + 1] for i in range(18, 24))
        R_W = scal[:, 24:27]
        IGAIN = scal[:, 27:28]

        @block.sync
        def _(sp):
            sp.dma_start(cst[:, :], consts).then_inc(sem("in_const"), 16)
            sp.dma_start(melT_sb, melT).then_inc(sem("in_tok"), 16)
            sp.dma_start(dct_sb, dct).then_inc(sem("in_tok"), 16)
            sp.dma_start(wproj_sb, w_proj).then_inc(sem("in_tok"), 16)
            sp.dma_start(wq0, w_qkv0).then_inc(sem("in_wq0"), 16)
            frames = x.rearrange("b (n s) -> (b n) s", s=HOP)

            def load_frames(t):
                at_least(sp, sem("frame_turned"), t)
                if isinstance(t, int) and t == NT - 1:
                    sp.dma_start(frame[0:LAST, :], frames[t * ROWS:TOKENS, 0:FRAME])\
                        .then_inc(sem("frame_in"), 16)
                else:
                    sp.dma_start(frame, frames[bass.ds(t * ROWS, ROWS), 0:FRAME])\
                        .then_inc(sem("frame_in"), 16)

            load_frames(0)
            for dst, src in ((bprojb, b_proj), (ginb, g_in), (goutb, g_out), (boutb, b_out),
                             (lnwb, ln_w)):
                sp.dma_start(dst[:, :], src.partition_broadcast(ROWS)).then_inc(sem("in_vec"), 16)
            sp.dma_start(win_raw, w_in).then_inc(sem("in_ffn"), 16)
            sp.dma_start(wout_raw, w_out0).then_inc(sem("in_ffn"), 16)
            with sp.Fori(1, NT - 1) as t:
                load_frames(t)
            load_frames(NT - 1)
            sp.dma_start(w1, w_qkv1).then_inc(sem("in_attn1"), 16)
            sp.dma_start(wo1[:, :, :], w_out1).then_inc(sem("in_attn1"), 16)
            sp.dma_start(router[:, :, :], w_router).then_inc(sem("in_attn1"), 16)
            sp.wait_ge(sem("pv0_mm"), 2 * NT)
            for pair in range(6):
                sp.dma_start(big[:, pair * PAIR:(pair + 1) * PAIR], experts[pair, :, :])\
                    .then_inc(sem("in_experts"), 16)

            def store_row(t):
                sp.wait_ge(sem("row_ready"), t + 1)
                sp.dma_start(rows_dram[bass.ds(t * ROWS, ROWS), :], row[:, :])\
                    .then_inc(sem("row_stored"), 16)

            pipeline(sp, [(store_row, 0)], NT)
            sp.wait_ge(sem("row_ready"), NT)
            for pair in range(6, 8):
                sp.dma_start(big[:, pair * PAIR:(pair + 1) * PAIR], experts[pair, :, :])\
                    .then_inc(sem("in_experts"), 16)

        @block.tensor
        def _(pe):
            ident = C("ident")

            pe.wait_ge(sem("in_const"), 16)
            pe.wait_ge(sem("in_tok"), 48)
            pe.matmul(bank[7][0:MELS, 0:DIM], dct_sb, wproj_sb, start=True, stop=True)\
                .then_inc(sem("emb_mm"), 1)
            pe.wait_ge(sem("colsum"), 1)
            pe.matmul(bank[6][:, 0:1], C("ones", KC), COLSUM[0:KC, 0:1], start=True, stop=True)\
                .then_inc(sem("wsum_mm"), 1)

            def frame_turn(t):
                pe.wait_ge(sem("frame_in"), 16 * (t + 1))
                at_least(pe, sem("frameT"), t)
                pe.transpose(bank[0][0:FRAME, 0:ROWS], frame, ident[0:ROWS, 0:ROWS])\
                    .then_inc(sem("frame_turned"), 1)

            def spectrum(t):
                pe.wait_ge(sem("frameT"), t + 1)
                at_least(pe, sem("power"), t)
                pe.matmul(bank[1][0:2 * BINS, 0:ROWS], C("dft", FRAME), frameT,
                          start=True, stop=True).then_inc(sem("spectrum_mm"), 1)

            def mel(t):
                pe.wait_ge(sem("power"), t + 1)
                at_least(pe, sem("logmel"), t)
                pe.matmul(bank[2][0:MELS, 0:ROWS], melT_sb, power, start=True, stop=True)\
                    .then_inc(sem("mel_mm"), 1)

            def embed(t):
                if isinstance(t, int) and t == 0:
                    pe.wait_ge(sem("w_emb"), 1)
                pe.wait_ge(sem("logmel"), t + 1)
                at_least(pe, sem("h0"), t)
                pe.matmul(bank[3][0:ROWS, 0:DIM], logmel, w_emb, start=True, stop=True)\
                    .then_inc(sem("embed_mm"), 1)

            def hn_turn(t):
                pe.wait_ge(sem("hn"), t + 1)
                at_least(pe, sem("hnT"), t)
                for c in range(2):
                    mm = pe.transpose(bank[4][0:KC, c * ROWS:(c + 1) * ROWS],
                                      hn[:, c * KC:(c + 1) * KC], ident[0:ROWS, 0:ROWS])
                mm.then_inc(sem("hn_turned"), 1)

            def project0(t):
                if isinstance(t, int) and t == 0:
                    pe.wait_ge(sem("wq0_ternary"), 1)
                pe.wait_ge(sem("hnT"), t + 1)
                at_least(pe, sem("qkv"), 2 * t)
                for half in range(2):
                    for c in range(2):
                        mm = pe.matmul(bank[5 + half][0:ROWS, 0:288], hnT[:, c, :],
                                       wq0[:, c, half * 288:(half + 1) * 288],
                                       start=(c == 0), stop=(c == 1))
                mm.then_inc(sem("qkv_mm"), 1)

            pipeline(pe, [(frame_turn, 0), (mel, 1), (hn_turn, 2),
                          (spectrum, 0), (embed, 1), (project0, 2)], NT)

            pe.wait_ge(sem("colsum"), 3)
            pe.matmul(bank[7][:, 0:1], C("ones", KC), COLSUM[0:KC, 1:2], start=True, stop=True)
            pe.matmul(bank[7][:, 1:2], C("ones"), COLSUM[:, 2:3], start=True, stop=True)\
                .then_inc(sem("wsum_mm"), 1)
            pe.wait_ge(sem("l1_parts"), 2)
            pe.matmul(bank[7][:, 8:11], C("ones", ROWS), PART1[0:ROWS, :], start=True, stop=False)
            pe.matmul(bank[7][:, 8:11], C("ones", LAST), PART2[0:LAST, :], start=False, stop=True)\
                .then_inc(sem("l1_mm"), 1)

            def qk_turn(t):
                pe.wait_ge(sem("qk_ternary"), t + 1)
                at_least(pe, sem("qkT0"), t)
                if isinstance(t, int) and t == 0:
                    pe.wait_ge(sem("ident16"), 5)
                for c in range(6):
                    mm = pe.transpose(bank16[0][:, c * PITCH16:c * PITCH16 + ROWS],
                                      qk_pad[:, c * 128:(c + 1) * 128], ident16[0:ROWS, 0:ROWS])
                mm.then_inc(sem("qk_turned"), 1)

            def scores0_mm(t):
                pe.wait_ge(sem("qkT0"), t + 1)
                at_least(pe, sem("scores0"), 4 * t)
                for b in range(3):
                    for r in range(4):
                        mm = pe.matmul(bank[1 + r][0:ROWS, b * ROWS:(b + 1) * ROWS],
                                       qkT0[32 * r:32 * r + D0, (3 + b) * ROWS:(4 + b) * ROWS],
                                       qkT0[32 * r:32 * r + D0, b * ROWS:(b + 1) * ROWS],
                                       start=True, stop=True)
                        if b == 2:
                            mm.then_inc(sem("scores0_mm"), 1)

            pipeline(pe, [(qk_turn, 0), (scores0_mm, 1)], NT)

            pe.wait_ge(sem("abs0"), NT)
            pe.matmul(bank[5][:, 0:NT - 1], C("ones", ROWS), abs0[:, 0:NT - 1],
                      start=True, stop=True)
            pe.matmul(bank[5][:, NT - 1:NT], C("ones", LAST), abs0[0:LAST, NT - 1:NT],
                      start=True, stop=True).then_inc(sem("abs0_mm"), 1)

            def pv0(half):
                def stage(t):
                    pe.wait_ge(sem("above_below"), 2 * t + half + 1)
                    at_least(pe, sem("h1"), 2 * t - 1 + half)
                    v, nv = tile_of(v16, t), tile_of(nv16, t)
                    for n in range(6):
                        head = 4 * (n % 3) + n // 3 + 2 * half
                        o = bank[6 * half][0:ROWS, head * D0:(head + 1) * D0]
                        pe.matmul(o, above[half][:, n * ROWS:(n + 1) * ROWS],
                                  v[:, head * D0:(head + 1) * D0], start=True, stop=False)
                        mm = pe.matmul(o, below[half][:, n * ROWS:(n + 1) * ROWS],
                                       nv[:, head * D0:(head + 1) * D0], start=False, stop=True)
                    mm.then_inc(sem("pv0_mm"), 1)
                return stage

            pipeline(pe, [(pv0(0), 0), (pv0(1), 0)], NT)

            pe.wait_ge(sem("h1"), 2 * NT)
            pe.wait_ge(sem("in_attn1"), 48)

            def x2_turn(t):
                pe.wait_ge(sem("x2"), t + 1)
                at_least(pe, sem("logits"), t - 3)
                for c in range(2):
                    mm = pe.transpose(bank[1][0:KC, c * ROWS:(c + 1) * ROWS],
                                      x2[:, c * KC:(c + 1) * KC], ident[0:ROWS, 0:ROWS])
                mm.then_inc(sem("x2_turned"), 1)

            def qk1(t):
                pe.wait_ge(sem("x2T"), t + 1)
                at_least(pe, sem("probs"), t)
                for j in range(12):
                    for c in range(2):
                        mm = pe.matmul(bank[5 + j // 4][:, (j % 4) * ROWS:(j % 4 + 1) * ROWS],
                                       w1[:, c, j * 128:(j + 1) * 128], x2T[:, c, :],
                                       start=(c == 0), stop=(c == 1))
                    if j % 4 == 3:
                        mm.then_inc(sem("qk1_mm"), 1)

            def xq_turn(t):
                pe.wait_ge(sem("xq"), t + 1)
                at_least(pe, sem("h2"), t)
                for c in range(2):
                    mm = pe.transpose(bank16[0][0:KC, c * PITCH16:c * PITCH16 + ROWS],
                                      xq[:, c * KC:(c + 1) * KC], ident16[0:ROWS, 0:ROWS])
                mm.then_inc(sem("xq_turned"), 1)

            def gated_turn(t):
                pe.wait_ge(sem("gated"), t + 1)
                at_least(pe, sem("hidden_read"), capped(t + 4))
                at_least(pe, sem("vx"), capped(t + 2))
                for c in range(6):
                    mm = pe.transpose(bank[3 + c // 3][:, (c % 3) * ROWS:(c % 3 + 1) * ROWS],
                                      prod[:, c * 128:(c + 1) * 128], ident[0:ROWS, 0:ROWS])
                mm.then_inc(sem("gated_turned"), 1)

            def ffn_in(t):
                if isinstance(t, int) and t == 0:
                    pe.wait_ge(sem("win_ternary"), 1)
                pe.wait_ge(sem("xqT"), t + 1)
                at_least(pe, sem("vx"), t - 1)
                for half in (1, 0):
                    for c in range(2):
                        mm = pe.matmul(bank[3 + half][0:ROWS, :], xqT[:, c * ROWS:(c + 1) * ROWS],
                                       win16[:, c, half * HID0:(half + 1) * HID0],
                                       start=(c == 0), stop=(c == 1))
                mm.then_inc(sem("ffn_in_mm"), 1)

            def probs_turn(t):
                pe.wait_ge(sem("probs"), t + 1)
                for n in range(HEADS):
                    if n % 4 == 0:
                        at_least(pe, sem("qkT1"), capped(3 * (t + 1) + n // 4 + 1, 3 * NT))
                    mm = pe.transpose(bank[5 + n // 4][0:ROWS, (n % 4) * ROWS:(n % 4 + 1) * ROWS],
                                      probs[:, n * ROWS:(n + 1) * ROWS], ident[0:ROWS, 0:ROWS])
                    if n % 4 == 3:
                        mm.then_inc(sem("probs_turned"), 1)

            def project1(t):
                pe.wait_ge(sem("outT"), t + 1)
                at_least(pe, sem("h3"), t)
                for c in range(6):
                    mm = pe.matmul(bank[2][0:ROWS, 0:DIM], outT[:, c * ROWS:(c + 1) * ROWS],
                                   wo1[:, c, :], start=(c == 0), stop=(c == 5))
                mm.then_inc(sem("project1_mm"), 1)

            def pv1(t):
                pe.wait_ge(sem("probsT"), 3 * (t + 1))
                pe.wait_ge(sem("vx"), t + 1)
                at_least(pe, sem("hidden_read"), capped(t + 3))
                at_least(pe, sem("outT"), t)
                for n, head in enumerate(ORDER1):
                    mm = pe.matmul(bank[3 + head // 6][0:ROWS, (head % 6) * 65:(head % 6 + 1) * 65],
                                   probsT[:, n * ROWS:(n + 1) * ROWS], vx[:, head, :],
                                   start=True, stop=True)
                mm.then_inc(sem("pv1_mm"), 1)

            def normed_turn(t):
                pe.wait_ge(sem("normed"), t + 1)
                at_least(pe, sem("x2T"), capped(t + 4))
                at_least(pe, sem("logits"), t)
                for c in range(2):
                    mm = pe.transpose(bank[1][0:KC, c * ROWS:(c + 1) * ROWS],
                                      row[:, c * KC:(c + 1) * KC], ident[0:ROWS, 0:ROWS])
                mm.then_inc(sem("normed_turned"), 1)

            def v1(t):
                at_least(pe, sem("prod"), t)
                at_least(pe, sem("hidden_read"), capped(t + 2))
                for half in range(2):
                    for c in range(2):
                        mm = pe.matmul(bank[3 + half][0:ROWS, 0:384], x2T[:, c, :],
                                       w1[:, c, 2 * INNER + half * 384:2 * INNER + (half + 1) * 384],
                                       start=(c == 0), stop=(c == 1))
                mm.then_inc(sem("v1_mm"), 1)

            def router_mm(t):
                pe.wait_ge(sem("nT"), t + 1)
                for c in range(2):
                    mm = pe.matmul(bank[1][0:ROWS, 0:EXPERTS], nT[:, c * ROWS:(c + 1) * ROWS],
                                   router[:, c, :], start=(c == 0), stop=(c == 1))
                mm.then_inc(sem("router_mm"), 1)

            def yq_turn(t):
                pe.wait_ge(sem("yq"), t + 1)
                pe.wait_ge(sem("xqT"), t + 1)
                for c in range(4):
                    mm = pe.transpose(bank16[0][:, c * PITCH16:c * PITCH16 + ROWS],
                                      yq[:, c * 128:(c + 1) * 128], ident16[0:ROWS, 0:ROWS])
                mm.then_inc(sem("yq_turned"), 1)

            def scores1(t):
                pe.wait_ge(sem("qkT1"), 3 * (t + 1))
                for b in range(3):
                    at_least(pe, sem("probsT"), 3 * t - 2 + b)
                    mm = pe.matmul(bank[5 + b][0:ROWS, 0:4 * ROWS], ident16[0:ROWS, 0:ROWS],
                                   other16[:, :].unsqueeze(1).to_broadcast([ROWS, 4, ROWS]),
                                   start=True, stop=False)
                mm.then_inc(sem("mask_mm"), 1)
                pe.wait_ge(sem("mask_mm"), t + 1)

                def one(n):
                    head = ORDER1[n]
                    p, j = 64 * (head % 2), head // 2
                    return pe.matmul(bank[5 + n // 4][0:ROWS, (n % 4) * ROWS:(n % 4 + 1) * ROWS],
                                     qkT1[p:p + 64, j * ROWS:(j + 1) * ROWS],
                                     qkT1[p:p + 64, (6 + j) * ROWS:(7 + j) * ROWS],
                                     start=False, stop=(n % 4 == 3))

                one(8)
                one(9).then_inc(sem("even_heads"), 1)
                for n in range(8):
                    mm = one(n)
                    if n % 4 == 3:
                        mm.then_inc(sem("scores1_mm"), 1)
                pe.wait_ge(sem("even_heads"), t + 1)
                one(10)
                one(11).then_inc(sem("scores1_mm"), 1)

            def ffn_out(t):
                pe.wait_ge(sem("yqT"), t + 1)
                for c in range(4):
                    mm = pe.matmul(bank[0][0:ROWS, FFN_OUT:FFN_OUT + DIM], yqT[:, c * ROWS:(c + 1) * ROWS],
                                   wout16[:, c, :], start=(c == 0), stop=(c == 3))
                mm.then_inc(sem("ffn_out_mm"), 1)

            pipeline(pe, [(x2_turn, 1), (qk1, 1), (xq_turn, 0), (probs_turn, 2), (ffn_in, 0),
                          (scores1, 1), (normed_turn, 4), (gated_turn, 3), (router_mm, 4),
                          (pv1, 2), (yq_turn, 0), (project1, 3), (ffn_out, 0), (v1, 1)], NT)

            pe.wait_ge(sem("onehot"), 1)
            rank = bank[2][0:ROWS, 0:NT * EXPERTS]
            real = [ROWS] * (NT - 1) + [LAST]
            hot16 = lambda i, n=ROWS: onehot16[0:n, i * EXPERTS:(i + 1) * EXPERTS]
            for i in range(NT):
                o = rank[:, i * EXPERTS:(i + 1) * EXPERTS]
                pe.matmul(o, tri16[0:real[i], 0:ROWS], hot16(i, real[i]), start=True, stop=(i == 0))
                for before in range(i):
                    pe.matmul(o, ones16[0:ROWS, 0:ROWS], hot16(before), start=False,
                              stop=(before == i - 1))
            for i in range(NT):
                mm = pe.matmul(bank[3][:, 0:EXPERTS], ones16[0:real[i], :],
                               onehot16[0:real[i], i * EXPERTS:(i + 1) * EXPERTS],
                               start=(i == 0), stop=(i == NT - 1))
            mm.then_inc(sem("rank_mm"), 1)
            pe.wait_ge(sem("lanes"), 1)
            for i in range(NT):
                mm = pe.matmul(bank[4][:, 0:NS], lane_hot[0:real[i], i, :], token_at[0:real[i], i, :],
                               start=(i == 0), stop=(i == NT - 1))
            mm.then_inc(sem("slots_mm"), 1)

            pe.wait_ge(sem("picks"), 1)
            pe.wait_ge(sem("in_experts"), 8 * 16)

            def rows_turn(s, p):
                pe.wait_ge(sem(f"rows_in{p}"), 4 * (s - p) + 16)
                at_least(pe, sem("rowsT"), 2 * s)
                for c in range(2):
                    mm = pe.transpose(bank[0][:, c * SLOTS:(c + 1) * SLOTS],
                                      slot_rows[p][:, c * 128:(c + 1) * 128], ident)
                mm.then_inc(sem("rows_turned"), 1)

            def expert_in(s, p):
                own = pe.value_load(picks[0:1, bass.ds(s, 1)], min_val=0, max_val=7 * PAIR + BLOCK)
                both = pe.value_load(picks[0:1, bass.ds(s + NS + 1, 1)], min_val=0,
                                     max_val=7 * PAIR + 2 * BLOCK)
                pe.wait_ge(sem("rowsT"), 2 * (s + 1))
                at_least(pe, sem("hid"), 2 * s)
                for half in range(2):
                    pe.matmul(bank[1 + half][:, 0:384], rowsT[p % 2][:, 0:SLOTS],
                              big[:, bass.ds(own + half * 384, 384)], start=True, stop=False)
                    mm = pe.matmul(bank[1 + half][:, 0:384], rowsT[p % 2][:, SLOTS:2 * SLOTS],
                                   big[:, bass.ds(both + half * 384, 384)], start=False, stop=True)
                    mm.then_inc(sem("expert_in_mm"), 1)

            def hid_turn(s, p):
                pe.wait_ge(sem("hid"), 2 * (s + 1))
                at_least(pe, sem("hidT"), 2 * s)
                for c in range(6):
                    mm = pe.transpose(bank[3 + c // 3][:, (c % 3) * SLOTS:(c % 3 + 1) * SLOTS],
                                      hid[:, c * 128:(c + 1) * 128], ident)
                    if c % 3 == 2:
                        mm.then_inc(sem("hid_turned"), 1)

            def expert_out(s, p):
                own = pe.value_load(picks[0:1, bass.ds(s, 1)], min_val=0, max_val=7 * PAIR + BLOCK)
                pe.wait_ge(sem("hidT"), 2 * (s + 1))
                at_least(pe, sem("y_slots"), s)
                for c in range(6):
                    mm = pe.matmul(bank[5][:, 0:DIM], hidT[:, c * SLOTS:(c + 1) * SLOTS],
                                   big[:, bass.ds(own + (FF + c * DIM), DIM)],
                                   start=(c == 0), stop=(c == 5))
                mm.then_inc(sem("expert_out_mm"), 1)

            slot_pipeline(pe, [(rows_turn, 0), (hid_turn, 2), (expert_in, 1), (expert_out, 2)])

        @block.scalar
        def _(act):
            def by_chunk(a):
                return a.rearrange("p (c n) -> p c n", n=ROWS)

            def turned16(n):
                return bank16[0][:, 0:n * PITCH16].rearrange("p (c n) -> p c n", n=PITCH16)[:, :, 0:ROWS]

            def copy(out_, in_):
                return act.activation(out_, in_, ACT.Copy)

            act.wait_ge(sem("emb_mm"), 1)
            copy(w_emb, bank[7][0:MELS, 0:DIM]).then_inc(sem("w_emb"), 1)

            def frame_copy(t):
                act.wait_ge(sem("frame_turned"), t + 1)
                at_least(act, sem("spectrum_mm"), t)
                copy(frameT, bank[0][0:FRAME, 0:ROWS]).then_inc(sem("frameT"), 1)

            def square(t):
                act.wait_ge(sem("spectrum_mm"), t + 1)
                at_least(act, sem("mel_mm"), t)
                act.activation(power, bank[1][0:2 * BINS, 0:ROWS], ACT.Square)\
                    .then_inc(sem("power"), 1)

            def log(t):
                act.wait_ge(sem("mel_mm"), t + 1)
                at_least(act, sem("embed_mm"), t)
                act.activation(logmel, bank[2][0:MELS, 0:ROWS], ACT.Ln, bias=C("eps6", MELS))\
                    .then_inc(sem("logmel"), 1)

            def hnT_copy(t):
                act.wait_ge(sem("hn_turned"), t + 1)
                at_least(act, sem("qkv_mm"), t)
                copy(hnT, bank[4][0:KC, 0:2 * ROWS].rearrange("p (c n) -> p c n", c=2))\
                    .then_inc(sem("hnT"), 1)

            def qkv_copy(t):
                act.wait_ge(sem("qkv_mm"), t + 1)
                for half in range(2):
                    copy(tile_of(qkv, t)[:, half * 288:(half + 1) * 288],
                         bank[5 + half][0:ROWS, 0:288]).then_inc(sem("qkv"), 1)

            pipeline(act, [(frame_copy, 0), (log, 1), (hnT_copy, 2), (square, 0), (qkv_copy, 2)], NT)

            def qkT0_copy(t):
                act.wait_ge(sem("qk_turned"), t + 1)
                at_least(act, sem("scores0_mm"), 4 * t)
                copy(by_chunk(qkT0), turned16(6)).then_inc(sem("qkT0"), 1)

            def abs_sum(t):
                act.wait_ge(sem("scores0"), 4 * (t + 1))
                at_least(act, sem("abs0"), t)
                col = abs0[:, t:t + 1] if isinstance(t, int) else abs0[:, bass.ds(t, 1)]
                act.activation(junk16, tile_of(scores0, t), ACT.Abs, accum_out=col)\
                    .then_inc(sem("abs0"), 1)

            pipeline(act, [(qkT0_copy, 0), (abs_sum, 1)], NT)

            def x2T_copy(t):
                act.wait_ge(sem("x2_turned"), t + 1)
                at_least(act, sem("v1_mm"), t)
                copy(x2T, bank[1][0:KC, 0:2 * ROWS].rearrange("p (c n) -> p c n", c=2))\
                    .then_inc(sem("x2T"), 1)

            def log_var(t):
                act.wait_ge(sem("var64"), t + 1)
                act.activation(logv[:, :], var64[:, :], ACT.Ln,
                               scale=1.0 / (HEADS - 1), accum_out=small[0:ROWS, 40:41])\
                    .then_inc(sem("logvar"), 1)

            def qkT1_copy(t):
                at_least(act, sem("scores1_mm"), 3 * t)
                for b in range(3):
                    act.wait_ge(sem("qk1_mm"), 3 * t + b + 1)
                    copy(qkT1[:, b * 500:(b + 1) * 500], bank[5 + b][:, 0:500])\
                        .then_inc(sem("qkT1"), 1)

            def xqT_copy(t):
                act.wait_ge(sem("xq_turned"), t + 1)
                at_least(act, sem("ffn_in_mm"), t)
                copy(by_chunk(xqT), turned16(2)[0:KC]).then_inc(sem("xqT"), 1)

            def outT_copy(t):
                act.wait_ge(sem("gated_turned"), t + 1)
                at_least(act, sem("project1_mm"), t)
                copy(outT[:, 0:375], bank[3][:, 0:375])
                copy(outT[:, 375:750], bank[4][:, 0:375]).then_inc(sem("outT"), 1)

            def gate_sigmoid(t):
                link = chain(act, "sigmoid_step", t, 2)
                act.wait_ge(sem("ffn_in_mm"), t + 1)
                act.wait_ge(sem("xq"), t + 1)
                at_least(act, sem("yq"), t)
                link(act.activation(egate, bank[4][0:ROWS, :], ACT.Exp, scale=small[0:ROWS, 12:13]))
                act.activation(yz, bank[3][0:ROWS, :], ACT.Copy, scale=small[0:ROWS, 13:14])\
                    .then_inc(sem("up"), 1)
                link(act.activation(egate, egate, ACT.Ln, bias=C("ones", ROWS)[:, 0:1]))
                act.activation(egate, egate, ACT.Exp, scale=-1.0).then_inc(sem("egate"), 1)

            def y_square(t):
                act.wait_ge(sem("y"), t + 1)
                act.activation(egate, ug, ACT.Square, accum_out=small[0:ROWS, 41:42])\
                    .then_inc(sem("ysum"), 1)

            def probsT_copy(t):
                at_least(act, sem("pv1_mm"), t)
                for b in range(3):
                    act.wait_ge(sem("probs_turned"), 3 * t + b + 1)
                    copy(probsT[:, b * 500:(b + 1) * 500], bank[5 + b][0:ROWS, 0:500])\
                        .then_inc(sem("probsT"), 1)

            def nT_copy(t):
                act.wait_ge(sem("normed_turned"), t + 1)
                at_least(act, sem("router_mm"), t)
                copy(nT, bank[1][0:KC, 0:2 * ROWS]).then_inc(sem("nT"), 1)

            def vx_copy(t):
                act.wait_ge(sem("v1_mm"), t + 1)
                at_least(act, sem("pv1_mm"), t)
                for half in range(2):
                    ins = copy(vx[:, half * 6:half * 6 + 6, 0:D1],
                               bank[3 + half][0:ROWS, 0:384].rearrange("p (h d) -> p h d", d=D1))
                ins.then_inc(sem("vx"), 1)

            def dev_square(t):
                act.wait_ge(sem("dev"), t + 1)
                act.activation(dev, dev, ACT.Square).then_inc(sem("sq"), 1)

            def router_exp(t):
                act.wait_ge(sem("logits"), t + 1)
                act.activation(small[0:ROWS, 44:60], tile_of(logits, t), ACT.Exp,
                               bias=small[0:ROWS, 43:44], accum_out=small[0:ROWS, 42:43])\
                    .then_inc(sem("router_exp"), 1)

            def yqT_copy(t):
                act.wait_ge(sem("yq_turned"), t + 1)
                at_least(act, sem("ffn_out_mm"), t)
                copy(by_chunk(yqT), turned16(4)).then_inc(sem("yqT"), 1)

            def softmax_exp(t):
                at_least(act, sem("probs_turned"), 3 * t)
                for n in range(HEADS):
                    if n % 4 == 0:
                        act.wait_ge(sem("rowmax"), 3 * t + n // 4 + 1)
                    ins = act.activation(probs[:, n * ROWS:(n + 1) * ROWS],
                                         bank[5 + n // 4][0:ROWS, (n % 4) * ROWS:(n % 4 + 1) * ROWS],
                                         ACT.Exp, bias=nmax[:, n:n + 1], scale=D1 ** -0.5)
                ins.then_inc(sem("probs"), 1)

            act.preload_act_table_set("natural_log_exp_and_others")
            pipeline(act, [(x2T_copy, 1), (dev_square, 3), (qkT1_copy, 1), (xqT_copy, 0),
                           (log_var, 3), (probsT_copy, 2), (gate_sigmoid, 0), (nT_copy, 4),
                           (outT_copy, 3), (y_square, 0), (router_exp, 4), (yqT_copy, 0),
                           (softmax_exp, 1), (vx_copy, 1)], NT)

            def hid_relu(s, p):
                at_least(act, sem("hid_turned"), 2 * s)
                for half in range(2):
                    act.wait_ge(sem("expert_in_mm"), 2 * s + half + 1)
                    act.activation(hid[:, half * 384:(half + 1) * 384], bank[1 + half][:, 0:384],
                                   ACT.Relu).then_inc(sem("hid"), 1)

            slot_pipeline(act, [(hid_relu, 1)])

        @block.vector
        def _(v):
            v.wait_ge(sem("in_const"), 16)
            for dst, src in ((ident16, "ident"), (tri16, "tri"), (ones16, "ones")):
                v.tensor_copy(dst[:, :], C(src)).then_inc(sem("ident16"), 1)
            v.tensor_copy(same16[:, :], C("same", ROWS)).then_inc(sem("ident16"), 1)
            v.tensor_copy(other16[:, :], C("other", ROWS)).then_inc(sem("ident16"), 1)
            v.memset(qk_pad, 0.0).then_inc(sem("pads"), 1)
            v.wait_ge(sem("in_wq0"), 16)
            v.tensor_reduce(COLSUM[0:KC, 0:1], wq0, AX.XY, ALU.add, apply_absolute_value=True)\
                .then_inc(sem("colsum"), 1)
            v.wait_ge(sem("in_ffn"), 32)
            v.tensor_reduce(COLSUM[0:KC, 1:2], win_raw, AX.XY, ALU.add, apply_absolute_value=True)\
                .then_inc(sem("colsum"), 1)
            v.tensor_reduce(COLSUM[:, 2:3], wout_raw, AX.XY, ALU.add, apply_absolute_value=True)\
                .then_inc(sem("colsum"), 1)
            link = chain(v, "w_step")
            v.wait_ge(sem("wsum_mm"), 1)
            link(v.tensor_scalar(S_W, bank[6][:, 0:1], 1.0 / (3 * DIM * DIM), 1e-5, ALU.mult, ALU.add))
            link(v.reciprocal(R_W[:, 2:3], S_W))
            link(v.tensor_scalar(wq0, wq0, R_W[0:KC, 2:3], ROUND, ALU.mult, ALU.add))
            link(v.tensor_scalar(wq0, wq0, ROUND, 1.0, ALU.subtract, ALU.min))
            v.tensor_scalar(wq0, wq0, -1.0, None, ALU.max).then_inc(sem("wq0_ternary"), 1)

            v.wait_ge(sem("in_vec"), 80)
            mv = small[0:ROWS, 0:2]

            def statistics(link, src):
                hold(v)
                link(v.bn_stats(stats6[:, :], src))
                hold(v)
                link(v.bn_aggr(mv, stats6[:, :]))

            def rsqrt(name, t):
                v.wait_ge(sem(name + "_rsqrt"), t + 1)

            def embed_norm(t):
                link = chain(v, "embed_step", t, 2)
                v.wait_ge(sem("embed_mm"), t + 1)
                v.tensor_tensor(tile_of(h, t), bank[3][0:ROWS, 0:DIM], bprojb[:, :], ALU.add)\
                    .then_inc(sem("h0"), 1)
                v.wait_ge(sem("h0"), t + 1)
                at_least(v, sem("hn_turned"), t)
                statistics(link, tile_of(h, t))
                v.tensor_scalar(small[0:ROWS, 24:25], mv[:, 1:2], 1e-5, None, ALU.add)\
                    .then_inc(sem("embed_var"), 1)
                rsqrt("embed", t)
                v.tensor_scalar(hn, tile_of(h, t), mv[:, 0:1], small[0:ROWS, 25:26],
                                ALU.subtract, ALU.mult).then_inc(sem("hn"), 1)

            def l1_sums(t):
                v.wait_ge(sem("qkv"), 2 * (t + 1))
                hold(v)
                v.tensor_reduce(tile_of(l1sum, t), tile_of(qkv, t).rearrange("p (g d) -> p g d", d=D0),
                                AX.X, ALU.add, apply_absolute_value=True).then_inc(sem("l1sum"), 1)

            pipeline(v, [(embed_norm, 1), (l1_sums, 2)], NT)

            v.wait_ge(sem("l1sum"), NT)
            sums = l1sum.rearrange("p t n -> p (t n)")
            link(v.tensor_scalar(sums, sums, S_W[0:ROWS, :], None, ALU.mult))
            link(v.tensor_scalar(l1unit, sums, 1e-5, None, ALU.add))
            link(v.reciprocal(l1inv, l1unit))
            link(v.tensor_tensor(l1ratio, sums, l1inv, ALU.mult))
            by_kind = l1ratio.rearrange("p (t g n) -> p g t n", t=NT, g=3)
            v.tensor_reduce(PART1[0:ROWS, :], by_kind[:, :, 0:NT - 1, :], AX.XY, ALU.add)\
                .then_inc(sem("l1_parts"), 1)
            v.tensor_reduce(PART2[0:ROWS, :], by_kind[:, :, NT - 1, :], AX.X, ALU.add)\
                .then_inc(sem("l1_parts"), 1)
            v.wait_ge(sem("l1_mm"), 1)
            link(v.tensor_scalar(S_QKV, bank[7][:, 8:11], 1.0 / (TOKENS * DIM), 1e-5, ALU.mult, ALU.add))
            link(v.reciprocal(R_QKV, S_QKV))
            link(v.tensor_scalar(l1inv, l1inv, S_W[0:ROWS, :], None, ALU.mult))
            link(v.tensor_tensor(
                l1unit.rearrange("p (t g n) -> p t g n", t=NT, g=3),
                l1inv.rearrange("p (t g n) -> p t g n", t=NT, g=3),
                R_QKV[0:ROWS, :].unsqueeze(1).unsqueeze(3).to_broadcast([ROWS, NT, 3, HEADS]),
                ALU.mult))
            unit3 = l1unit.rearrange("p (t n) -> p t n", t=NT)

            def ternary(t):
                link = chain(v, "ternary_step", t, 3)
                link(v.tensor_tensor(
                    unit.rearrange("p (g d) -> p g d", d=D0),
                    tile_of(qkv, t).rearrange("p (g d) -> p g d", d=D0),
                    tile_of(unit3, t).unsqueeze(2).to_broadcast([ROWS, 3 * HEADS, D0]), ALU.mult))
                link(v.tensor_scalar(whole, unit, ROUND, ROUND, ALU.add, ALU.subtract))
                at_least(v, sem("qk_turned"), t)
                v.tensor_scalar(qk_pad.rearrange("p (g w) -> p g w", w=32)[:, :, 0:D0],
                                whole[:, 0:2 * DIM].rearrange("p (g d) -> p g d", d=D0),
                                1.0, -1.0, ALU.min, ALU.max).then_inc(sem("qk_ternary"), 1)
                link(v.tensor_scalar(tile_of(v16, t), whole[:, 2 * DIM:3 * DIM], 1.0, -1.0,
                                     ALU.min, ALU.max))
                v.tensor_scalar(tile_of(nv16, t), tile_of(v16, t), -1.0, None, ALU.mult)\
                    .then_inc(sem("values16"), 1)

            def mask0(t):
                for r in range(4):
                    v.wait_ge(sem("scores0_mm"), 4 * t + r + 1)
                    v.tensor_tensor(tile_of(scores0, t)[:, r * 375:(r + 1) * 375]
                                    .rearrange("p (h n) -> p h n", h=3),
                                    bank[1 + r][0:ROWS, 0:375].rearrange("p (h n) -> p h n", h=3),
                                    same16[:, :].unsqueeze(1).to_broadcast([ROWS, 3, ROWS]),
                                    ALU.mult).then_inc(sem("scores0"), 1)

            v.wait_ge(sem("pads"), 1)
            pipeline(v, [(ternary, 0), (mask0, 1)], NT)

            v.wait_ge(sem("wsum_mm"), 2)
            link(v.tensor_scalar(S_IN, bank[7][:, 0:1], 1.0 / (2 * HID0 * DIM), 1e-5, ALU.mult, ALU.max))
            link(v.tensor_scalar(S_OUT, bank[7][:, 1:2], 1.0 / (HID0 * DIM), 1e-5, ALU.mult, ALU.max))
            link(v.reciprocal(R_W[:, 0:2], scal[:, 1:3]))
            link2 = chain(v, "w2_step")
            link2(v.tensor_scalar(win_raw, win_raw, R_W[0:KC, 0:1], ROUND, ALU.mult, ALU.add))
            link2(v.tensor_scalar(win_raw, win_raw, ROUND, 1.0, ALU.subtract, ALU.min))
            v.tensor_scalar(win16[:, :, :], win_raw, -1.0, None, ALU.max).then_inc(sem("win_ternary"), 1)
            link2(v.tensor_scalar(wout_raw, wout_raw, R_W[:, 1:2], ROUND, ALU.mult, ALU.add))
            link2(v.tensor_scalar(wout_raw, wout_raw, ROUND, 1.0, ALU.subtract, ALU.min))
            v.tensor_scalar(wout16[:, :, :], wout_raw, -1.0, None, ALU.max).then_inc(sem("win_ternary"), 1)

            v.wait_ge(sem("abs0_mm"), 1)
            link2(v.tensor_reduce(INT_SUM, bank[5][:, 0:NT], AX.X, ALU.add))
            link2(v.scalar_tensor_tensor(GAIN, S_QKV[:, 0:1], D0 ** -0.5, S_QKV[:, 1:2], ALU.mult, ALU.mult))
            link2(v.tensor_tensor(S_A, INT_SUM, GAIN, ALU.mult))
            link2(v.tensor_scalar(S_A, S_A, 1.0 / (CLIPS * HEADS * SEQ * SEQ), 1e-5, ALU.mult, ALU.add))
            link2(v.reciprocal(IGAIN, GAIN))
            link2(v.scalar_tensor_tensor(T_HI, S_A, 0.5, IGAIN, ALU.mult, ALU.mult))
            link2(v.tensor_scalar(T_LO, T_HI, -1.0, None, ALU.mult))
            link2(v.tensor_tensor(FAC0, S_A, S_QKV[:, 2:3], ALU.mult))

            def thresholds(half):
                def stage(t):
                    at_least(v, sem("pv0_mm"), 2 * t - 1 + half)
                    s = tile_of(scores0, t)[:, half * WIDE // 2:(half + 1) * WIDE // 2]
                    v.tensor_scalar(above[half], s, T_HI[0:ROWS, :], None, ALU.is_gt)
                    v.tensor_scalar(below[half], s, T_LO[0:ROWS, :], None, ALU.is_lt)\
                        .then_inc(sem("above_below"), 1)
                return stage

            def add_attn0(half):
                def stage(t):
                    v.wait_ge(sem("pv0_mm"), 2 * t + half + 1)
                    heads = lambda a: a.rearrange("p (b n) -> p b n", b=3)[:, :, 32 * half:32 * half + 32]
                    v.scalar_tensor_tensor(heads(tile_of(h, t)), heads(bank[6 * half][0:ROWS, 0:DIM]),
                                           FAC0[0:ROWS, :], heads(tile_of(h, t)),
                                           ALU.mult, ALU.add).then_inc(sem("h1"), 1)
                return stage

            pipeline(v, [(thresholds(0), 0), (add_attn0(0), 1), (thresholds(1), 0),
                         (add_attn0(1), 1)], NT)

            v.memset(vx[:, :, D1:D1 + 1], 1.0).then_inc(sem("vx_ones"), 1)

            def quantise(t):
                link = chain(v, "quant_step", t, 7)
                s = lambda a: small[0:ROWS, a:a + 1]
                v.wait_ge(sem("h1"), 2 * (t + 1))
                x = tile_of(h, t)
                statistics(link, x)
                v.tensor_scalar(s(26), s(1), 1 + 1e-6, 1e-11, ALU.mult, ALU.add)\
                    .then_inc(sem("quant_var"), 1)
                link(v.scalar_tensor_tensor(xz, x, s(0), ginb[:, :], ALU.subtract, ALU.mult))
                link(v.tensor_reduce(s(5), xz, AX.X, ALU.max, apply_absolute_value=True))
                rsqrt("quant", t)
                link(v.tensor_tensor(s(7), s(5), s(27), ALU.mult))
                link(v.tensor_scalar(s(8), s(7), 1e-5, 1.0 / 127, ALU.max, ALU.mult))
                link(v.reciprocal(s(9), s(8)))
                link2 = chain(v, "quant_step2", t, 5)
                link2(v.tensor_tensor(s(10), s(27), s(9), ALU.mult))
                link2(v.tensor_tensor(s(11), s(8), S_IN[0:ROWS, :], ALU.mult))
                link2(v.tensor_tensor(s(13), s(11), s(11), ALU.mult))
                link2(v.tensor_scalar(s(12), s(11), -1.0, None, ALU.mult))
                link2(v.tensor_scalar(xz, xz, s(10), ROUND, ALU.mult, ALU.add))
                at_least(v, sem("xq_turned"), t)
                v.tensor_scalar(xq, xz, ROUND, None, ALU.subtract).then_inc(sem("xq"), 1)

            def silu(t):
                s = lambda a: small[0:ROWS, a:a + 1]
                link = chain(v, "y_step", t, 1)
                v.wait_ge(sem("up"), t + 1)
                v.tensor_tensor(ug, bank[4][0:ROWS, :], yz, ALU.mult).then_inc(sem("hidden_read"), 1)
                v.wait_ge(sem("hidden_read"), t + 1)
                v.wait_ge(sem("egate"), t + 1)
                v.tensor_tensor(ug, ug, egate, ALU.mult).then_inc(sem("y"), 1)
                v.wait_ge(sem("y"), t + 1)
                link(v.tensor_tensor(yz, ug, goutb[:, :], ALU.mult))
                v.tensor_reduce(s(14), yz, AX.X, ALU.max, apply_absolute_value=True)\
                    .then_inc(sem("ymax"), 1)
                v.wait_ge(sem("ysum"), t + 1)
                v.tensor_scalar(s(28), s(41), 1.0 / HID0, 1e-6, ALU.mult, ALU.add)\
                    .then_inc(sem("y_var"), 1)

            def quantise_y(t):
                s = lambda a: small[0:ROWS, a:a + 1]
                link = chain(v, "y_step2", t, 6)
                v.wait_ge(sem("ymax"), t + 1)
                rsqrt("y", t)
                link(v.tensor_tensor(s(17), s(14), s(29), ALU.mult))
                link(v.tensor_scalar(s(18), s(17), 1e-5, 1.0 / 127, ALU.max, ALU.mult))
                link(v.reciprocal(s(19), s(18)))
                link(v.tensor_tensor(s(20), s(19), s(29), ALU.mult))
                link(v.tensor_scalar(yz, yz, s(20), ROUND, ALU.mult, ALU.add))
                at_least(v, sem("yq_turned"), t)
                v.tensor_scalar(yq, yz, ROUND, None, ALU.subtract).then_inc(sem("yq"), 1)
                link(v.tensor_tensor(s(21), s(18), S_OUT[0:ROWS, :], ALU.mult))

            def add_ffn_norm(t):
                link = chain(v, "x2_step", t, 2)
                v.wait_ge(sem("ffn_out_mm"), t + 1)
                v.scalar_tensor_tensor(tile_of(h, t), bank[0][0:ROWS, FFN_OUT:FFN_OUT + DIM], small[0:ROWS, 21:22],
                                       tile_of(h, t), ALU.mult, ALU.add).then_inc(sem("h2"), 1)
                v.wait_ge(sem("h2"), t + 1)
                at_least(v, sem("x2_turned"), t)
                statistics(link, tile_of(h, t))
                v.tensor_scalar(small[0:ROWS, 30:31], mv[:, 1:2], 1e-5, None, ALU.add)\
                    .then_inc(sem("x2_var"), 1)
                rsqrt("x2", t)
                v.tensor_scalar(x2, tile_of(h, t), mv[:, 0:1], small[0:ROWS, 31:32],
                                ALU.subtract, ALU.mult).then_inc(sem("x2"), 1)

            def row_max(t):
                at_least(v, sem("probs"), t)
                for b in range(3):
                    link = chain(v, f"max_step{b}", t, 1)
                    v.wait_ge(sem("scores1_mm"), 3 * t + b + 1)
                    hold(v)
                    link(v.tensor_reduce(rowmax[:, 4 * b:4 * b + 4], bank[5 + b][0:ROWS, 0:500]
                                         .rearrange("p (h n) -> p h n", h=4), AX.X, ALU.max))
                    v.tensor_scalar(nmax[:, 4 * b:4 * b + 4], rowmax[:, 4 * b:4 * b + 4],
                                    -(D1 ** -0.5), None, ALU.mult).then_inc(sem("rowmax"), 1)

            def product(t):
                link = chain(v, "prod_step", t, 1)
                v.wait_ge(sem("pv1_mm"), t + 1)
                prod3 = prod.rearrange("p (h d) -> p h d", h=HEADS)
                pv = [bank[3 + i][0:ROWS, 0:390].rearrange("p (h d) -> p h d", d=D1 + 1) for i in range(2)]
                v.reciprocal(rsum[:, 0:6], pv[0][:, :, D1:D1 + 1].rearrange("p h a -> p (h a)"))
                link(v.reciprocal(rsum[:, 6:12], pv[1][:, :, D1:D1 + 1].rearrange("p h a -> p (h a)")))
                at_least(v, sem("gated_turned"), t)
                for i in range(2):
                    ins = v.tensor_tensor(
                        prod3[:, 6 * i:6 * i + 6, :], pv[i][:, :, 0:D1],
                        rsum[:, 6 * i:6 * i + 6].unsqueeze(2).to_broadcast([ROWS, 6, D1]), ALU.mult)
                ins.then_inc(sem("prod"), 1)

            def mean_heads(t):
                link = chain(v, "mean_step", t, 1)
                v.wait_ge(sem("prod"), t + 1)
                at_least(v, sem("dev"), t)
                link(v.tensor_reduce(mean64[:, :], prod.rearrange("p (h d) -> p d h", h=HEADS),
                                     AX.X, ALU.add))
                v.tensor_scalar(mean64[:, :], mean64[:, :], 1.0 / HEADS, None, ALU.mult)\
                    .then_inc(sem("mean"), 1)

            def variance(t):
                v.wait_ge(sem("sq"), t + 1)
                v.tensor_reduce(var64[:, :], dev.rearrange("p (h d) -> p d h", h=HEADS),
                                AX.X, ALU.add).then_inc(sem("var64"), 1)
                v.wait_ge(sem("var64"), t + 1)
                v.reciprocal(ivar64[:, :], var64[:, :]).then_inc(sem("ivar"), 1)

            def gate_heads(t):
                link = chain(v, "gate_step", t, 3)
                v.wait_ge(sem("scaled"), t + 1)
                link(v.tensor_reduce(factor[:, :], dev.rearrange("p (h d) -> p h d", h=HEADS),
                                     AX.X, ALU.add))
                v.wait_ge(sem("logvar"), t + 1)
                link(v.tensor_scalar(small[0:ROWS, 22:23], small[0:ROWS, 40:41], -1.0,
                                     -0.5 * D1 * LOG2PI, ALU.mult, ALU.add))
                link(v.tensor_scalar(factor[:, :], factor[:, :], 0.25 * (HEADS - 1),
                                     small[0:ROWS, 22:23], ALU.mult, ALU.add))
                v.tensor_tensor(prod.rearrange("p (h d) -> p h d", h=HEADS),
                                prod.rearrange("p (h d) -> p h d", h=HEADS),
                                factor[:, :].unsqueeze(2).to_broadcast([ROWS, HEADS, D1]),
                                ALU.mult).then_inc(sem("gated"), 1)

            def add_attn1_norm(t):
                link = chain(v, "h3_step", t, 5)
                v.wait_ge(sem("project1_mm"), t + 1)
                at_least(v, sem("row_stored"), 16 * t)
                v.tensor_tensor(h3, bank[2][0:ROWS, 0:DIM], tile_of(h, t), ALU.add)\
                    .then_inc(sem("h3"), 1)
                v.wait_ge(sem("h3"), t + 1)
                link(v.tensor_tensor(h3, h3, boutb[:, :], ALU.add))
                s = lambda a: small[0:ROWS, a:a + 1]
                x3 = tile_of(h, t)
                statistics(link, h3)
                link(v.tensor_scalar(s(33), s(1), 1 + 1e-6, 1e-11, ALU.mult, ALU.add))
                v.tensor_scalar(s(32), s(1), 1e-5, None, ALU.add).then_inc(sem("h3_var"), 1)
                rsqrt("h3", t)
                v.scalar_tensor_tensor(row[:, 0:DIM], h3, s(0), lnwb[:, :], ALU.subtract, ALU.mult)\
                    .then_inc(sem("h3_centred"), 1)
                link(v.tensor_scalar(x3, h3, s(0), s(34), ALU.subtract, ALU.mult))
                v.wait_ge(sem("h3_centred"), t + 1)
                v.tensor_scalar(row[:, 0:DIM], row[:, 0:DIM], s(35), None, ALU.mult)\
                    .then_inc(sem("normed"), 1)
                v.wait_ge(sem("normed"), t + 1)
                v.tensor_copy(row[:, DIM:DIM + 64], row[:, 128:DIM])
                v.tensor_tensor(h3, x3, h3, ALU.add).then_inc(sem("row_dup"), 1)

            def router_max(t):
                v.wait_ge(sem("router_mm"), t + 1)
                link = chain(v, "router_step", t, 2)
                lg = tile_of(logits, t)
                link(v.tensor_copy(lg, bank[1][0:ROWS, 0:EXPERTS]))
                hold(v)
                link(v.tensor_reduce(small[0:ROWS, 23:24], lg, AX.X, ALU.max))
                v.tensor_scalar(small[0:ROWS, 43:44], small[0:ROWS, 23:24], -1.0, None, ALU.mult)\
                    .then_inc(sem("logits"), 1)

            def router_prob(t):
                v.wait_ge(sem("router_exp"), t + 1)
                v.wait_ge(sem("row_dup"), t + 1)
                v.reciprocal(row[:, GATE:GATE + 1], small[0:ROWS, 42:43]).then_inc(sem("row_ready"), 1)

            v.memset(row[:, :], 0.0).then_inc(sem("vx_ones"), 1)
            v.wait_ge(sem("vx_ones"), 2)
            pipeline(v, [(quantise, 0), (variance, 3), (add_attn1_norm, 4), (gate_heads, 3),
                         (silu, 0), (router_max, 4), (quantise_y, 0), (product, 2),
                         (router_prob, 4), (row_max, 1), (add_ffn_norm, 0), (mean_heads, 2)], NT)

            link = chain(v, "route_step")
            v.wait_ge(sem("logits"), NT)
            grid = [ROWS, NT, EXPERTS]
            lg = logits[:, :, :]
            link(v.tensor_reduce(best, lg, AX.X, ALU.max))
            link(v.tensor_tensor(hot, lg, best.unsqueeze(2).to_broadcast(grid), ALU.is_equal))
            link(v.tensor_tensor(hot, hot, C("rev", ROWS).unsqueeze(1).to_broadcast(grid), ALU.mult))
            link(v.tensor_reduce(best, hot, AX.X, ALU.max))
            link(v.tensor_tensor(hot, hot, best.unsqueeze(2).to_broadcast(grid), ALU.is_equal))
            v.tensor_copy(onehot16, hot.rearrange("p t e -> p (t e)")).then_inc(sem("onehot"), 1)
            v.wait_ge(sem("rank_mm"), 1)
            link(v.tensor_copy(cnt, bank[3][:, 0:EXPERTS]))
            link(v.tensor_tensor(cmp13, cnt.unsqueeze(2).to_broadcast([128, EXPERTS, NT]),
                                 C("count").unsqueeze(1).to_broadcast([128, EXPERTS, NT]), ALU.is_gt))
            link(v.tensor_reduce(ntile, cmp13, AX.X, ALU.add))
            link(v.tensor_tensor(cmp16, ntile.unsqueeze(1).to_broadcast([128, EXPERTS, EXPERTS]),
                                 C("below").rearrange("p (a b) -> p a b", a=EXPERTS), ALU.mult))
            link(v.tensor_reduce(base, cmp16, AX.X, ALU.add))
            link(v.tensor_scalar(base128, base, float(SLOTS), None, ALU.mult))
            link(v.tensor_tensor(where, bank[2][0:ROWS, 0:NT * EXPERTS]
                                 .rearrange("p (t e) -> p t e", e=EXPERTS),
                                 base128[0:ROWS, :].unsqueeze(1).to_broadcast(grid), ALU.add))
            link(v.tensor_tensor(where, where, hot, ALU.mult))
            link(v.tensor_reduce(pos, where, AX.X, ALU.add))
            link(v.tensor_copy(pos_i, pos))
            link(v.tensor_scalar(lane_i, pos_i, SLOTS - 1, None, ALU.bitwise_and))
            link(v.tensor_scalar(tile_i, pos_i, 7, None, ALU.logical_shift_right))
            link(v.tensor_copy(lane_f, lane_i))
            link(v.tensor_copy(tile_f, tile_i))
            link(v.tensor_tensor(lane_hot, C("lane", ROWS).unsqueeze(1).to_broadcast([ROWS, NT, 128]),
                                 lane_f.unsqueeze(2).to_broadcast([ROWS, NT, 128]), ALU.is_equal))
            link(v.tensor_tensor(token_at, C("slot", ROWS).unsqueeze(1).to_broadcast([ROWS, NT, NS]),
                                 tile_f.unsqueeze(2).to_broadcast([ROWS, NT, NS]), ALU.is_equal))
            v.tensor_tensor(token_at, token_at, C("token", ROWS).unsqueeze(2)
                            .to_broadcast([ROWS, NT, NS]), ALU.mult).then_inc(sem("lanes"), 1)
            link(v.tensor_tensor(ends, base, ntile, ALU.add))
            link(v.tensor_tensor(cmp28, ends.unsqueeze(1).to_broadcast([128, NS, EXPERTS]),
                                 C("slot").unsqueeze(2).to_broadcast([128, NS, EXPERTS]), ALU.is_le))
            link(v.tensor_reduce(expert, cmp28, AX.X, ALU.add))
            link(v.tensor_scalar(expert, expert, float(EXPERTS - 1), None, ALU.min))
            link(v.tensor_copy(expert_i, expert))
            link(v.tensor_scalar(odd_i, expert_i, 1, None, ALU.bitwise_and))
            link(v.tensor_copy(odd, odd_i))
            link(v.tensor_tensor(pair2, expert, odd, ALU.subtract))
            link(v.tensor_scalar(own_f, pair2, PAIR / 2.0, None, ALU.mult))
            link(v.tensor_scalar(both_f, own_f, float(2 * BLOCK), None, ALU.add))
            link(v.scalar_tensor_tensor(own_f, odd, float(BLOCK), own_f, ALU.mult, ALU.add))
            link(v.tensor_scalar(mine[:, 0:NS], odd, C("side"), None, ALU.is_equal))
            v.tensor_copy(picks[:, 0:NS], own_f)
            v.tensor_copy(picks[:, NS + 1:2 * NS + 1], both_f).then_inc(sem("picks"), 1)
            v.wait_ge(sem("slots_mm"), 1)
            link(v.tensor_copy(slot_f, bank[4][:, 0:NS]))
            link(v.tensor_scalar(empty, slot_f, 0.0, float(4 * TOKENS), ALU.is_equal, ALU.mult))
            link(v.scalar_tensor_tensor(slot_f, slot_f, -1.0, empty, ALU.add, ALU.add))
            for p in range(4):
                v.memset(slot_rows[p], 0.0).then_inc(sem("slots"), 1)
            v.tensor_copy(slot_i, slot_f).then_inc(sem("slots"), 1)

            def rowsT_copy(s, p):
                v.wait_ge(sem("rows_turned"), s + 1)
                at_least(v, sem("expert_in_mm"), 2 * (s - 1))
                v.tensor_copy(rowsT[p % 2][:, 0:SLOTS], bank[0][:, 0:SLOTS]).then_inc(sem("rowsT"), 1)
                m = mine[:, s:s + 1] if isinstance(s, int) else mine[:, bass.ds(s, 1)]
                v.tensor_scalar(rowsT[p % 2][:, SLOTS:2 * SLOTS], bank[0][:, SLOTS:2 * SLOTS], m, None,
                                ALU.mult).then_inc(sem("rowsT"), 1)

            def hidT_copy(s, p):
                at_least(v, sem("expert_out_mm"), s)
                for half in range(2):
                    v.wait_ge(sem("hid_turned"), 2 * s + half + 1)
                    v.tensor_copy(hidT[:, half * 384:(half + 1) * 384], bank[3 + half][:, 0:384])\
                        .then_inc(sem("hidT"), 1)

            def combine(s, p):
                v.wait_ge(sem("expert_out_mm"), s + 1)
                at_least(v, sem(f"y_stored{p % 2}"), 8 * (s - p % 2))
                r = slot_rows[p]
                v.scalar_tensor_tensor(y_out[p % 2], bank[5][:, 0:DIM], r[:, GATE:GATE + 1],
                                       r[:, RES:RES + DIM], ALU.mult, ALU.add)\
                    .then_inc(sem("y_slots"), 1)

            slot_pipeline(v, [(rowsT_copy, 0), (hidT_copy, 2), (combine, 2)])

        @block.gpsimd
        def _(g):
            def powers(name, a, n=1):
                def stage(t):
                    g.wait_ge(sem(name + "_var"), t + 1)
                    g.tensor_tensor(small[0:ROWS, a + n:a + 2 * n], small[0:ROWS, a:a + n],
                                    C("minus_half", ROWS)[:, 0:n], ALU.pow)\
                        .then_inc(sem(name + "_rsqrt"), 1)
                return stage

            g.wait_ge(sem("in_const"), 16)
            pipeline(g, [(powers("embed", 24), 0)], NT)
            prod3 = prod.rearrange("p (h d) -> p h d", h=HEADS)
            dev3 = dev.rearrange("p (h d) -> p h d", h=HEADS)

            def deviation(t):
                g.wait_ge(sem("mean"), t + 1)
                g.tensor_tensor(dev3, prod3, mean64[:, :].unsqueeze(1).to_broadcast([ROWS, HEADS, D1]),
                                ALU.subtract).then_inc(sem("dev"), 1)

            def scale_squares(t):
                g.wait_ge(sem("ivar"), t + 1)
                g.tensor_tensor(dev3, dev3, ivar64[:, :].unsqueeze(1).to_broadcast([ROWS, HEADS, D1]),
                                ALU.mult).then_inc(sem("scaled"), 1)

            pipeline(g, [(powers("quant", 26), 0), (scale_squares, 3), (powers("h3", 32, 2), 4),
                         (powers("y", 28), 0), (powers("x2", 30), 0), (deviation, 2)], NT)

            g.wait_ge(sem("slots"), 5)
            g.wait_ge(sem("row_stored"), 16 * NT)

            def gather(s):
                if s >= 4:
                    g.wait_ge(sem("y_slots"), s - 3)
                g.indirect_dma_start(slot_rows[s % 4], None, rows_dram,
                                     bass.IndirectOffsetOnAxis(ap=slot_i[:, s:s + 1], axis=0),
                                     bounds_check=TOKENS - 1, oob_is_err=False)\
                    .then_inc(sem(f"rows_in{s % 4}"), 16)

            for s in range(4):
                gather(s)
            for s in range(NS):
                if s + 4 < NS:
                    gather(s + 4)
                g.wait_ge(sem("y_slots"), s + 1)
                g.indirect_dma_start(out_rows, bass.IndirectOffsetOnAxis(ap=slot_i[:, s:s + 1], axis=0),
                                     y_out[s % 2], None,
                                     bounds_check=TOKENS - 1, oob_is_err=False)\
                    .then_inc(sem(f"y_stored{s % 2}"), 16)
            for p in range(2):
                g.wait_ge(sem(f"y_stored{p}"), 8 * NS)

        for name, n, steps in chains:
            assert not steps or n[0] == steps, (name, n[0], steps)


def kernel(**inputs):
    import numpy as np
    import concourse.bacc as bacc
    from concourse.bass_utils import run_bass_kernel_spmd

    nc = bacc.Bacc("TRN2", target_bir_lowering=False, num_devices=1)
    arrays, args = {}, []

    def give(name, a):
        a = np.ascontiguousarray(a)
        arrays[name] = a
        args.append(nc.dram_tensor(name, a.shape, mybir.dt.from_np(a.dtype), kind="ExternalInput").ap())

    def chunks(w, rows):
        return w.reshape(-1, rows, w.shape[1]).transpose(1, 0, 2)

    i = {k: np.asarray(v) for k, v in inputs.items()}
    give("in_x", i["x"])
    give("in_consts", constants())
    mel = i["L0_tok_mel_filters"].T
    give("in_melT", np.concatenate([mel, mel], 0))
    give("in_dct", i["L0_tok_dct"])
    give("in_w_proj", i["L0_tok_w_proj"])
    give("in_b_proj", i["L0_tok_b_proj"])
    give("in_w_qkv0", chunks(i["L0_attn_w_qkv"].T, KC))
    give("in_w_in", chunks(i["L0_ffn_w_in"].T, KC))
    give("in_g_in", i["L0_ffn_g_in"])
    give("in_w_out0", chunks(i["L0_ffn_w_out"].T, 128))
    give("in_g_out", i["L0_ffn_g_out"])
    give("in_w_qkv1", chunks(i["L1_attn_w_qkv"], KC))
    give("in_w_out1", chunks(i["L1_attn_w_out"], 128))
    give("in_b_out", i["L1_attn_b_out"])
    give("in_ln_w", i["L1_ffn_ln_w"])
    give("in_w_router", chunks(i["L1_ffn_w_router"], KC))
    wi, wo = i["L1_ffn_wi"], i["L1_ffn_wo"]
    first = wi[:, 0:128, :]
    last = wi[:, 128:DIM, :].reshape(EXPERTS // 2, 128, FF)
    down = wo.reshape(EXPERTS, 6, 128, DIM).transpose(0, 2, 1, 3).reshape(EXPERTS, 128, 6 * DIM)
    give("in_experts", np.concatenate([first[0::2], down[0::2], first[1::2], down[1::2], last], 2))
    out = nc.dram_tensor("out", (CLIPS, SEQ, DIM), F32, kind="ExternalOutput").ap()
    rows_dram = nc.dram_tensor("rows_dram", (NT * ROWS, ROWLEN), F32, kind="Internal").ap()
    build(nc, *args, out, rows_dram)
    r = run_bass_kernel_spmd(nc, [arrays], core_ids=[0])
    return r.results[0]["out"]
```

```python
import concourse.bass as bass
from concourse import mybir
from contextlib import ExitStack

F32, BF16, I32 = mybir.dt.float32, mybir.dt.bfloat16, mybir.dt.int32
U32 = mybir.dt.uint32
ALU = mybir.AluOpType
ACT = mybir.ActivationFunctionType
AX = mybir.AxisListType

CLIPS, SAMPLES, FRAME, HOP = 64, 4000, 100, 160
SEQ, DIM = 25, 192
TOKENS = CLIPS * SEQ
ROWS = 5 * SEQ
NT = -(-TOKENS // ROWS)
LAST = TOKENS - (NT - 1) * ROWS
BINS, MELS, MFCC = FRAME // 2 + 1, 40, 13
KC = DIM // 2
HEADS = 12
D0 = DIM // HEADS
D1 = 64
INNER = HEADS * D1
HID0 = 512
FF, EXPERTS, SLOTS = 768, 16, 128
NS = (TOKENS - EXPERTS) // SLOTS + EXPERTS
RK = NT - 1
ROWLEN = 450
RES, GATE = 256, 448
BLOCK = FF + 6 * DIM
PAIR = 2 * BLOCK + FF
PITCH16 = ROWS + 1
WIDE = HEADS * ROWS
ORDER1 = (0, 2, 4, 6, 1, 3, 5, 7, 8, 10, 9, 11)
ROUND = 12582912.0
FFN_OUT = 256
ROOT_2PI = 2.5066282746310002
NEG = -1.0e30

CONST = {}
_at = 0
for _name, _n in (("ident", 128), ("tri", 128), ("ones", 128), ("same", ROWS), ("other", ROWS),
                  ("rev", EXPERTS), ("count", NT), ("below", EXPERTS * EXPERTS), ("slot", NS),
                  ("tile", NT), ("row", 1), ("lane", 128), ("side", 1), ("eps6", 1), ("minus_half", 2), ("dft", 2 * BINS)):
    CONST[_name] = (_at, _at + _n)
    _at += _n
CONSTS = _at


def constants():
    import numpy as np
    c = np.zeros((128, CONSTS), np.float64)

    def put(name, value, rows=128):
        a, b = CONST[name]
        c[:rows, a:b] = value

    p = np.arange(128)[:, None]
    j = np.arange(128)[None, :]
    put("ident", p == j)
    put("tri", p < j)
    put("ones", 1.0)
    q = np.arange(ROWS)[None, :]
    put("same", (p // SEQ) == (q // SEQ))
    put("other", np.where((p // SEQ) == (q // SEQ), 0.0, NEG))
    put("rev", EXPERTS - np.arange(EXPERTS)[None, :])
    put("count", SLOTS * np.arange(NT)[None, :])
    e = np.arange(EXPERTS)
    put("below", (e[None, :] < e[:, None]).reshape(1, -1))
    put("slot", np.arange(NS)[None, :])
    put("tile", np.arange(NT)[None, :])
    put("row", p + 1)
    put("lane", j)
    put("side", p >= 64)
    put("eps6", 1e-6)
    put("minus_half", -0.5)
    n = np.arange(FRAME)[:, None]
    k = np.arange(BINS)[None, :]
    window = 0.54 - 0.46 * np.cos(2 * np.pi * n / (FRAME - 1))
    put("dft", np.concatenate([window * np.cos(2 * np.pi * n * k / FRAME),
                               -window * np.sin(2 * np.pi * n * k / FRAME)], 1), FRAME)
    return c.astype(np.float32)


def at_least(eng, sem, n):
    if not (isinstance(n, int) and n <= 0):
        eng.wait_ge(sem, n)


def capped(n, top=NT):
    return min(n, top) if isinstance(n, int) else n


def pipeline(eng, stages, tiles):
    top = max(lag for _, lag in stages)

    def step(s):
        for stage, lag in stages:
            if not isinstance(s, int) or 0 <= s - lag < tiles:
                stage(s - lag)

    for s in range(top + 1):
        step(s)
    with eng.Fori(top + 1, tiles) as s:
        step(s)
    for s in range(tiles, tiles + top):
        step(s)


def tile_of(t3, t):
    if isinstance(t, int):
        return t3[:, t, :]
    return t3[:, bass.ds(t, 1), :].rearrange("p a n -> p (a n)")


def build(nc, x, consts, melT, dct, w_proj, b_proj, w_qkv0, w_in, g_in, w_out0, g_out,
          w_qkv1, w_out1, b_out, ln_w, w_router, experts, out, rows_dram):
    ctx = ExitStack()
    with ctx:
        def sb(name, shape, dt=F32):
            return ctx.enter_context(nc.sbuf_tensor(name, shape, dt))

        sems = {}

        def sem(name):
            if name not in sems:
                sems[name] = ctx.enter_context(nc.semaphore(name))
            return sems[name]

        bank = [ctx.enter_context(nc.psum_tensor("bank0", [128, 512], F32))]
        bank1234 = ctx.enter_context(nc.psum_tensor("bank1234", [128, 4, 512], F32))
        bank += [bank1234[:, i, :] for i in range(4)]
        bank567 = ctx.enter_context(nc.psum_tensor("bank567", [128, 3, 512], F32))
        bank += [bank567[:, i, :] for i in range(3)]
        bank16 = [b[:, :].bitcast(BF16) for b in bank]

        cst = sb("cst", [128, CONSTS])

        def C(name, rows=128):
            a, b = CONST[name]
            return cst[0:rows, a:b]

        h = sb("h", [ROWS, NT, DIM])
        ident16 = sb("ident16", [128, 128], BF16)
        tri16 = sb("tri16", [128, 128], BF16)
        ones16 = sb("ones16", [128, 128], BF16)
        same16 = sb("same16", [ROWS, ROWS], BF16)
        other16 = sb("other16", [ROWS, ROWS], BF16)
        bprojb = sb("bprojb", [ROWS, DIM])
        ginb = sb("ginb", [ROWS, DIM])
        goutb = sb("goutb", [ROWS, HID0])
        boutb = sb("boutb", [ROWS, DIM])
        lnwb = sb("lnwb", [ROWS, DIM])
        router = sb("router", [KC, 2, EXPERTS])
        win16 = sb("win16", [KC, 2, 2 * HID0], BF16)
        wout16 = sb("wout16", [128, 4, DIM], BF16)
        w1_mem = sb("w1_mem", [128, 2 * 3 * INNER])
        w1 = w1_mem[0:KC, :].rearrange("p (c n) -> p c n", c=2)
        wo1 = sb("wo1", [128, 6, DIM])
        scal = sb("scal", [128, 32])
        small = sb("small", [128, 64])
        logits = sb("logits", [ROWS, NT, EXPERTS])
        big = sb("big", [128, 8 * PAIR])

        def carve(start):
            at = [start]

            def take(n, dt=F32, rows=128):
                words = n if dt is not BF16 else -(-n // 2)
                a = big[0:rows, at[0]:at[0] + words]
                at[0] += words
                assert at[0] <= 8 * PAIR
                return a if dt is F32 else a.bitcast(dt)[:, 0:n]
            return take, at

        EARLY = 6 * PAIR
        take, early_end = carve(0)
        qkv = take(NT * 3 * DIM, rows=ROWS).rearrange("p (t n) -> p t n", t=NT)
        scores0 = take(NT * WIDE, BF16, ROWS).rearrange("p (t n) -> p t n", t=NT)
        v16 = take(NT * DIM, BF16, ROWS).rearrange("p (t n) -> p t n", t=NT)
        signs = [take(WIDE // 2, BF16, ROWS) for _ in range(2)]
        below = [take(WIDE // 2, BF16, ROWS) for _ in range(2)]
        melT_sb = take(MELS, rows=2 * BINS)
        dct_sb = take(MELS, rows=MFCC)
        wproj_sb = take(DIM, rows=MFCC)
        w_emb = take(DIM, rows=MELS)
        wq0 = take(2 * 3 * DIM, rows=KC).rearrange("p (c n) -> p c n", c=2)
        frame = take(FRAME, rows=ROWS)
        frameT = take(ROWS, rows=FRAME)
        power = take(ROWS, rows=2 * BINS)
        logmel = take(ROWS, rows=MELS)
        hn = take(DIM, rows=ROWS)
        hnT = take(2 * ROWS, rows=KC).rearrange("p (c n) -> p c n", c=2)
        assert early_end[0] <= EARLY, early_end[0]
        take, _ = carve(EARLY)
        win_raw = take(2 * 2 * HID0, rows=KC).rearrange("p (c n) -> p c n", c=2)
        wout_raw = take(4 * DIM).rearrange("p (c n) -> p c n", c=4)
        l1sum = take(NT * 3 * HEADS, rows=ROWS).rearrange("p (t n) -> p t n", t=NT)
        l1inv = take(NT * 3 * HEADS, rows=ROWS)
        l1ratio = take(NT * 3 * HEADS, rows=ROWS)
        l1unit = take(NT * 3 * HEADS, rows=ROWS)
        unit = take(3 * DIM, rows=ROWS)
        whole = take(3 * DIM, rows=ROWS)
        qk_pad = take(2 * HEADS * 32, BF16, ROWS)
        qkT0 = take(6 * ROWS, BF16)
        junk16 = take(WIDE, BF16, ROWS)
        abs0 = take(NT, rows=ROWS)

        take, _ = carve(EARLY)
        xq = take(DIM, BF16, ROWS)
        xz = take(DIM, rows=ROWS)
        xqT = take(2 * ROWS, BF16, KC)
        egate = take(HID0, rows=ROWS)
        ug = take(HID0, rows=ROWS)
        yz = take(HID0, rows=ROWS)
        yq = take(HID0, BF16, ROWS)
        yqT = take(4 * ROWS, BF16)
        x2 = take(DIM, rows=ROWS)
        x2T = take(2 * ROWS, rows=KC).rearrange("p (c n) -> p c n", c=2)
        qkT1 = take(12 * ROWS)
        vx = take(HEADS * (D1 + 1), rows=ROWS).rearrange("p (h d) -> p h d", h=HEADS)
        probs = take(WIDE, rows=ROWS)
        probsT = take(WIDE, rows=ROWS)
        outT = take(6 * ROWS)
        nT = take(2 * ROWS, rows=KC)
        row = sb("row", [ROWS, ROWLEN])
        h3 = row[:, RES:RES + DIM]
        heads_mem = sb("heads_mem", [128, NT * 128])
        prod = heads_mem[0:ROWS, 0:INNER]
        dev = heads_mem[0:ROWS, INNER:2 * INNER]
        mean64 = sb("mean64", [ROWS, D1])
        var64 = sb("var64", [ROWS, D1])
        ivar64 = sb("ivar64", [ROWS, D1])
        logv = sb("logv", [ROWS, D1])
        stats6 = sb("stats6", [ROWS, 6])
        rowmax, nmax, rsum, factor = (sb(n, [ROWS, HEADS]) for n in ("rowmax", "nmax", "rsum", "factor"))

        def reuse_of(mem, size):
            spot = [0]

            def take(n, dt=F32, rows=128):
                words = n if dt is not BF16 else -(-n // 2)
                a = mem[0:rows, spot[0]:spot[0] + words]
                spot[0] += words
                assert spot[0] <= size
                return a if dt is F32 else a.bitcast(dt)[:, 0:n]
            return take

        reuse = reuse_of(w1_mem, 6 * INNER)

        slot_rows = [reuse(ROWLEN) for _ in range(4)]
        rowsT = [reuse(2 * SLOTS) for _ in range(2)]
        hid = reuse(FF)
        hidT = reuse(FF)
        y_out = [reuse(DIM) for _ in range(2)]
        token_at = reuse(2 * NT * NS, BF16, ROWS).rearrange("p (a t s) -> p a t s", a=2, t=NT)
        reuse = reuse_of(wo1[:, :, :].rearrange("p c n -> p (c n)"), 6 * DIM)
        onehot16 = reuse((NT + 1) * EXPERTS, BF16, ROWS)
        hot = reuse(NT * EXPERTS, rows=ROWS).rearrange("p (t e) -> p t e", t=NT)
        where = reuse(NT * EXPERTS, rows=ROWS).rearrange("p (t e) -> p t e", t=NT)
        cmp13 = reuse(EXPERTS * NT).rearrange("p (e k) -> p e k", e=EXPERTS)
        cmp16 = reuse(EXPERTS * EXPERTS).rearrange("p (a b) -> p a b", a=EXPERTS)
        lane_hot = heads_mem[0:ROWS, 0:NT * 64].bitcast(BF16).rearrange("p (t l) -> p t l", t=NT)
        cmp28 = sb("cmp28", [128, NS, EXPERTS])[:, :, :]
        best, pos, lane_f, tile_f = (sb(n, [ROWS, NT])[:, :] for n in ("best", "pos", "lane_f", "tile_f"))
        pos_i, lane_i, tile_i = (sb(n, [ROWS, NT], I32)[:, :] for n in ("pos_i", "lane_i", "tile_i"))
        cnt, ntile, base, base128, ends = (sb(n, [128, EXPERTS])[:, :]
                                           for n in ("cnt", "ntile", "base", "base128", "ends"))
        expert, odd, pair2, both_f = (
            sb(n, [128, NS])[:, :] for n in ("expert", "odd", "pair2", "both_f"))
        mine = sb("mine", [128, NS + 4])
        expert_i, odd_i = (sb(n, [128, NS], I32)[:, :] for n in ("expert_i", "odd_i"))
        own_f, late, last_pair, slot_f, empty = (reuse(NS) for _ in range(5))
        slot_i = sb("slot_i", [128, NS], I32)[:, :]
        picks = sb("picks", [128, 3 * NS + 7], I32)[:, :]
        out_rows = out.rearrange("b n c -> (b n) c")

        def slot_pipeline(eng, stages):
            assert NS % 4 == 0

            def step(s, k):
                for stage, lag in stages:
                    if not isinstance(s, int) or 0 <= s - lag < NS:
                        stage(s - lag, (k - lag) % 4)

            for k in range(4):
                step(k, k)
            with eng.Fori(4, NS, 4) as s:
                for k in range(4):
                    step(s + k, k)
            for k in range(max(lag for _, lag in stages)):
                step(NS + k, k)

        block = ctx.enter_context(nc.Block())

        chains = []

        def chain(eng, name, t=0, steps=0):
            n = [0]
            chains.append((name, n, steps))

            def link(ins):
                n[0] += 1
                ins.then_inc(sem(name), 1)
                eng.wait_ge(sem(name), t * steps + n[0] if steps else n[0])
            return link

        def hold(eng):
            eng.sem_inc(sem("held"), 1)

        S_W, S_IN, S_OUT = (scal[:, i:i + 1] for i in (0, 1, 2))
        COLSUM = scal[:, 3:6]
        S_QKV, R_QKV = scal[:, 6:9], scal[:, 9:12]
        PART1, PART2 = scal[:, 12:15], scal[:, 15:18]
        GAIN, INT_SUM, S_A, T_HI, T_LO, FAC0 = (scal[:, i:i + 1] for i in range(18, 24))
        R_W = scal[:, 24:27]
        IGAIN = scal[:, 27:28]

        @block.sync
        def _(sp):
            sp.dma_start(cst[:, :], consts).then_inc(sem("in_const"), 16)
            sp.dma_start(melT_sb, melT).then_inc(sem("in_tok"), 16)
            sp.dma_start(dct_sb, dct).then_inc(sem("in_tok"), 16)
            sp.dma_start(wproj_sb, w_proj).then_inc(sem("in_tok"), 16)
            sp.dma_start(wq0, w_qkv0).then_inc(sem("in_wq0"), 16)
            frames = x.rearrange("b (n s) -> (b n) s", s=HOP)

            def load_frames(t):
                at_least(sp, sem("frame_turned"), t)
                if isinstance(t, int) and t == NT - 1:
                    sp.dma_start(frame[0:LAST, :], frames[t * ROWS:TOKENS, 0:FRAME])\
                        .then_inc(sem("frame_in"), 16)
                else:
                    sp.dma_start(frame, frames[bass.ds(t * ROWS, ROWS), 0:FRAME])\
                        .then_inc(sem("frame_in"), 16)

            load_frames(0)
            for dst, src in ((bprojb, b_proj), (ginb, g_in), (goutb, g_out), (boutb, b_out),
                             (lnwb, ln_w)):
                sp.dma_start(dst[:, :], src.partition_broadcast(ROWS)).then_inc(sem("in_vec"), 16)
            sp.dma_start(win_raw, w_in).then_inc(sem("in_ffn"), 16)
            sp.dma_start(wout_raw, w_out0).then_inc(sem("in_ffn"), 16)
            with sp.Fori(1, NT - 1) as t:
                load_frames(t)
            load_frames(NT - 1)
            sp.dma_start(w1, w_qkv1).then_inc(sem("in_attn1"), 16)
            sp.dma_start(wo1[:, :, :], w_out1).then_inc(sem("in_attn1"), 16)
            sp.dma_start(router[:, :, :], w_router).then_inc(sem("in_attn1"), 16)
            sp.wait_ge(sem("pv0_mm"), 2 * NT)
            for pair in range(6):
                sp.dma_start(big[:, pair * PAIR:(pair + 1) * PAIR], experts[pair, :, :])\
                    .then_inc(sem("in_experts"), 16)

            def store_row(t):
                sp.wait_ge(sem("row_ready"), t + 1)
                sp.dma_start(rows_dram[bass.ds(t * ROWS, ROWS), :], row[:, :])\
                    .then_inc(sem("row_stored"), 16)

            pipeline(sp, [(store_row, 0)], NT)
            sp.wait_ge(sem("row_ready"), NT)
            sp.sem_inc(sem("late_experts"), 1)
            for pair in (6, 7):
                if pair == 7:
                    sp.wait_ge(sem("late_experts"), 1 + 16)
                sp.dma_start(big[:, pair * PAIR:(pair + 1) * PAIR], experts[pair, :, :])\
                    .then_inc(sem("late_experts"), 16)

        @block.tensor
        def _(pe):
            ident = C("ident")

            pe.wait_ge(sem("in_const"), 16)
            pe.wait_ge(sem("in_tok"), 48)
            pe.matmul(bank[7][0:MELS, 0:DIM], dct_sb, wproj_sb, start=True, stop=True)\
                .then_inc(sem("emb_mm"), 1)
            pe.wait_ge(sem("colsum"), 1)
            pe.matmul(bank[6][:, 0:1], C("ones", KC), COLSUM[0:KC, 0:1], start=True, stop=True)\
                .then_inc(sem("wsum_mm"), 1)

            def frame_turn(t):
                pe.wait_ge(sem("frame_in"), 16 * (t + 1))
                at_least(pe, sem("frameT"), t)
                pe.transpose(bank[0][0:FRAME, 0:ROWS], frame, ident[0:ROWS, 0:ROWS])\
                    .then_inc(sem("frame_turned"), 1)

            def spectrum(t):
                pe.wait_ge(sem("frameT"), t + 1)
                at_least(pe, sem("power"), t)
                pe.matmul(bank[1][0:2 * BINS, 0:ROWS], C("dft", FRAME), frameT,
                          start=True, stop=True).then_inc(sem("spectrum_mm"), 1)

            def mel(t):
                pe.wait_ge(sem("power"), t + 1)
                at_least(pe, sem("logmel"), t)
                pe.matmul(bank[2][0:MELS, 0:ROWS], melT_sb, power, start=True, stop=True)\
                    .then_inc(sem("mel_mm"), 1)

            def embed(t):
                if isinstance(t, int) and t == 0:
                    pe.wait_ge(sem("w_emb"), 1)
                pe.wait_ge(sem("logmel"), t + 1)
                at_least(pe, sem("h0"), t)
                pe.matmul(bank[3][0:ROWS, 0:DIM], logmel, w_emb, start=True, stop=True)\
                    .then_inc(sem("embed_mm"), 1)

            def hn_turn(t):
                pe.wait_ge(sem("hn"), t + 1)
                at_least(pe, sem("hnT"), t)
                for c in range(2):
                    mm = pe.transpose(bank[4][0:KC, c * ROWS:(c + 1) * ROWS],
                                      hn[:, c * KC:(c + 1) * KC], ident[0:ROWS, 0:ROWS])
                mm.then_inc(sem("hn_turned"), 1)

            def project0(t):
                if isinstance(t, int) and t == 0:
                    pe.wait_ge(sem("wq0_ternary"), 1)
                pe.wait_ge(sem("hnT"), t + 1)
                at_least(pe, sem("qkv"), 2 * t)
                for half in range(2):
                    for c in range(2):
                        mm = pe.matmul(bank[5 + half][0:ROWS, 0:288], hnT[:, c, :],
                                       wq0[:, c, half * 288:(half + 1) * 288],
                                       start=(c == 0), stop=(c == 1))
                mm.then_inc(sem("qkv_mm"), 1)

            pipeline(pe, [(frame_turn, 0), (mel, 1), (hn_turn, 2),
                          (spectrum, 0), (embed, 1), (project0, 2)], NT)

            pe.wait_ge(sem("l1_parts"), 2)
            pe.matmul(bank[7][:, 8:11], C("ones", ROWS), PART1[0:ROWS, :], start=True, stop=False)
            pe.matmul(bank[7][:, 8:11], C("ones", LAST), PART2[0:LAST, :], start=False, stop=True)\
                .then_inc(sem("l1_mm"), 1)
            pe.wait_ge(sem("colsum"), 3)
            pe.matmul(bank[6][:, 0:1], C("ones", KC), COLSUM[0:KC, 1:2], start=True, stop=True)
            pe.matmul(bank[6][:, 1:2], C("ones"), COLSUM[:, 2:3], start=True, stop=True)\
                .then_inc(sem("wsum_mm"), 1)

            def qk_turn(t):
                pe.wait_ge(sem("qk_ternary"), t + 1)
                at_least(pe, sem("qkT0"), t)
                if isinstance(t, int) and t == 0:
                    pe.wait_ge(sem("ident16"), 5)
                for c in range(6):
                    mm = pe.transpose(bank16[0][:, c * PITCH16:c * PITCH16 + ROWS],
                                      qk_pad[:, c * 128:(c + 1) * 128], ident16[0:ROWS, 0:ROWS])
                mm.then_inc(sem("qk_turned"), 1)

            def scores0_mm(t):
                pe.wait_ge(sem("qkT0"), t + 1)
                at_least(pe, sem("scores0"), t)
                for b in range(3):
                    for r in range(4):
                        mm = pe.matmul(bank[1 + r][0:ROWS, b * ROWS:(b + 1) * ROWS],
                                       qkT0[32 * r:32 * r + D0, (3 + b) * ROWS:(4 + b) * ROWS],
                                       qkT0[32 * r:32 * r + D0, b * ROWS:(b + 1) * ROWS],
                                       start=True, stop=True)
                        if b == 2:
                            mm.then_inc(sem("scores0_mm"), 1)

            pipeline(pe, [(scores0_mm, 1), (qk_turn, 0)], NT)

            pe.wait_ge(sem("abs0"), NT)
            pe.matmul(bank[5][:, 0:NT - 1], C("ones", ROWS), abs0[:, 0:NT - 1],
                      start=True, stop=True)
            pe.matmul(bank[5][:, NT - 1:NT], C("ones", LAST), abs0[0:LAST, NT - 1:NT],
                      start=True, stop=True).then_inc(sem("abs0_mm"), 1)

            def pv0(half):
                def stage(t):
                    pe.wait_ge(sem("signs"), 2 * t + half + 1)
                    at_least(pe, sem("h1"), 2 * t - 1 + half)
                    v = tile_of(v16, t)
                    for n in range(6):
                        head = 4 * (n % 3) + n // 3 + 2 * half
                        o = bank[6 * half][0:ROWS, head * D0:(head + 1) * D0]
                        mm = pe.matmul(o, signs[half][:, n * ROWS:(n + 1) * ROWS],
                                       v[:, head * D0:(head + 1) * D0], start=True, stop=True)
                    mm.then_inc(sem("pv0_mm"), 1)
                return stage

            pipeline(pe, [(pv0(0), 0), (pv0(1), 0)], NT)

            pe.wait_ge(sem("h1"), 2 * NT)
            pe.wait_ge(sem("in_attn1"), 48)

            def x2_turn(t):
                pe.wait_ge(sem("x2"), t + 1)
                at_least(pe, sem("logits"), t - 3)
                for c in range(2):
                    mm = pe.transpose(bank[1][0:KC, c * ROWS:(c + 1) * ROWS],
                                      x2[:, c * KC:(c + 1) * KC], ident[0:ROWS, 0:ROWS])
                mm.then_inc(sem("x2_turned"), 1)

            def qk1(t):
                pe.wait_ge(sem("x2T"), t + 1)
                at_least(pe, sem("probs"), t)
                for j in range(12):
                    for c in range(2):
                        mm = pe.matmul(bank[5 + j // 4][:, (j % 4) * ROWS:(j % 4 + 1) * ROWS],
                                       w1[:, c, j * 128:(j + 1) * 128], x2T[:, c, :],
                                       start=(c == 0), stop=(c == 1))
                    if j % 4 == 3:
                        mm.then_inc(sem("qk1_mm"), 1)

            def xq_turn(t):
                pe.wait_ge(sem("xq"), t + 1)
                at_least(pe, sem("h2"), t)
                for c in range(2):
                    mm = pe.transpose(bank16[0][0:KC, c * PITCH16:c * PITCH16 + ROWS],
                                      xq[:, c * KC:(c + 1) * KC], ident16[0:ROWS, 0:ROWS])
                mm.then_inc(sem("xq_turned"), 1)

            def gated_turn(t):
                pe.wait_ge(sem("gated"), t + 1)
                at_least(pe, sem("hidden_read"), capped(t + 4))
                at_least(pe, sem("vx"), capped(t + 2))
                for c in range(6):
                    mm = pe.transpose(bank[3 + c // 3][:, (c % 3) * ROWS:(c % 3 + 1) * ROWS],
                                      prod[:, c * 128:(c + 1) * 128], ident[0:ROWS, 0:ROWS])
                mm.then_inc(sem("gated_turned"), 1)

            def ffn_in(t):
                if isinstance(t, int) and t == 0:
                    pe.wait_ge(sem("win_ternary"), 2)
                pe.wait_ge(sem("xqT"), t + 1)
                at_least(pe, sem("vx"), t - 1)
                for half in (1, 0):
                    for c in range(2):
                        mm = pe.matmul(bank[3 + half][0:ROWS, :], xqT[:, c * ROWS:(c + 1) * ROWS],
                                       win16[:, c, half * HID0:(half + 1) * HID0],
                                       start=(c == 0), stop=(c == 1))
                mm.then_inc(sem("ffn_in_mm"), 1)

            def probs_turn(t):
                pe.wait_ge(sem("probs"), t + 1)
                for n in range(HEADS):
                    if n % 4 == 0:
                        at_least(pe, sem("qkT1"), capped(3 * (t + 1) + n // 4 + 1, 3 * NT))
                    mm = pe.transpose(bank[5 + n // 4][0:ROWS, (n % 4) * ROWS:(n % 4 + 1) * ROWS],
                                      probs[:, n * ROWS:(n + 1) * ROWS], ident[0:ROWS, 0:ROWS])
                    if n % 4 == 3:
                        mm.then_inc(sem("probs_turned"), 1)

            def project1(t):
                pe.wait_ge(sem("outT"), t + 1)
                at_least(pe, sem("h3"), t)
                for c in range(6):
                    mm = pe.matmul(bank[2][0:ROWS, 0:DIM], outT[:, c * ROWS:(c + 1) * ROWS],
                                   wo1[:, c, :], start=(c == 0), stop=(c == 5))
                mm.then_inc(sem("project1_mm"), 1)

            def pv1(t):
                pe.wait_ge(sem("probsT"), 3 * (t + 1))
                pe.wait_ge(sem("vx"), t + 1)
                at_least(pe, sem("hidden_read"), capped(t + 3))
                at_least(pe, sem("outT"), t)
                for n, head in enumerate(ORDER1):
                    mm = pe.matmul(bank[3 + head // 6][0:ROWS, (head % 6) * 65:(head % 6 + 1) * 65],
                                   probsT[:, n * ROWS:(n + 1) * ROWS], vx[:, head, :],
                                   start=True, stop=True)
                mm.then_inc(sem("pv1_mm"), 1)

            def normed_turn(t):
                pe.wait_ge(sem("normed"), t + 1)
                at_least(pe, sem("x2T"), capped(t + 4))
                at_least(pe, sem("logits"), t)
                for c in range(2):
                    mm = pe.transpose(bank[1][0:KC, c * ROWS:(c + 1) * ROWS],
                                      row[:, c * KC:(c + 1) * KC], ident[0:ROWS, 0:ROWS])
                mm.then_inc(sem("normed_turned"), 1)

            def v1(t):
                at_least(pe, sem("prod"), t)
                at_least(pe, sem("hidden_read"), capped(t + 2))
                for half in range(2):
                    for c in range(2):
                        mm = pe.matmul(bank[3 + half][0:ROWS, 0:384], x2T[:, c, :],
                                       w1[:, c, 2 * INNER + half * 384:2 * INNER + (half + 1) * 384],
                                       start=(c == 0), stop=(c == 1))
                mm.then_inc(sem("v1_mm"), 1)

            def router_mm(t):
                pe.wait_ge(sem("nT"), t + 1)
                for c in range(2):
                    mm = pe.matmul(bank[1][0:ROWS, 0:EXPERTS], nT[:, c * ROWS:(c + 1) * ROWS],
                                   router[:, c, :], start=(c == 0), stop=(c == 1))
                mm.then_inc(sem("router_mm"), 1)

            def yq_turn(t):
                pe.wait_ge(sem("yq"), t + 1)
                pe.wait_ge(sem("xqT"), t + 1)
                for c in range(4):
                    mm = pe.transpose(bank16[0][:, c * PITCH16:c * PITCH16 + ROWS],
                                      yq[:, c * 128:(c + 1) * 128], ident16[0:ROWS, 0:ROWS])
                mm.then_inc(sem("yq_turned"), 1)

            def scores1(t):
                pe.wait_ge(sem("qkT1"), 3 * (t + 1))
                for b in range(3):
                    at_least(pe, sem("probsT"), 3 * t - 2 + b)
                    mm = pe.matmul(bank[5 + b][0:ROWS, 0:4 * ROWS], ident16[0:ROWS, 0:ROWS],
                                   other16[:, :].unsqueeze(1).to_broadcast([ROWS, 4, ROWS]),
                                   start=True, stop=False)
                mm.then_inc(sem("mask_mm"), 1)
                pe.wait_ge(sem("mask_mm"), t + 1)

                def one(n):
                    head = ORDER1[n]
                    p, j = 64 * (head % 2), head // 2
                    return pe.matmul(bank[5 + n // 4][0:ROWS, (n % 4) * ROWS:(n % 4 + 1) * ROWS],
                                     qkT1[p:p + 64, j * ROWS:(j + 1) * ROWS],
                                     qkT1[p:p + 64, (6 + j) * ROWS:(7 + j) * ROWS],
                                     start=False, stop=(n % 4 == 3))

                one(8)
                one(9).then_inc(sem("even_heads"), 1)
                for n in range(8):
                    mm = one(n)
                    if n % 4 == 3:
                        mm.then_inc(sem("scores1_mm"), 1)
                pe.wait_ge(sem("even_heads"), t + 1)
                one(10)
                one(11).then_inc(sem("scores1_mm"), 1)

            def ffn_out(t):
                pe.wait_ge(sem("yqT"), t + 1)
                for c in range(4):
                    mm = pe.matmul(bank[0][0:ROWS, FFN_OUT:FFN_OUT + DIM], yqT[:, c * ROWS:(c + 1) * ROWS],
                                   wout16[:, c, :], start=(c == 0), stop=(c == 3))
                mm.then_inc(sem("ffn_out_mm"), 1)

            pipeline(pe, [(x2_turn, 2), (ffn_in, 1), (qk1, 2), (normed_turn, 5),
                          (probs_turn, 3), (router_mm, 5), (yq_turn, 1), (scores1, 2),
                          (gated_turn, 4), (ffn_out, 1), (pv1, 3), (project1, 4), (v1, 2),
                          (xq_turn, 0)], NT)

            pe.wait_ge(sem("onehot"), 2)
            rank = bank[2][:, 0:(NT + 1) * EXPERTS]
            pe.matmul(rank, tri16[0:ROWS, :], onehot16, start=True, stop=False)
            for i in range(NT):
                n = ROWS if i < NT - 1 else LAST
                after = NT - i
                mm = pe.matmul(bank[2][:, (i + 1) * EXPERTS:(NT + 1) * EXPERTS]
                               .rearrange("p (t e) -> p t e", e=EXPERTS), ones16[0:n, :],
                               onehot16[0:n, i * EXPERTS:(i + 1) * EXPERTS].unsqueeze(1)
                               .to_broadcast([n, after, EXPERTS]), start=False, stop=(i == NT - 1))
            mm.then_inc(sem("rank_mm"), 1)
            pe.wait_ge(sem("lanes"), 1)
            for i in range(NT):
                n = ROWS if i < NT - 1 else LAST
                mm = pe.matmul(bank[4][:, 0:2 * NS].rearrange("p (a s) -> p a s", a=2),
                               lane_hot[0:n, i, :], token_at[0:n, :, i, :],
                               start=(i == 0), stop=(i == NT - 1))
            mm.then_inc(sem("slots_mm"), 1)

            pe.wait_ge(sem("picks"), 1)
            pe.wait_ge(sem("in_experts"), 6 * 16)

            def rows_turn(s, p):
                pe.wait_ge(sem(f"rows_in{p}"), 4 * (s - p) + 16)
                at_least(pe, sem("rowsT"), 2 * s)
                for c in range(2):
                    mm = pe.transpose(bank[0][:, c * SLOTS:(c + 1) * SLOTS],
                                      slot_rows[p][:, c * 128:(c + 1) * 128], ident)
                mm.then_inc(sem("rows_turned"), 1)

            def expert_in(s, p):
                own = pe.value_load(picks[0:1, bass.ds(s, 1)], min_val=0, max_val=7 * PAIR + BLOCK)
                both = pe.value_load(picks[0:1, bass.ds(s + NS + 1, 1)], min_val=0,
                                     max_val=7 * PAIR + 2 * BLOCK)
                if isinstance(s, int) and s < 3:
                    late = pe.value_load(picks[0:1, 2 * NS + 2 + s:2 * NS + 3 + s], min_val=1, max_val=33)
                    pe.wait_ge(sem("late_experts"), late)
                else:
                    pe.wait_ge(sem("late_experts"), 33)
                pe.wait_ge(sem("rowsT"), 2 * (s + 1))
                at_least(pe, sem("hid"), 2 * s)
                for half in range(2):
                    pe.matmul(bank[1 + half][:, 0:384], rowsT[p % 2][:, 0:SLOTS],
                              big[:, bass.ds(own + half * 384, 384)], start=True, stop=False)
                    mm = pe.matmul(bank[1 + half][:, 0:384], rowsT[p % 2][:, SLOTS:2 * SLOTS],
                                   big[:, bass.ds(both + half * 384, 384)], start=False, stop=True)
                    mm.then_inc(sem("expert_in_mm"), 1)

            def hid_turn(s, p):
                pe.wait_ge(sem("hid"), 2 * (s + 1))
                at_least(pe, sem("hidT"), 2 * s)
                for c in range(6):
                    mm = pe.transpose(bank[3 + c // 3][:, (c % 3) * SLOTS:(c % 3 + 1) * SLOTS],
                                      hid[:, c * 128:(c + 1) * 128], ident)
                    if c % 3 == 2:
                        mm.then_inc(sem("hid_turned"), 1)

            def expert_out(s, p):
                own = pe.value_load(picks[0:1, bass.ds(s, 1)], min_val=0, max_val=7 * PAIR + BLOCK)
                pe.wait_ge(sem("hidT"), 2 * (s + 1))
                at_least(pe, sem("y_slots"), s)
                for c in range(6):
                    mm = pe.matmul(bank[5][:, 0:DIM], hidT[:, c * SLOTS:(c + 1) * SLOTS],
                                   big[:, bass.ds(own + (FF + c * DIM), DIM)],
                                   start=(c == 0), stop=(c == 5))
                mm.then_inc(sem("expert_out_mm"), 1)

            slot_pipeline(pe, [(rows_turn, 0), (hid_turn, 2), (expert_in, 1), (expert_out, 2)])

        @block.scalar
        def _(act):
            def by_chunk(a):
                return a.rearrange("p (c n) -> p c n", n=ROWS)

            def turned16(n):
                return bank16[0][:, 0:n * PITCH16].rearrange("p (c n) -> p c n", n=PITCH16)[:, :, 0:ROWS]

            def copy(out_, in_):
                return act.activation(out_, in_, ACT.Copy)

            act.wait_ge(sem("emb_mm"), 1)
            copy(w_emb, bank[7][0:MELS, 0:DIM]).then_inc(sem("w_emb"), 1)

            def frame_copy(t):
                act.wait_ge(sem("frame_turned"), t + 1)
                at_least(act, sem("spectrum_mm"), t)
                copy(frameT, bank[0][0:FRAME, 0:ROWS]).then_inc(sem("frameT"), 1)

            def square(t):
                act.wait_ge(sem("spectrum_mm"), t + 1)
                at_least(act, sem("mel_mm"), t)
                act.activation(power, bank[1][0:2 * BINS, 0:ROWS], ACT.Square)\
                    .then_inc(sem("power"), 1)

            def log(t):
                act.wait_ge(sem("mel_mm"), t + 1)
                at_least(act, sem("embed_mm"), t)
                act.activation(logmel, bank[2][0:MELS, 0:ROWS], ACT.Ln, bias=C("eps6", MELS))\
                    .then_inc(sem("logmel"), 1)

            def hnT_copy(t):
                act.wait_ge(sem("hn_turned"), t + 1)
                at_least(act, sem("qkv_mm"), t)
                copy(hnT, bank[4][0:KC, 0:2 * ROWS].rearrange("p (c n) -> p c n", c=2))\
                    .then_inc(sem("hnT"), 1)

            def qkv_copy(t):
                act.wait_ge(sem("qkv_mm"), t + 1)
                for half in range(2):
                    copy(tile_of(qkv, t)[:, half * 288:(half + 1) * 288],
                         bank[5 + half][0:ROWS, 0:288]).then_inc(sem("qkv"), 1)

            pipeline(act, [(frame_copy, 0), (log, 1), (hnT_copy, 2), (square, 0), (qkv_copy, 2)], NT)

            act.wait_ge(sem("in_ffn"), 32)
            act.activation(win16[:, :, :], win_raw, ACT.Abs, accum_out=COLSUM[0:KC, 1:2])\
                .then_inc(sem("colsum"), 1)
            act.activation(wout16[:, :, :], wout_raw, ACT.Abs, accum_out=COLSUM[:, 2:3])\
                .then_inc(sem("colsum"), 1)

            def qkT0_copy(t):
                act.wait_ge(sem("qk_turned"), t + 1)
                at_least(act, sem("scores0_mm"), 4 * t)
                copy(by_chunk(qkT0), turned16(6)).then_inc(sem("qkT0"), 1)

            def abs_sum(t):
                act.wait_ge(sem("scores0"), t + 1)
                at_least(act, sem("abs0"), t)
                col = abs0[:, t:t + 1] if isinstance(t, int) else abs0[:, bass.ds(t, 1)]
                act.activation(junk16, tile_of(scores0, t), ACT.Abs, accum_out=col)\
                    .then_inc(sem("abs0"), 1)

            pipeline(act, [(qkT0_copy, 0), (abs_sum, 2)], NT)

            def x2T_copy(t):
                act.wait_ge(sem("x2_turned"), t + 1)
                at_least(act, sem("v1_mm"), t)
                copy(x2T, bank[1][0:KC, 0:2 * ROWS].rearrange("p (c n) -> p c n", c=2))\
                    .then_inc(sem("x2T"), 1)

            def log_var(t):
                act.wait_ge(sem("var64"), t + 1)
                act.activation(logv[:, :], var64[:, :], ACT.Ln,
                               scale=ROOT_2PI / (HEADS - 1), accum_out=small[0:ROWS, 40:41])\
                    .then_inc(sem("logvar"), 1)

            def qkT1_copy(t):
                at_least(act, sem("scores1_mm"), 3 * t)
                for b in range(3):
                    act.wait_ge(sem("qk1_mm"), 3 * t + b + 1)
                    copy(qkT1[:, b * 500:(b + 1) * 500], bank[5 + b][:, 0:500])\
                        .then_inc(sem("qkT1"), 1)

            def xqT_copy(t):
                act.wait_ge(sem("xq_turned"), t + 1)
                at_least(act, sem("ffn_in_mm"), t)
                copy(by_chunk(xqT), turned16(2)[0:KC]).then_inc(sem("xqT"), 1)

            def outT_copy(t):
                act.wait_ge(sem("gated_turned"), t + 1)
                at_least(act, sem("project1_mm"), t)
                copy(outT[:, 0:375], bank[3][:, 0:375])
                copy(outT[:, 375:750], bank[4][:, 0:375]).then_inc(sem("outT"), 1)

            def gate_sigmoid(t):
                link = chain(act, "sigmoid_step", t, 2)
                act.wait_ge(sem("ffn_in_mm"), t + 1)
                act.wait_ge(sem("scales"), t + 1)
                at_least(act, sem("yq"), t)
                link(act.activation(egate, bank[4][0:ROWS, :], ACT.Exp, scale=small[0:ROWS, 12:13]))
                act.activation(yz, bank[3][0:ROWS, :], ACT.Copy, scale=small[0:ROWS, 13:14])\
                    .then_inc(sem("up"), 1)
                link(act.activation(egate, egate, ACT.Ln, bias=C("ones", ROWS)[:, 0:1]))
                act.activation(egate, egate, ACT.Exp, scale=-1.0).then_inc(sem("egate"), 1)

            def y_square(t):
                act.wait_ge(sem("y"), t + 1)
                act.activation(egate, ug, ACT.Square, accum_out=small[0:ROWS, 41:42])\
                    .then_inc(sem("ysum"), 1)

            def probsT_copy(t):
                at_least(act, sem("pv1_mm"), t)
                for b in range(3):
                    act.wait_ge(sem("probs_turned"), 3 * t + b + 1)
                    copy(probsT[:, b * 500:(b + 1) * 500], bank[5 + b][0:ROWS, 0:500])\
                        .then_inc(sem("probsT"), 1)

            def nT_copy(t):
                act.wait_ge(sem("normed_turned"), t + 1)
                at_least(act, sem("router_mm"), t)
                copy(nT, bank[1][0:KC, 0:2 * ROWS]).then_inc(sem("nT"), 1)

            def scale_row(t):
                act.wait_ge(sem("h3_centred"), t + 1)
                act.wait_ge(sem("h3_rsqrt"), t + 1)
                s = small[0:ROWS, 35:36]
                act.activation(row[:, 0:DIM], row[:, 0:DIM], ACT.Copy, scale=s)\
                    .then_inc(sem("normed"), 1)
                act.wait_ge(sem("normed"), t + 1)
                copy(row[:, DIM:DIM + 64], row[:, 128:DIM]).then_inc(sem("row_dup"), 1)

            def vx_copy(t):
                act.wait_ge(sem("v1_mm"), t + 1)
                at_least(act, sem("pv1_mm"), t)
                for half in range(2):
                    ins = copy(vx[:, half * 6:half * 6 + 6, 0:D1],
                               bank[3 + half][0:ROWS, 0:384].rearrange("p (h d) -> p h d", d=D1))
                ins.then_inc(sem("vx"), 1)

            def dev_square(t):
                act.wait_ge(sem("dev"), t + 1)
                act.activation(dev, dev, ACT.Square).then_inc(sem("sq"), 1)

            def router_exp(t):
                act.wait_ge(sem("logits"), t + 1)
                act.wait_ge(sem("logits_kept"), t + 1)
                act.activation(small[0:ROWS, 44:60], tile_of(logits, t), ACT.Exp,
                               bias=small[0:ROWS, 43:44], accum_out=small[0:ROWS, 42:43])\
                    .then_inc(sem("router_exp"), 1)

            def yqT_copy(t):
                act.wait_ge(sem("yq_turned"), t + 1)
                at_least(act, sem("ffn_out_mm"), t)
                copy(by_chunk(yqT), turned16(4)).then_inc(sem("yqT"), 1)

            def softmax_exp(t):
                at_least(act, sem("probs_turned"), 3 * t)
                act.wait_ge(sem("rowmax"), t + 1)
                for n in range(HEADS):
                    ins = act.activation(probs[:, n * ROWS:(n + 1) * ROWS],
                                         bank[5 + n // 4][0:ROWS, (n % 4) * ROWS:(n % 4 + 1) * ROWS],
                                         ACT.Exp, bias=nmax[:, n:n + 1], scale=D1 ** -0.5)
                ins.then_inc(sem("probs"), 1)

            act.preload_act_table_set("natural_log_exp_and_others")
            pipeline(act, [(x2T_copy, 2), (dev_square, 4), (gate_sigmoid, 1), (log_var, 4),
                          (y_square, 1), (qkT1_copy, 2), (scale_row, 5), (nT_copy, 5),
                          (probsT_copy, 3), (yqT_copy, 1), (outT_copy, 4), (router_exp, 5),
                          (softmax_exp, 2), (vx_copy, 2), (xqT_copy, 0)], NT)

            def hid_relu(s, p):
                at_least(act, sem("hid_turned"), 2 * s)
                for half in range(2):
                    act.wait_ge(sem("expert_in_mm"), 2 * s + half + 1)
                    act.activation(hid[:, half * 384:(half + 1) * 384], bank[1 + half][:, 0:384],
                                   ACT.Relu).then_inc(sem("hid"), 1)

            slot_pipeline(act, [(hid_relu, 1)])

        @block.vector
        def _(v):
            v.wait_ge(sem("in_const"), 16)
            for dst, src in ((ident16, "ident"), (tri16, "tri"), (ones16, "ones")):
                v.tensor_copy(dst[:, :], C(src)).then_inc(sem("ident16"), 1)
            v.tensor_copy(same16[:, :], C("same", ROWS)).then_inc(sem("ident16"), 1)
            v.tensor_copy(other16[:, :], C("other", ROWS)).then_inc(sem("ident16"), 1)
            v.memset(qk_pad, 0.0).then_inc(sem("pads"), 1)
            v.wait_ge(sem("in_wq0"), 16)
            v.tensor_reduce(COLSUM[0:KC, 0:1], wq0, AX.XY, ALU.add, apply_absolute_value=True)\
                .then_inc(sem("colsum"), 1)
            link = chain(v, "w_step")
            v.wait_ge(sem("wsum_mm"), 1)
            link(v.tensor_scalar(S_W, bank[6][:, 0:1], 1.0 / (3 * DIM * DIM), 1e-5, ALU.mult, ALU.add))
            link(v.reciprocal(R_W[:, 2:3], S_W))
            link(v.tensor_scalar(wq0, wq0, R_W[0:KC, 2:3], ROUND, ALU.mult, ALU.add))
            link(v.tensor_scalar(wq0, wq0, ROUND, 1.0, ALU.subtract, ALU.min))
            v.tensor_scalar(wq0, wq0, -1.0, None, ALU.max).then_inc(sem("wq0_ternary"), 1)

            v.wait_ge(sem("in_vec"), 80)
            mv = small[0:ROWS, 0:2]

            def statistics(link, src):
                hold(v)
                link(v.bn_stats(stats6[:, :], src))
                hold(v)
                link(v.bn_aggr(mv, stats6[:, :]))

            def rsqrt(name, t):
                v.wait_ge(sem(name + "_rsqrt"), t + 1)

            def embed_norm(t):
                link = chain(v, "embed_step", t, 2)
                v.wait_ge(sem("embed_mm"), t + 1)
                v.tensor_tensor(tile_of(h, t), bank[3][0:ROWS, 0:DIM], bprojb[:, :], ALU.add)\
                    .then_inc(sem("h0"), 1)
                v.wait_ge(sem("h0"), t + 1)
                at_least(v, sem("hn_turned"), t)
                statistics(link, tile_of(h, t))
                v.tensor_scalar(small[0:ROWS, 24:25], mv[:, 1:2], 1e-5, None, ALU.add)\
                    .then_inc(sem("embed_var"), 1)
                rsqrt("embed", t)
                v.tensor_scalar(hn, tile_of(h, t), mv[:, 0:1], small[0:ROWS, 25:26],
                                ALU.subtract, ALU.mult).then_inc(sem("hn"), 1)

            def l1_sums(t):
                v.wait_ge(sem("qkv"), 2 * (t + 1))
                hold(v)
                v.tensor_reduce(tile_of(l1sum, t), tile_of(qkv, t).rearrange("p (g d) -> p g d", d=D0),
                                AX.X, ALU.add, apply_absolute_value=True).then_inc(sem("l1sum"), 1)

            pipeline(v, [(embed_norm, 1), (l1_sums, 2)], NT)

            v.wait_ge(sem("l1sum"), NT)
            sums = l1sum.rearrange("p t n -> p (t n)")
            link(v.tensor_scalar(sums, sums, S_W[0:ROWS, :], None, ALU.mult))
            link(v.tensor_scalar(l1unit, sums, 1e-5, None, ALU.add))
            link(v.reciprocal(l1inv, l1unit))
            link(v.tensor_tensor(l1ratio, sums, l1inv, ALU.mult))
            by_kind = l1ratio.rearrange("p (t g n) -> p g t n", t=NT, g=3)
            v.tensor_reduce(PART1[0:ROWS, :], by_kind[:, :, 0:NT - 1, :], AX.XY, ALU.add)\
                .then_inc(sem("l1_parts"), 1)
            v.tensor_reduce(PART2[0:ROWS, :], by_kind[:, :, NT - 1, :], AX.X, ALU.add)\
                .then_inc(sem("l1_parts"), 1)
            v.wait_ge(sem("l1_mm"), 1)
            link(v.tensor_scalar(S_QKV, bank[7][:, 8:11], 1.0 / (TOKENS * DIM), 1e-5, ALU.mult, ALU.add))
            link(v.reciprocal(R_QKV, S_QKV))
            link(v.tensor_scalar(l1inv, l1inv, S_W[0:ROWS, :], None, ALU.mult))
            link(v.tensor_tensor(
                l1unit.rearrange("p (t g n) -> p t g n", t=NT, g=3),
                l1inv.rearrange("p (t g n) -> p t g n", t=NT, g=3),
                R_QKV[0:ROWS, :].unsqueeze(1).unsqueeze(3).to_broadcast([ROWS, NT, 3, HEADS]),
                ALU.mult))
            unit3 = l1unit.rearrange("p (t n) -> p t n", t=NT)
            v.wait_ge(sem("wsum_mm"), 2)
            link(v.tensor_scalar(S_IN, bank[6][:, 0:1], 1.0 / (2 * HID0 * DIM), 1e-5, ALU.mult, ALU.max))
            link(v.tensor_scalar(S_OUT, bank[6][:, 1:2], 1.0 / (HID0 * DIM), 1e-5, ALU.mult, ALU.max))
            v.reciprocal(R_W[:, 0:2], scal[:, 1:3]).then_inc(sem("ffn_scales"), 1)

            def ternary(t):
                link = chain(v, "ternary_step", t, 2)
                link(v.tensor_tensor(
                    unit.rearrange("p (g d) -> p g d", d=D0),
                    tile_of(qkv, t).rearrange("p (g d) -> p g d", d=D0),
                    tile_of(unit3, t).unsqueeze(2).to_broadcast([ROWS, 3 * HEADS, D0]), ALU.mult))
                link(v.tensor_scalar(whole, unit, ROUND, ROUND, ALU.add, ALU.subtract))
                at_least(v, sem("qk_turned"), t)
                v.tensor_scalar(qk_pad.rearrange("p (g w) -> p g w", w=32)[:, :, 0:D0],
                                whole[:, 0:2 * DIM].rearrange("p (g d) -> p g d", d=D0),
                                1.0, -1.0, ALU.min, ALU.max).then_inc(sem("qk_ternary"), 1)
                v.tensor_scalar(tile_of(v16, t), whole[:, 2 * DIM:3 * DIM], 1.0, -1.0,
                                ALU.min, ALU.max).then_inc(sem("values16"), 1)

            def mask0(t):
                v.wait_ge(sem("scores0_mm"), 4 * (t + 1))
                v.tensor_tensor(tile_of(scores0, t).rearrange("p (r h n) -> p r h n", r=4, h=3),
                                bank1234[0:ROWS, :, 0:375].rearrange("p r (h n) -> p r h n", h=3),
                                same16[:, :].unsqueeze(1).unsqueeze(1).to_broadcast([ROWS, 4, 3, ROWS]),
                                ALU.mult).then_inc(sem("scores0"), 1)

            v.wait_ge(sem("pads"), 1)
            pipeline(v, [(mask0, 2), (ternary, 0)], NT)

            link2 = chain(v, "w2_step")
            v.wait_ge(sem("abs0_mm"), 1)
            link2(v.tensor_reduce(INT_SUM, bank[5][:, 0:NT], AX.X, ALU.add))
            link2(v.scalar_tensor_tensor(GAIN, S_QKV[:, 0:1], D0 ** -0.5, S_QKV[:, 1:2], ALU.mult, ALU.mult))
            link2(v.tensor_tensor(S_A, INT_SUM, GAIN, ALU.mult))
            link2(v.tensor_scalar(S_A, S_A, 1.0 / (CLIPS * HEADS * SEQ * SEQ), 1e-5, ALU.mult, ALU.add))
            link2(v.reciprocal(IGAIN, GAIN))
            link2(v.scalar_tensor_tensor(T_HI, S_A, 0.5, IGAIN, ALU.mult, ALU.mult))
            link2(v.tensor_scalar(T_LO, T_HI, -1.0, None, ALU.mult))
            link2(v.tensor_tensor(FAC0, S_A, S_QKV[:, 2:3], ALU.mult))

            def thresholds(half):
                def stage(t):
                    at_least(v, sem("pv0_mm"), 2 * t - 1 + half)
                    s = tile_of(scores0, t)[:, half * WIDE // 2:(half + 1) * WIDE // 2]
                    v.tensor_scalar(below[half], s, T_LO[0:ROWS, :], None, ALU.is_lt)\
                        .then_inc(sem("below"), 1)
                    v.wait_ge(sem("below"), 2 * t + half + 1)
                    v.scalar_tensor_tensor(signs[half], s, T_HI[0:ROWS, :], below[half], ALU.is_gt,
                                           ALU.subtract).then_inc(sem("signs"), 1)
                return stage

            def add_attn0(half):
                def stage(t):
                    v.wait_ge(sem("pv0_mm"), 2 * t + half + 1)
                    heads = lambda a: a.rearrange("p (b n) -> p b n", b=3)[:, :, 32 * half:32 * half + 32]
                    v.scalar_tensor_tensor(heads(tile_of(h, t)), heads(bank[6 * half][0:ROWS, 0:DIM]),
                                           FAC0[0:ROWS, :], heads(tile_of(h, t)),
                                           ALU.mult, ALU.add).then_inc(sem("h1"), 1)
                return stage

            pipeline(v, [(thresholds(0), 0), (add_attn0(0), 1), (thresholds(1), 0),
                         (add_attn0(1), 1)], NT)

            v.wait_ge(sem("win_ternary"), 2)
            v.memset(vx[:, :, D1:D1 + 1], 1.0).then_inc(sem("vx_ones"), 1)

            def quantise(t):
                link = chain(v, "quant_step", t, 6)
                s = lambda a: small[0:ROWS, a:a + 1]
                v.wait_ge(sem("h1"), 2 * (t + 1))
                x = tile_of(h, t)
                statistics(link, x)
                v.tensor_scalar(s(26), s(1), 1 + 1e-6, 1e-11, ALU.mult, ALU.add)\
                    .then_inc(sem("quant_var"), 1)
                link(v.scalar_tensor_tensor(xz, x, s(0), ginb[:, :], ALU.subtract, ALU.mult))
                link(v.tensor_reduce(s(5), xz, AX.X, ALU.max, apply_absolute_value=True))
                rsqrt("quant", t)
                link(v.tensor_scalar(s(8), s(5), s(27), 1e-5, ALU.mult, ALU.max))
                link(v.reciprocal(s(9), s(8)))
                link2 = chain(v, "quant_step2", t, 2)
                link2(v.tensor_scalar(s(10), s(9), s(27), 127.0, ALU.mult, ALU.mult))
                link2(v.tensor_scalar(xz, xz, s(10), ROUND, ALU.mult, ALU.add))
                at_least(v, sem("xq_turned"), t)
                v.tensor_scalar(xq, xz, ROUND, None, ALU.subtract).then_inc(sem("xq"), 1)

            def hidden_scales(t):
                s = lambda a: small[0:ROWS, a:a + 1]
                link = chain(v, "scales_step", t, 1)
                link(v.tensor_scalar(s(11), s(8), S_IN[0:ROWS, :], 1.0 / 127, ALU.mult, ALU.mult))
                v.tensor_tensor(s(13), s(11), s(11), ALU.mult)
                v.tensor_scalar(s(12), s(11), -1.0, None, ALU.mult).then_inc(sem("scales"), 1)

            def silu(t):
                s = lambda a: small[0:ROWS, a:a + 1]
                link = chain(v, "y_step", t, 1)
                v.wait_ge(sem("up"), t + 1)
                v.tensor_tensor(ug, bank[4][0:ROWS, :], yz, ALU.mult).then_inc(sem("hidden_read"), 1)
                v.wait_ge(sem("hidden_read"), t + 1)
                v.wait_ge(sem("egate"), t + 1)
                v.tensor_tensor(ug, ug, egate, ALU.mult).then_inc(sem("y"), 1)
                v.wait_ge(sem("y"), t + 1)
                link(v.tensor_tensor(yz, ug, goutb[:, :], ALU.mult))
                v.tensor_reduce(s(14), yz, AX.X, ALU.max, apply_absolute_value=True)\
                    .then_inc(sem("ymax"), 1)
                v.wait_ge(sem("ysum"), t + 1)
                v.tensor_scalar(s(28), s(41), 1.0 / HID0, 1e-6, ALU.mult, ALU.add)\
                    .then_inc(sem("y_var"), 1)

            def quantise_y(t):
                s = lambda a: small[0:ROWS, a:a + 1]
                link = chain(v, "y_step2", t, 5)
                v.wait_ge(sem("ymax"), t + 1)
                rsqrt("y", t)
                link(v.tensor_scalar(s(18), s(14), s(29), 1e-5, ALU.mult, ALU.max))
                link(v.reciprocal(s(19), s(18)))
                link(v.tensor_scalar(s(20), s(19), s(29), 127.0, ALU.mult, ALU.mult))
                link(v.tensor_scalar(yz, yz, s(20), ROUND, ALU.mult, ALU.add))
                at_least(v, sem("yq_turned"), t)
                v.tensor_scalar(yq, yz, ROUND, None, ALU.subtract).then_inc(sem("yq"), 1)
                link(v.tensor_scalar(s(21), s(18), S_OUT[0:ROWS, :], 1.0 / 127, ALU.mult, ALU.mult))

            def add_ffn_norm(t):
                link = chain(v, "x2_step", t, 2)
                v.wait_ge(sem("ffn_out_mm"), t + 1)
                v.scalar_tensor_tensor(tile_of(h, t), bank[0][0:ROWS, FFN_OUT:FFN_OUT + DIM], small[0:ROWS, 21:22],
                                       tile_of(h, t), ALU.mult, ALU.add).then_inc(sem("h2"), 1)
                v.wait_ge(sem("h2"), t + 1)
                at_least(v, sem("x2_turned"), t)
                statistics(link, tile_of(h, t))
                v.tensor_scalar(small[0:ROWS, 30:31], mv[:, 1:2], 1e-5, None, ALU.add)\
                    .then_inc(sem("x2_var"), 1)
                rsqrt("x2", t)
                v.tensor_scalar(x2, tile_of(h, t), mv[:, 0:1], small[0:ROWS, 31:32],
                                ALU.subtract, ALU.mult).then_inc(sem("x2"), 1)

            def row_max(t):
                link = chain(v, "max_step", t, 1)
                at_least(v, sem("probs"), t)
                v.wait_ge(sem("scores1_mm"), 3 * (t + 1))
                hold(v)
                link(v.tensor_reduce(rowmax[:, :].rearrange("p (b h) -> p b h", b=3),
                                     bank567[0:ROWS, :, 0:500].rearrange("p b (h n) -> p b h n", h=4),
                                     AX.X, ALU.max))
                v.tensor_scalar(nmax[:, :], rowmax[:, :], -(D1 ** -0.5), None, ALU.mult)\
                    .then_inc(sem("rowmax"), 1)

            def product(t):
                link = chain(v, "prod_step", t, 1)
                v.wait_ge(sem("pv1_mm"), t + 1)
                pv = bank1234[0:ROWS, 2:4, 0:390].rearrange("p b (h d) -> p b h d", d=D1 + 1)
                rs = rsum[:, :].rearrange("p (b h) -> p b h", b=2)
                link(v.reciprocal(rs.unsqueeze(3), pv[:, :, :, D1:D1 + 1]))
                at_least(v, sem("gated_turned"), t)
                v.tensor_tensor(prod.rearrange("p (b h d) -> p b h d", b=2, h=6), pv[:, :, :, 0:D1],
                                rs.unsqueeze(3).to_broadcast([ROWS, 2, 6, D1]), ALU.mult)\
                    .then_inc(sem("prod"), 1)

            def mean_heads(t):
                link = chain(v, "mean_step", t, 1)
                v.wait_ge(sem("prod"), t + 1)
                at_least(v, sem("dev"), t)
                link(v.tensor_reduce(mean64[:, :], prod.rearrange("p (h d) -> p d h", h=HEADS),
                                     AX.X, ALU.add))
                v.tensor_scalar(mean64[:, :], mean64[:, :], 1.0 / HEADS, None, ALU.mult)\
                    .then_inc(sem("mean"), 1)

            def variance(t):
                v.wait_ge(sem("sq"), t + 1)
                v.tensor_reduce(var64[:, :], dev.rearrange("p (h d) -> p d h", h=HEADS),
                                AX.X, ALU.add).then_inc(sem("var64"), 1)
                v.wait_ge(sem("var64"), t + 1)
                v.reciprocal(ivar64[:, :], var64[:, :]).then_inc(sem("ivar"), 1)

            def gate_heads(t):
                link = chain(v, "gate_step", t, 2)
                v.wait_ge(sem("scaled"), t + 1)
                link(v.tensor_reduce(factor[:, :], dev.rearrange("p (h d) -> p h d", h=HEADS),
                                     AX.X, ALU.add))
                v.wait_ge(sem("logvar"), t + 1)
                link(v.tensor_scalar(factor[:, :], factor[:, :], 0.25 * (HEADS - 1),
                                     small[0:ROWS, 40:41], ALU.mult, ALU.subtract))
                v.tensor_tensor(prod.rearrange("p (h d) -> p h d", h=HEADS),
                                prod.rearrange("p (h d) -> p h d", h=HEADS),
                                factor[:, :].unsqueeze(2).to_broadcast([ROWS, HEADS, D1]),
                                ALU.mult).then_inc(sem("gated"), 1)

            def add_attn1_norm(t):
                link = chain(v, "h3_step", t, 3)
                v.wait_ge(sem("project1_mm"), t + 1)
                at_least(v, sem("row_stored"), 16 * t)
                v.wait_ge(sem("h2_biased"), t + 1)
                v.tensor_tensor(h3, bank[2][0:ROWS, 0:DIM], tile_of(h, t), ALU.add)\
                    .then_inc(sem("h3"), 1)
                v.wait_ge(sem("h3"), t + 1)
                s = lambda a: small[0:ROWS, a:a + 1]
                x3 = tile_of(h, t)
                statistics(link, h3)
                link(v.tensor_scalar(s(33), s(1), 1 + 1e-6, 1e-11, ALU.mult, ALU.add))
                v.tensor_scalar(s(32), s(1), 1e-5, None, ALU.add).then_inc(sem("h3_var"), 1)
                rsqrt("h3", t)
                v.scalar_tensor_tensor(row[:, 0:DIM], h3, s(0), lnwb[:, :], ALU.subtract, ALU.mult)\
                    .then_inc(sem("h3_centred"), 1)
                v.tensor_scalar(x3, h3, s(0), s(34), ALU.subtract, ALU.mult).then_inc(sem("x3"), 1)

            def router_max(t):
                v.wait_ge(sem("router_mm"), t + 1)
                link = chain(v, "router_step", t, 1)
                lg = tile_of(logits, t)
                v.tensor_copy(lg, bank[1][0:ROWS, 0:EXPERTS]).then_inc(sem("logits_kept"), 1)
                link(v.tensor_reduce(small[0:ROWS, 23:24], bank[1][0:ROWS, 0:EXPERTS], AX.X, ALU.max))
                v.tensor_scalar(small[0:ROWS, 43:44], small[0:ROWS, 23:24], -1.0, None, ALU.mult)\
                    .then_inc(sem("logits"), 1)

            def router_prob(t):
                v.wait_ge(sem("router_exp"), t + 1)
                v.wait_ge(sem("row_dup"), t + 1)
                v.wait_ge(sem("residual"), t + 1)
                v.reciprocal(row[:, GATE:GATE + 1], small[0:ROWS, 42:43]).then_inc(sem("row_ready"), 1)

            v.memset(row[:, :], 0.0).then_inc(sem("vx_ones"), 1)
            v.wait_ge(sem("vx_ones"), 2)
            pipeline(v, [(variance, 4), (silu, 1), (quantise_y, 1), (gate_heads, 4),
                          (router_max, 5), (quantise, 0), (hidden_scales, 0),
                          (router_prob, 5), (row_max, 2), (product, 3), (add_ffn_norm, 1),
                          (mean_heads, 3), (add_attn1_norm, 4)], NT)

            link = chain(v, "route_step")
            v.wait_ge(sem("logits"), NT)
            v.wait_ge(sem("logits_kept"), NT)
            grid = [ROWS, NT, EXPERTS]
            lg = logits[:, :, :]
            link(v.tensor_reduce(best, lg, AX.X, ALU.max))
            link(v.tensor_tensor(hot, lg, best.unsqueeze(2).to_broadcast(grid), ALU.is_equal))
            link(v.tensor_tensor(hot, hot, C("rev", ROWS).unsqueeze(1).to_broadcast(grid), ALU.mult))
            link(v.tensor_reduce(best, hot, AX.X, ALU.max))
            link(v.tensor_tensor(hot, hot, best.unsqueeze(2).to_broadcast(grid), ALU.is_equal))
            v.memset(onehot16[:, NT * EXPERTS:(NT + 1) * EXPERTS], 0.0).then_inc(sem("onehot"), 1)
            v.tensor_copy(onehot16[:, 0:NT * EXPERTS], hot.rearrange("p t e -> p (t e)"))\
                .then_inc(sem("onehot"), 1)
            v.wait_ge(sem("rank_mm"), 1)
            link(v.tensor_copy(cnt, bank[2][:, NT * EXPERTS:(NT + 1) * EXPERTS]))
            link(v.tensor_tensor(cmp13, cnt.unsqueeze(2).to_broadcast([128, EXPERTS, NT]),
                                 C("count").unsqueeze(1).to_broadcast([128, EXPERTS, NT]), ALU.is_gt))
            link(v.tensor_reduce(ntile, cmp13, AX.X, ALU.add))
            link(v.tensor_tensor(cmp16, ntile.unsqueeze(1).to_broadcast([128, EXPERTS, EXPERTS]),
                                 C("below").rearrange("p (a b) -> p a b", a=EXPERTS), ALU.mult))
            link(v.tensor_reduce(base, cmp16, AX.X, ALU.add))
            link(v.tensor_scalar(base128, base, float(SLOTS), None, ALU.mult))
            link(v.tensor_tensor(where, bank[2][0:ROWS, 0:NT * EXPERTS]
                                 .rearrange("p (t e) -> p t e", e=EXPERTS),
                                 base128[0:ROWS, :].unsqueeze(1).to_broadcast(grid), ALU.add))
            link(v.tensor_tensor(where, where, hot, ALU.mult))
            link(v.tensor_reduce(pos, where, AX.X, ALU.add))
            link(v.tensor_copy(pos_i, pos))
            link(v.tensor_scalar(lane_i, pos_i, SLOTS - 1, None, ALU.bitwise_and))
            link(v.tensor_scalar(tile_i, pos_i, 7, None, ALU.logical_shift_right))
            link(v.tensor_copy(lane_f, lane_i))
            link(v.tensor_copy(tile_f, tile_i))
            link(v.tensor_tensor(lane_hot, C("lane", ROWS).unsqueeze(1).to_broadcast([ROWS, NT, 128]),
                                 lane_f.unsqueeze(2).to_broadcast([ROWS, NT, 128]), ALU.is_equal))
            link(v.tensor_tensor(token_at[:, 0], C("slot", ROWS).unsqueeze(1).to_broadcast([ROWS, NT, NS]),
                                 tile_f.unsqueeze(2).to_broadcast([ROWS, NT, NS]), ALU.is_equal))
            link(v.tensor_tensor(token_at[:, 1], token_at[:, 0], C("tile", ROWS).unsqueeze(2)
                                 .to_broadcast([ROWS, NT, NS]), ALU.mult))
            v.tensor_scalar(token_at[:, 0], token_at[:, 0], C("row", ROWS), None, ALU.mult)\
                .then_inc(sem("lanes"), 1)
            link(v.tensor_tensor(ends, base, ntile, ALU.add))
            link(v.tensor_tensor(cmp28, ends.unsqueeze(1).to_broadcast([128, NS, EXPERTS]),
                                 C("slot").unsqueeze(2).to_broadcast([128, NS, EXPERTS]), ALU.is_le))
            link(v.tensor_reduce(expert, cmp28, AX.X, ALU.add))
            v.wait_ge(sem("slots_mm"), 1)
            link(v.tensor_scalar(slot_f, bank[4][:, NS:2 * NS], float(ROWS), None, ALU.mult))
            link(v.tensor_tensor(slot_f, slot_f, bank[4][:, 0:NS], ALU.add))
            link(v.tensor_scalar(empty, slot_f, 0.0, float(4 * TOKENS), ALU.is_equal, ALU.mult))
            link(v.scalar_tensor_tensor(slot_f, slot_f, -1.0, empty, ALU.add, ALU.add))
            v.tensor_copy(slot_i, slot_f).then_inc(sem("slots"), 1)
            link(v.tensor_scalar(expert, expert, float(EXPERTS - 1), None, ALU.min))
            link(v.tensor_copy(expert_i, expert))
            link(v.tensor_scalar(odd_i, expert_i, 1, None, ALU.bitwise_and))
            link(v.tensor_copy(odd, odd_i))
            link(v.tensor_tensor(pair2, expert, odd, ALU.subtract))
            link(v.tensor_scalar(own_f, pair2, PAIR / 2.0, None, ALU.mult))
            link(v.tensor_scalar(both_f, own_f, float(2 * BLOCK), None, ALU.add))
            link(v.scalar_tensor_tensor(own_f, odd, float(BLOCK), own_f, ALU.mult, ALU.add))
            link(v.tensor_scalar(mine[:, 0:NS], odd, C("side"), None, ALU.is_equal))
            link(v.tensor_scalar(late, expert, 12.0, 16.0, ALU.is_ge, ALU.mult))
            link(v.tensor_scalar(last_pair, expert, 14.0, 16.0, ALU.is_ge, ALU.mult))
            link(v.scalar_tensor_tensor(late, late, 1.0, last_pair, ALU.add, ALU.add))
            v.tensor_copy(picks[:, 2 * NS + 2:3 * NS + 2], late)
            v.tensor_copy(picks[:, 0:NS], own_f)
            v.tensor_copy(picks[:, NS + 1:2 * NS + 1], both_f).then_inc(sem("picks"), 1)
            def rowsT_copy(s, p):
                v.wait_ge(sem("rows_turned"), s + 1)
                at_least(v, sem("expert_in_mm"), 2 * (s - 1))
                v.tensor_copy(rowsT[p % 2][:, 0:SLOTS], bank[0][:, 0:SLOTS]).then_inc(sem("rowsT"), 1)
                m = mine[:, s:s + 1] if isinstance(s, int) else mine[:, bass.ds(s, 1)]
                v.tensor_scalar(rowsT[p % 2][:, SLOTS:2 * SLOTS], bank[0][:, SLOTS:2 * SLOTS], m, None,
                                ALU.mult).then_inc(sem("rowsT"), 1)

            def hidT_copy(s, p):
                at_least(v, sem("expert_out_mm"), s)
                for half in range(2):
                    v.wait_ge(sem("hid_turned"), 2 * s + half + 1)
                    v.tensor_copy(hidT[:, half * 384:(half + 1) * 384], bank[3 + half][:, 0:384])\
                        .then_inc(sem("hidT"), 1)

            def combine(s, p):
                v.wait_ge(sem("expert_out_mm"), s + 1)
                at_least(v, sem(f"y_stored{p % 2}"), 8 * (s - p % 2))
                r = slot_rows[p]
                v.scalar_tensor_tensor(y_out[p % 2], bank[5][:, 0:DIM], r[:, GATE:GATE + 1],
                                       r[:, RES:RES + DIM], ALU.mult, ALU.add)\
                    .then_inc(sem("y_slots"), 1)

            slot_pipeline(v, [(rowsT_copy, 0), (hidT_copy, 2), (combine, 2)])

        @block.gpsimd
        def _(g):
            def powers(name, a, n=1):
                def stage(t):
                    g.wait_ge(sem(name + "_var"), t + 1)
                    g.tensor_tensor(small[0:ROWS, a + n:a + 2 * n], small[0:ROWS, a:a + n],
                                    C("minus_half", ROWS)[:, 0:n], ALU.pow)\
                        .then_inc(sem(name + "_rsqrt"), 1)
                return stage

            g.wait_ge(sem("in_const"), 16)
            pipeline(g, [(powers("embed", 24), 0)], NT)

            g.wait_ge(sem("ffn_scales"), 1)
            link = chain(g, "w_round")
            for w, w16, scale in ((win_raw, win16, R_W[0:KC, 0:1]), (wout_raw, wout16, R_W[:, 1:2])):
                link(g.tensor_scalar(w, w, scale, ROUND, ALU.mult, ALU.add))
                link(g.tensor_scalar(w, w, ROUND, 1.0, ALU.subtract, ALU.min))
                g.tensor_scalar(w16[:, :, :], w, -1.0, None, ALU.max).then_inc(sem("win_ternary"), 1)
            prod3 = prod.rearrange("p (h d) -> p h d", h=HEADS)
            dev3 = dev.rearrange("p (h d) -> p h d", h=HEADS)

            def add_bias(t):
                g.wait_ge(sem("x2"), t + 1)
                g.tensor_tensor(tile_of(h, t), tile_of(h, t), boutb[:, :], ALU.add)\
                    .then_inc(sem("h2_biased"), 1)

            def residual(t):
                g.wait_ge(sem("x3"), t + 1)
                g.tensor_tensor(h3, tile_of(h, t), h3, ALU.add).then_inc(sem("residual"), 1)

            def deviation(t):
                g.wait_ge(sem("mean"), t + 1)
                g.tensor_tensor(dev3, prod3, mean64[:, :].unsqueeze(1).to_broadcast([ROWS, HEADS, D1]),
                                ALU.subtract).then_inc(sem("dev"), 1)

            def scale_squares(t):
                g.wait_ge(sem("ivar"), t + 1)
                g.tensor_tensor(dev3, dev3, ivar64[:, :].unsqueeze(1).to_broadcast([ROWS, HEADS, D1]),
                                ALU.mult).then_inc(sem("scaled"), 1)

            pipeline(g, [(scale_squares, 4), (powers("y", 28), 1), (powers("quant", 26), 0),
                          (powers("x2", 30), 1), (deviation, 3), (powers("h3", 32, 2), 4),
                          (residual, 4), (add_bias, 1)], NT)

            g.wait_ge(sem("onehot"), 2)
            for p in range(4):
                g.memset(slot_rows[p], 0.0).then_inc(sem("rows_zero"), 1)
            g.wait_ge(sem("rows_zero"), 4)
            g.wait_ge(sem("slots"), 1)
            g.wait_ge(sem("row_stored"), 16 * NT)

            def gather(s):
                if s >= 4:
                    g.wait_ge(sem("y_slots"), s - 3)
                g.indirect_dma_start(slot_rows[s % 4], None, rows_dram,
                                     bass.IndirectOffsetOnAxis(ap=slot_i[:, s:s + 1], axis=0),
                                     bounds_check=TOKENS - 1, oob_is_err=False)\
                    .then_inc(sem(f"rows_in{s % 4}"), 16)

            for s in range(4):
                gather(s)
            for s in range(NS):
                if s + 4 < NS:
                    gather(s + 4)
                g.wait_ge(sem("y_slots"), s + 1)
                g.indirect_dma_start(out_rows, bass.IndirectOffsetOnAxis(ap=slot_i[:, s:s + 1], axis=0),
                                     y_out[s % 2], None,
                                     bounds_check=TOKENS - 1, oob_is_err=False)\
                    .then_inc(sem(f"y_stored{s % 2}"), 16)
            for p in range(2):
                g.wait_ge(sem(f"y_stored{p}"), 8 * NS)

        for name, n, steps in chains:
            assert not steps or n[0] == steps, (name, n[0], steps)


def kernel(**inputs):
    import numpy as np
    import concourse.bacc as bacc
    from concourse.bass_utils import run_bass_kernel_spmd

    nc = bacc.Bacc("TRN2", target_bir_lowering=False, num_devices=1)
    arrays, args = {}, []

    def give(name, a):
        a = np.ascontiguousarray(a)
        arrays[name] = a
        args.append(nc.dram_tensor(name, a.shape, mybir.dt.from_np(a.dtype), kind="ExternalInput").ap())

    def chunks(w, rows):
        return w.reshape(-1, rows, w.shape[1]).transpose(1, 0, 2)

    i = {k: np.asarray(v) for k, v in inputs.items()}
    give("in_x", i["x"])
    give("in_consts", constants())
    mel = i["L0_tok_mel_filters"].T
    give("in_melT", np.concatenate([mel, mel], 0))
    give("in_dct", i["L0_tok_dct"])
    give("in_w_proj", i["L0_tok_w_proj"])
    give("in_b_proj", i["L0_tok_b_proj"])
    give("in_w_qkv0", chunks(i["L0_attn_w_qkv"].T, KC))
    give("in_w_in", chunks(i["L0_ffn_w_in"].T, KC))
    give("in_g_in", i["L0_ffn_g_in"])
    give("in_w_out0", chunks(i["L0_ffn_w_out"].T, 128))
    give("in_g_out", i["L0_ffn_g_out"])
    give("in_w_qkv1", chunks(i["L1_attn_w_qkv"], KC))
    give("in_w_out1", chunks(i["L1_attn_w_out"], 128))
    give("in_b_out", i["L1_attn_b_out"])
    give("in_ln_w", i["L1_ffn_ln_w"])
    give("in_w_router", chunks(i["L1_ffn_w_router"], KC))
    wi, wo = i["L1_ffn_wi"], i["L1_ffn_wo"]
    first = wi[:, 0:128, :]
    last = wi[:, 128:DIM, :].reshape(EXPERTS // 2, 128, FF)
    down = wo.reshape(EXPERTS, 6, 128, DIM).transpose(0, 2, 1, 3).reshape(EXPERTS, 128, 6 * DIM)
    give("in_experts", np.concatenate([first[0::2], down[0::2], first[1::2], down[1::2], last], 2))
    out = nc.dram_tensor("out", (CLIPS, SEQ, DIM), F32, kind="ExternalOutput").ap()
    rows_dram = nc.dram_tensor("rows_dram", (NT * ROWS, ROWLEN), F32, kind="Internal").ap()
    build(nc, *args, out, rows_dram)
    r = run_bass_kernel_spmd(nc, [arrays], core_ids=[0])
    return r.results[0]["out"]
```
